# Optimizing a Trainium2 kernel written in Bass

```python
import numpy as np
import jax
import jax.numpy as jnp

def _softmax(x, axis=-1):
    return jax.nn.softmax(x, axis=axis)

def _gelu(x):
    return jax.nn.gelu(x, approximate=True)

def _silu(x):
    return jax.nn.silu(x)

def _sigmoid(x):
    return jax.nn.sigmoid(x)

def _layernorm(x, axis=-1, eps=1e-05):
    m = jnp.mean(x, axis=axis, keepdims=True)
    v = jnp.var(x, axis=axis, keepdims=True)
    return (x - m) / jnp.sqrt(v + eps)

def _scatter_add(tgt, idx, src, axis=0):
    return tgt.at[idx].add(src)

def _segment_sum(src, seg, n):
    return jax.ops.segment_sum(src, seg, n)
kernel_name = 'mk_adaln_d2_jaxref_r8_f4f94f'

def setup_inputs(seed: int=0):
    np.random.seed(seed)
    _w = jnp.asarray

    def _L0_attn_setup():
        import jax, jax.numpy as jnp
        import numpy as np
        B, S, HID = (1, 256, 128)
        H, HKV, D = (16, 4, 64)
        THETA = 10000.0

        def _rope_tables(seq_len, head_dim):
            inv_freq = 1.0 / THETA ** (jnp.arange(0, head_dim, 2, dtype=jnp.float32) / head_dim)
            freqs = jnp.arange(seq_len, dtype=jnp.float32)[:, None] * inv_freq[None, :]
            emb = jnp.concatenate([freqs, freqs], axis=-1)
            return (jnp.cos(emb)[:, 0::2], jnp.sin(emb)[:, 0::2])

        def _apply_rope(x, cos, sin):
            xe, xo = (x[..., 0::2], x[..., 1::2])
            re = xe * cos - xo * sin
            ro = xe * sin + xo * cos
            return jnp.stack([re, ro], axis=-1).reshape(x.shape)
        key = jax.random.key(seed)
        k0, k1, k2, k3, k4 = jax.random.split(key, 5)
        return {'hidden_states': jax.random.normal(k0, (B, S, HID), dtype=jnp.float32), 'Wq': jax.random.normal(k1, (HID, H * D), dtype=jnp.float32) * 0.02, 'Wk': jax.random.normal(k2, (HID, HKV * D), dtype=jnp.float32) * 0.02, 'Wv': jax.random.normal(k3, (HID, HKV * D), dtype=jnp.float32) * 0.02, 'Wo': jax.random.normal(k4, (H * D, HID), dtype=jnp.float32) * 0.02}
    _L0_attn_in = _L0_attn_setup()

    def _L0_ffn_setup():
        import jax, jax.numpy as jnp
        import numpy as np
        NUM_EXPERTS = 8
        EXPERT_CAPACITY = 2.0
        DIM = 128
        HIDDEN_DIM = 512
        key = jax.random.key(seed)
        k_x, k_g, k_w1, k_w2 = jax.random.split(key, 4)
        n, t, d, f, e = (8, 128, DIM, HIDDEN_DIM, NUM_EXPERTS)
        x = jax.random.normal(k_x, (n, t, d), dtype=jnp.float32)
        gate_w = jax.random.normal(k_g, (e, d), dtype=jnp.float32) * 0.02
        w1 = jax.random.normal(k_w1, (e, d, f), dtype=jnp.float32) * 0.02
        w2 = jax.random.normal(k_w2, (e, f, d), dtype=jnp.float32) * 0.02
        return {'x': x, 'gate_w': gate_w, 'w1': w1, 'w2': w2}
    _L0_ffn_in = _L0_ffn_setup()
    _L0_c = _w((lambda *s: np.random.randn(*s).astype(np.float32) * 0.05)(8, 128))
    _L0_wmod = _w((lambda *s: np.random.randn(*s).astype(np.float32) * 0.05)(128, 6 * 128) * 128 ** (-0.5))

    def _L1_attn_setup():
        import jax, jax.numpy as jnp
        import numpy as np
        from math import sqrt
        HEADS = 16
        MODEL_DIM = 128
        DIM_PER_HEAD = MODEL_DIM // HEADS
        MAX_REL_POS = 32
        ROPE_BASE = 10000.0
        NEG_INF = -1e+18

        def _rope_cos_sin(seq_len, dim):
            inv_freq = 1.0 / ROPE_BASE ** (jnp.arange(0, dim, 2, dtype=jnp.float32) / dim)
            t = jnp.arange(seq_len, dtype=jnp.float32)
            ang = jnp.outer(t, inv_freq)
            return (jnp.cos(ang), jnp.sin(ang))

        def _apply_rotary_interleave(x, cos, sin):
            B, H, L, D = x.shape
            x_ = x.reshape(B, H, L, D // 2, 2)
            xe, xo = (x_[..., 0], x_[..., 1])
            c = cos[None, None, :, :]
            s = sin[None, None, :, :]
            oe = xe * c - xo * s
            oo = xe * s + xo * c
            return jnp.stack([oe, oo], axis=-1).reshape(B, H, L, D)
        key = jax.random.key(seed)
        ks = jax.random.split(key, 6)
        B, L = (2, 128)
        scale = 0.02
        x = jax.random.normal(ks[0], (B, L, MODEL_DIM), dtype=jnp.float32)
        w_q = jax.random.normal(ks[1], (MODEL_DIM, MODEL_DIM), dtype=jnp.float32) * scale
        w_k = jax.random.normal(ks[2], (MODEL_DIM, MODEL_DIM), dtype=jnp.float32) * scale
        w_v = jax.random.normal(ks[3], (MODEL_DIM, MODEL_DIM), dtype=jnp.float32) * scale
        w_o = jax.random.normal(ks[4], (MODEL_DIM, MODEL_DIM), dtype=jnp.float32) * scale
        rel_emb = jax.random.normal(ks[5], (2 * MAX_REL_POS + 1, DIM_PER_HEAD), dtype=jnp.float32) * scale
        return {'x': x, 'w_q': w_q, 'w_k': w_k, 'w_v': w_v, 'w_o': w_o, 'rel_emb': rel_emb}
    _L1_attn_in = _L1_attn_setup()

    def _L1_ffn_setup():
        import jax, jax.numpy as jnp
        import numpy as np
        E = 8
        K = 2
        D = 128
        P = 512
        key = jax.random.key(seed)
        ks = jax.random.split(key, 8)
        s = lambda fan_in: 1.0 / np.sqrt(fan_in)
        x = jax.random.normal(ks[0], (2, 256, D), dtype=jnp.float32)
        W1 = jax.random.normal(ks[1], (E, D, P), dtype=jnp.float32) * s(D)
        b1 = jax.random.normal(ks[2], (E, P), dtype=jnp.float32) * 0.01
        W2 = jax.random.normal(ks[3], (E, P, D), dtype=jnp.float32) * s(P)
        b2 = jax.random.normal(ks[4], (E, D), dtype=jnp.float32) * 0.01
        Wr = jax.random.normal(ks[5], (D, E), dtype=jnp.float32) * s(D)
        br = jax.random.normal(ks[6], (E,), dtype=jnp.float32) * 0.01
        return {'x': x, 'W1': W1, 'b1': b1, 'W2': W2, 'b2': b2, 'Wr': Wr, 'br': br}
    _L1_ffn_in = _L1_ffn_setup()
    _L1_c = _w((lambda *s: np.random.randn(*s).astype(np.float32) * 0.05)(8, 128))
    _L1_wmod = _w((lambda *s: np.random.randn(*s).astype(np.float32) * 0.05)(128, 6 * 128) * 128 ** (-0.5))
    _d = {'L0_attn_hidden_states': _L0_attn_in['hidden_states'], 'L0_attn_Wq': _L0_attn_in['Wq'], 'L0_attn_Wk': _L0_attn_in['Wk'], 'L0_attn_Wv': _L0_attn_in['Wv'], 'L0_attn_Wo': _L0_attn_in['Wo'], 'L0_ffn_gate_w': _L0_ffn_in['gate_w'], 'L0_ffn_w1': _L0_ffn_in['w1'], 'L0_ffn_w2': _L0_ffn_in['w2'], 'L0_c': _L0_c, 'L0_wmod': _L0_wmod, 'L1_attn_w_q': _L1_attn_in['w_q'], 'L1_attn_w_k': _L1_attn_in['w_k'], 'L1_attn_w_v': _L1_attn_in['w_v'], 'L1_attn_w_o': _L1_attn_in['w_o'], 'L1_attn_rel_emb': _L1_attn_in['rel_emb'], 'L1_ffn_W1': _L1_ffn_in['W1'], 'L1_ffn_b1': _L1_ffn_in['b1'], 'L1_ffn_W2': _L1_ffn_in['W2'], 'L1_ffn_b2': _L1_ffn_in['b2'], 'L1_ffn_Wr': _L1_ffn_in['Wr'], 'L1_ffn_br': _L1_ffn_in['br'], 'L1_c': _L1_c, 'L1_wmod': _L1_wmod}
    _x0 = _d['L0_attn_hidden_states']
    _d['L0_attn_hidden_states'] = jax.random.normal(jax.random.fold_in(jax.random.key(seed), 1), (8, 512, 128), dtype=_x0.dtype)
    del _x0
    return _d

def reference(L0_attn_hidden_states, L0_attn_Wq, L0_attn_Wk, L0_attn_Wv, L0_attn_Wo, L0_ffn_gate_w, L0_ffn_w1, L0_ffn_w2, L0_c, L0_wmod, L1_attn_w_q, L1_attn_w_k, L1_attn_w_v, L1_attn_w_o, L1_attn_rel_emb, L1_ffn_W1, L1_ffn_b1, L1_ffn_W2, L1_ffn_b2, L1_ffn_Wr, L1_ffn_br, L1_c, L1_wmod):

    def _L0_attn_ref(hidden_states, Wq, Wk, Wv, Wo):
        import jax, jax.numpy as jnp
        import numpy as np
        B, S, HID = (1, 256, 128)
        H, HKV, D = (16, 4, 64)
        THETA = 10000.0

        def _rope_tables(seq_len, head_dim):
            inv_freq = 1.0 / THETA ** (jnp.arange(0, head_dim, 2, dtype=jnp.float32) / head_dim)
            freqs = jnp.arange(seq_len, dtype=jnp.float32)[:, None] * inv_freq[None, :]
            emb = jnp.concatenate([freqs, freqs], axis=-1)
            return (jnp.cos(emb)[:, 0::2], jnp.sin(emb)[:, 0::2])

        def _apply_rope(x, cos, sin):
            xe, xo = (x[..., 0::2], x[..., 1::2])
            re = xe * cos - xo * sin
            ro = xe * sin + xo * cos
            return jnp.stack([re, ro], axis=-1).reshape(x.shape)
        b, s, _ = hidden_states.shape
        q = (hidden_states @ Wq).reshape(b, s, H, D).transpose(0, 2, 1, 3)
        k = (hidden_states @ Wk).reshape(b, s, HKV, D).transpose(0, 2, 1, 3)
        v = (hidden_states @ Wv).reshape(b, s, HKV, D).transpose(0, 2, 1, 3)
        cos, sin = _rope_tables(s, D)
        q = _apply_rope(q, cos, sin)
        k = _apply_rope(k, cos, sin)
        G = H // HKV
        qg = q.reshape(b, HKV, G, s, D)
        scale = jnp.float32(D) ** (-0.5)
        scores = jnp.einsum('bkgqd,bkpd->bkgqp', qg, k) * scale
        causal = jnp.tril(jnp.ones((s, s), dtype=bool))
        scores = jnp.where(causal, scores, jnp.float32(-1e+30))
        probs = jax.nn.softmax(scores, axis=-1)
        out = jnp.einsum('bkgqp,bkpd->bkgqd', probs, v).reshape(b, H, s, D)
        out = out.transpose(0, 2, 1, 3).reshape(b, s, H * D)
        return out @ Wo

    def _L0_ffn_ref(x, gate_w, w1, w2):
        import jax, jax.numpy as jnp
        import numpy as np
        NUM_EXPERTS = 8
        EXPERT_CAPACITY = 2.0
        DIM = 128
        HIDDEN_DIM = 512
        n, t, d = x.shape
        e = gate_w.shape[0]
        k = int(EXPERT_CAPACITY * t / e)
        scores = jnp.einsum('ntd,ed->nte', x, gate_w)
        probs = jax.nn.softmax(scores, axis=-1)
        g, m = jax.lax.top_k(probs.transpose(0, 2, 1), k)
        batch_idx = jnp.arange(n)[:, None, None]
        xin = x[batch_idx, m]
        h = jnp.einsum('nekd,edf->nekf', xin, w1)
        h = jax.nn.gelu(h, approximate=False)
        h = jnp.einsum('nekf,efd->nekd', h, w2)
        out_tok = g[..., None] * h
        out = jnp.zeros((n, t, d), dtype=x.dtype).at[batch_idx, m].add(out_tok)
        return out

    def _L1_attn_ref(x, w_q, w_k, w_v, w_o, rel_emb):
        import jax, jax.numpy as jnp
        import numpy as np
        from math import sqrt
        HEADS = 16
        MODEL_DIM = 128
        DIM_PER_HEAD = MODEL_DIM // HEADS
        MAX_REL_POS = 32
        ROPE_BASE = 10000.0
        NEG_INF = -1e+18

        def _rope_cos_sin(seq_len, dim):
            inv_freq = 1.0 / ROPE_BASE ** (jnp.arange(0, dim, 2, dtype=jnp.float32) / dim)
            t = jnp.arange(seq_len, dtype=jnp.float32)
            ang = jnp.outer(t, inv_freq)
            return (jnp.cos(ang), jnp.sin(ang))

        def _apply_rotary_interleave(x, cos, sin):
            B, H, L, D = x.shape
            x_ = x.reshape(B, H, L, D // 2, 2)
            xe, xo = (x_[..., 0], x_[..., 1])
            c = cos[None, None, :, :]
            s = sin[None, None, :, :]
            oe = xe * c - xo * s
            oo = xe * s + xo * c
            return jnp.stack([oe, oo], axis=-1).reshape(B, H, L, D)
        B, L, _ = x.shape

        def shape(t):
            return t.reshape(B, L, HEADS, DIM_PER_HEAD).transpose(0, 2, 1, 3)
        q = shape(x @ w_q.T)
        k = shape(x @ w_k.T)
        v = shape(x @ w_v.T)
        cos, sin = _rope_cos_sin(L, DIM_PER_HEAD)
        q = _apply_rotary_interleave(q, cos, sin)
        k = _apply_rotary_interleave(k, cos, sin)
        q = q / sqrt(DIM_PER_HEAD)
        scores = jnp.einsum('bhqd,bhkd->bhqk', q, k)
        pos = jnp.arange(L)
        rel_idx = jnp.clip(pos[None, :] - pos[:, None], -MAX_REL_POS, MAX_REL_POS) + MAX_REL_POS
        rel = rel_emb[rel_idx]
        scores = scores + jnp.einsum('bhqd,qkd->bhqk', q, rel)
        causal = jnp.tril(jnp.ones((L, L), dtype=bool))
        scores = jnp.where(causal[None, None], scores, NEG_INF)
        attn = jax.nn.softmax(scores, axis=-1)
        ctx = jnp.einsum('bhqk,bhkd->bhqd', attn, v)
        ctx = ctx + jnp.einsum('bhqk,qkd->bhqd', attn, rel)
        out = ctx.transpose(0, 2, 1, 3).reshape(B, L, MODEL_DIM) @ w_o.T
        return out

    def _L1_ffn_ref(x, W1, b1, W2, b2, Wr, br):
        import jax, jax.numpy as jnp
        import numpy as np
        E = 8
        K = 2
        D = 128
        P = 512
        B, S, _ = x.shape
        xf = x.reshape(B * S, D)
        scores = xf @ Wr + br
        _, top_idx = jax.lax.top_k(scores, K)
        mask = jax.nn.one_hot(top_idx, E, dtype=scores.dtype).sum(-2) > 0
        router_weights = jax.nn.softmax(jnp.where(mask, scores, -jnp.inf), axis=-1)
        h = jax.nn.gelu(jnp.einsum('td,edp->etp', xf, W1) + b1[:, None, :])
        y = jnp.einsum('etp,epd->etd', h, W2) + b2[:, None, :]
        out = jnp.einsum('te,etd->td', router_weights, y)
        return out.reshape(B, S, D)
    x = L0_attn_hidden_states
    mod = (_silu(L0_c) @ L0_wmod).reshape(L0_c.shape[0], 6, 1, -1)
    sa, ca, ga, sb, cb, gb = (mod[:, 0], mod[:, 1], mod[:, 2], mod[:, 3], mod[:, 4], mod[:, 5])
    ga = (2 * (ga >= 0) - 1) * jnp.maximum(jnp.abs(ga), 0.25)
    gb = (2 * (gb >= 0) - 1) * jnp.maximum(jnp.abs(gb), 0.25)
    h = _layernorm(x, axis=-1) * (1 + ca) + sa
    x = x + ga * _L0_attn_ref(h, L0_attn_Wq, L0_attn_Wk, L0_attn_Wv, L0_attn_Wo)
    h = _layernorm(x, axis=-1) * (1 + cb) + sb
    x = x + gb * _L0_ffn_ref(h, L0_ffn_gate_w, L0_ffn_w1, L0_ffn_w2)
    mod = (_silu(L1_c) @ L1_wmod).reshape(L1_c.shape[0], 6, 1, -1)
    sa, ca, ga, sb, cb, gb = (mod[:, 0], mod[:, 1], mod[:, 2], mod[:, 3], mod[:, 4], mod[:, 5])
    ga = (2 * (ga >= 0) - 1) * jnp.maximum(jnp.abs(ga), 0.25)
    gb = (2 * (gb >= 0) - 1) * jnp.maximum(jnp.abs(gb), 0.25)
    h = _layernorm(x, axis=-1) * (1 + ca) + sa
    x = x + ga * _L1_attn_ref(h, L1_attn_w_q, L1_attn_w_k, L1_attn_w_v, L1_attn_w_o, L1_attn_rel_emb)
    h = _layernorm(x, axis=-1) * (1 + cb) + sb
    x = x + gb * _L1_ffn_ref(h, L1_ffn_W1, L1_ffn_b1, L1_ffn_W2, L1_ffn_b2, L1_ffn_Wr, L1_ffn_br)
    return x

_drawn_inputs = setup_inputs


def setup_inputs(seed=0):
    import zlib

    import numpy as np

    out = dict(_drawn_inputs(seed))
    spreads = {}
    factors = {'L0_attn_Wq': 8.0,
     'L0_attn_Wk': 8.0,
     'L0_attn_Wv': 8.0,
     'L0_attn_Wo': 8.0,
     'L0_ffn_gate_w': 8.0,
     'L0_ffn_w1': 8.0,
     'L0_ffn_w2': 8.0,
     'L0_c': 7.064,
     'L0_wmod': 7.047,
     'L1_attn_w_q': 8.0,
     'L1_attn_w_k': 8.0,
     'L1_attn_w_v': 8.0,
     'L1_attn_w_o': 8.0,
     'L1_attn_rel_emb': 8.0,
     'L1_ffn_b1': 64.0,
     'L1_ffn_b2': 56.237,
     'L1_ffn_br': 29.975}
    for name, (base, spread) in spreads.items():
        noise = np.random.default_rng([zlib.crc32(name.encode()), seed]).standard_normal(out[name].shape)
        drawn = base * np.exp(spread * noise) if base else spread * noise
        out[name] = jnp.asarray(drawn.astype(out[name].dtype))
    for name, factor in factors.items():
        out[name] = (out[name] * factor).astype(out[name].dtype)
    return out
```

```python
from contextlib import ExitStack

import concourse.bass as bass
import numpy as np
from concourse import mybir

F32 = mybir.dt.float32
BF16 = mybir.dt.bfloat16
ALU = mybir.AluOpType
ACT = mybir.ActivationFunctionType
AX = mybir.AxisListType

P = 128
B, S, D = 8, 512, 128
NT = S // P
BANK = 512
H0, KV0, HD0 = 16, 4, 64
PAIRS = H0 // 2
H1, HD1 = 16, 8
RMAX = 32
NREL = RMAX + 1
CH = 16
NCH = P // CH
GRP = 4
E, F = 8, 512
FC = F // P
CAP = 2 * S // E
EPS = 1e-5
NEG = -1e30
BAND_E0 = P + CH
BAND_W = BAND_E0 + P

ARENA = 30700

ENGINES = ("tensor", "vector", "scalar", "gpsimd", "sync")


class Token:

    def __init__(self, owner):
        self.owner, self.used, self.value = owner, False, None


class DmaGroup:

    def __init__(self, sem):
        self.sem, self.count = sem, 0
        self.used = True

    @property
    def value(self):
        return 16 * self.count


class Program:

    def __init__(self, nc, ctx):
        self.nc, self.ctx = nc, ctx
        self.queue = {e: [] for e in ENGINES}
        self.sem = {e: ctx.enter_context(nc.semaphore(f"{e}_progress")) for e in ENGINES}
        self.last = {}

    def op(self, engine, wait, emit, *args, **kw):
        token = Token(engine)
        waits = [w for w in flat(wait) if w is not None]
        for w in waits:
            w.used = True
        self.queue[engine].append((waits, lambda e: emit(e, *args, **kw), token))
        self.last[engine] = token
        return token

    def pe(self, wait, emit, *args, **kw):
        return self.op("tensor", wait, emit, *args, **kw)

    def dve(self, wait, emit, *args, **kw):
        return self.op("vector", wait, emit, *args, **kw)

    def act(self, wait, emit, *args, **kw):
        return self.op("scalar", wait, emit, *args, **kw)

    def pool(self, wait, emit, *args, **kw):
        return self.op("gpsimd", [wait, self.last.get("gpsimd")], emit, *args, **kw)

    def dma_group(self, name):
        return DmaGroup(self.ctx.enter_context(self.nc.semaphore(name)))

    def dma(self, group, out, src, wait=(), engine="sync"):
        waits = [w for w in flat(wait) if w is not None]
        for w in waits:
            w.used = True
        group.count += 1
        self.queue[engine].append((waits, lambda e: e.dma_start(out, src).then_inc(group.sem, 16), None))

    def wait_only(self, engine, wait):
        waits = [w for w in flat(wait) if w is not None]
        for w in waits:
            w.used = True
        self.queue[engine].append((waits, None, None))

    def run(self, block):
        for e in ENGINES:
            n = 0
            for _, _, token in self.queue[e]:
                if token is not None and token.used:
                    n += 1
                    token.value = n
        for e in ENGINES:
            getter = {"tensor": block.tensor, "vector": block.vector, "scalar": block.scalar,
                      "gpsimd": block.gpsimd, "sync": block.sync}[e]

            def body(eng, items=self.queue[e], own=self.sem[e]):
                passed = {}
                for waits, emit, token in items:
                    need = {}
                    for w in waits:
                        s = w.sem if isinstance(w, DmaGroup) else self.sem[w.owner]
                        k = id(s) if isinstance(w, DmaGroup) else w.owner
                        if w.value > max(passed.get(k, 0), need.get(k, (None, 0))[1]):
                            need[k] = (s, w.value)
                    for k, (s, v) in need.items():
                        eng.wait_ge(s, v)
                        passed[k] = v
                    if emit is None:
                        continue
                    ins = emit(eng)
                    if token is not None and token.used:
                        ins.then_inc(own, 1)

            getter(body)


def activation(eng, *args, **kw):
    return eng.activation(*args, **kw)


def bn_aggr(eng, *args, **kw):
    return eng.bn_aggr(*args, **kw)


def bn_stats(eng, *args, **kw):
    return eng.bn_stats(*args, **kw)


def copy(eng, *args, **kw):
    return eng.copy(*args, **kw)


def match_replace(eng, *args, **kw):
    return eng.match_replace(*args, **kw)


def matmul(eng, *args, **kw):
    return eng.matmul(*args, **kw)


def max8(eng, *args, **kw):
    return eng.max(*args, **kw)


def memset(eng, *args, **kw):
    return eng.memset(*args, **kw)


def reciprocal(eng, *args, **kw):
    return eng.reciprocal(*args, **kw)


def scalar_tensor_tensor(eng, *args, **kw):
    return eng.scalar_tensor_tensor(*args, **kw)


def tensor_copy(eng, *args, **kw):
    return eng.tensor_copy(*args, **kw)


def tensor_reduce(eng, *args, **kw):
    return eng.tensor_reduce(*args, **kw)


def tensor_scalar(eng, *args, **kw):
    return eng.tensor_scalar(*args, **kw)


def tensor_tensor(eng, *args, **kw):
    return eng.tensor_tensor(*args, **kw)


def tensor_tensor_scan(eng, *args, **kw):
    return eng.tensor_tensor_scan(*args, **kw)


def transpose(eng, *args, **kw):
    return eng.transpose(*args, **kw)


def flat(x):
    if isinstance(x, (list, tuple)):
        return [z for y in x for z in flat(y)]
    return [x]


def rope_tables(seq, dim, pick_even):
    inv = 1.0 / np.float32(10000.0) ** (np.arange(0, dim, 2, dtype=np.float32) / np.float32(dim))
    ang = np.arange(seq, dtype=np.float32)[:, None] * inv.astype(np.float32)[None, :]
    cos, sin = np.cos(ang), np.sin(ang)
    if pick_even:
        cos = np.concatenate([cos, cos], -1)[:, 0::2]
        sin = np.concatenate([sin, sin], -1)[:, 0::2]
    return np.repeat(cos.T, 2, 0).astype(np.float32), np.repeat(sin.T, 2, 0).astype(np.float32)


def shape_constants():
    c0, s0 = rope_tables(S, HD0, True)
    c1, s1 = rope_tables(S, HD1, False)
    p = np.arange(P)
    out = {
        "rope0": np.stack([np.tile(c0, (P // HD0, 1)), np.tile(s0, (P // HD0, 1))], 1),
        "rope1": np.stack([np.tile(c1, (P // HD1, 1)), np.tile(s1, (P // HD1, 1))], 1),
        "ident": np.eye(P, dtype=np.float32),
        "causal": np.where(p[:, None] <= p[None, :], 0.0, NEG).astype(np.float32),
        "chunk_mask": (p[None, :] % CH == p[:, None] // HD1).astype(np.float32),
        "head_rows": (p[:, None] // HD1 == np.arange(H1)[None, :]).astype(np.float32),
        "iota": np.tile(np.arange(P, dtype=np.float32), (P, 1)),
        "iota_col": p[:, None].astype(np.float32),
    }
    fold = np.zeros((P, 8, P), np.float32)
    for h in range(8):
        for i in range(CH):
            for d in range(HD1):
                fold[i * HD1 + d, h, h * HD1 + d] = 1.0
    out["fold"] = fold
    out["spread"] = (p[:, None, None] == np.arange(H1)[None, :, None] * HD1 + p[None, None, :] % HD1).astype(np.float32)
    keep = np.ones((P, NT * E), np.float32)
    keep[:, 0::E] = 0.0
    out["keep"] = keep
    return out


def band_index():
    i = np.arange(CH)[:, None]
    e = np.arange(BAND_W)[None, :] - BAND_E0
    return np.clip(e - i, -RMAX, 0) + RMAX


def build(nc, t, out):
    ctx = ExitStack()
    with ctx:
        prog = Program(nc, ctx)
        pe, dve, act, pool = prog.pe, prog.dve, prog.act, prog.pool

        def sb(name, shape, dt=F32):
            return ctx.enter_context(nc.sbuf_tensor(name, shape, dt))

        psum = ctx.enter_context(nc.psum_tensor("psum", [P, 8, BANK], F32))
        xT = sb("xT", [P, B * S])
        ffw = sb("ffw", [P, 2 * E * F])
        w1 = ffw[:, 0:E * F].rearrange("p (e f) -> p e f", e=E)
        w2 = ffw[:, E * F:2 * E * F].rearrange("p (e c d) -> p e c d", e=E, c=FC)
        arena = sb("arena", [P, ARENA])
        ident = sb("ident", [P, P])
        ident_bf = sb("ident_bf", [P, P], BF16)
        neg_ident = sb("neg_ident", [P, P], BF16)
        ones_bf = sb("ones_bf", [P, P], BF16)
        causal_f = sb("causal_f", [P, P])
        causal = sb("causal", [P, P], BF16)
        modc = sb("modc", [P, 2, B])
        mod_e = sb("mod_e", [P, 2, B])
        mod = sb("mod", [P, 2, 6, B])
        modg = sb("modg", [P, 2, 2, 2, B])
        prob = sb("prob", [P, 2, 4 * BANK])
        colmax = sb("colmax", [P, 2, BANK])
        rowmax = sb("rowmax", [P, 2, GRP])
        negmax = sb("negmax", [P, 2, GRP, P], BF16)
        hT = sb("hT", [P, 2, S])
        rope_a = sb("rope_a", [P, 2, S])
        rope_b = sb("rope_b", [P, 2, S])
        recip = sb("recip", [64, BANK])
        stats = sb("stats", [P, NT, 6])
        moments = sb("moments", [P, NT, 2])
        rstd = sb("rstd", [P, NT])
        minus_half = sb("minus_half", [P, NT])

        class Arena:
            at = 0

        def carve(shape, restart=False):
            if restart:
                Arena.at = 0
            n = int(np.prod(shape))
            a = arena[:, Arena.at:Arena.at + n]
            Arena.at += n
            assert Arena.at <= ARENA, Arena.at
            names = "abcd"[:len(shape)]
            if len(shape) == 1:
                return a
            return a.rearrange(f"p ({' '.join(names)}) -> p {' '.join(names)}",
                               **{k: v for k, v in zip(names, shape)})

        bank_free = [[] for _ in range(8)]

        def mm(wait, o, lhsT, rhs, start, stop=True):
            return pe(wait, matmul, o, lhsT, rhs, start=start, stop=stop,
                                               skip_group_check=True)

        def barrier():
            ends = [prog.last[e] for e in ENGINES if e in prog.last]
            for e in ENGINES:
                prog.wait_only(e, ends)

        g_const, g_x, g_w0, g_ff0 = (prog.dma_group(n) for n in ("d_const", "d_x", "d_w0", "d_ff0"))
        g_w1, g_ff1, g_out = (prog.dma_group(n) for n in ("d_w1", "d_ff1", "d_out"))

        xn = carve([B * NT, D], restart=True)
        wq = carve([D * H0 * HD0 // P])
        wq_rot = carve([D * H0 * HD0 // P])
        wk = carve([KV0 * P])
        wk_rot = carve([KV0 * P])
        wv = carve([KV0 * HD0])
        wo = carve([PAIRS, D])
        gate = carve([E])
        rope0 = carve([2, S])
        prob_tok = carve([NT, B, E])
        gmax = carve([NT])
        gsum = carve([NT])
        gexp = carve([NT, E])
        qT = carve([PAIRS, S])
        k_even = carve([KV0, S])
        k_odd = carve([KV0, S])
        v_ones = carve([NT, KV0, P])
        ctxT = carve([PAIRS, S])
        wmod = carve([2, 6 * D])

        prog.dma(g_const, ident[:, :], t["ident"])
        prog.dma(g_const, causal_f[:, :], t["causal"])
        prog.dma(g_const, modc[:, 0, :], t["L0_cT"])
        prog.dma(g_const, modc[:, 1, :], t["L1_cT"])
        prog.dma(g_const, wmod[:, 0, :], t["L0_wmod"])
        prog.dma(g_const, wmod[:, 1, :], t["L1_wmod"])
        prog.dma(g_const, rope0, t["rope0"])
        x_tok = t["x"].rearrange("b (n p) d -> p (b n) d", p=P)
        for h in range(2):
            n = B * NT // 2
            prog.dma(g_x, xn[:, h * n:(h + 1) * n, :], x_tok[:, h * n:(h + 1) * n, :])
        prog.dma(g_w0, wq, t["Wq"])
        for c in range(2):
            prog.dma(g_w0, wk.rearrange("p (k c d) -> p k c d", k=KV0, c=2)[:, :, c, :],
                     t["Wk"].rearrange("p (k d) -> p k d", k=KV0))
        prog.dma(g_w0, wv, t["Wv"])
        prog.dma(g_w0, wo, t["Wo"].rearrange("(n p) d -> p n d", p=P))
        prog.dma(g_w0, gate, t["gateT"])
        prog.dma(g_ff0, w1, t["L0_w1"].rearrange("e d f -> d e f"))
        prog.dma(g_ff0, w2, t["L0_w2"].rearrange("e (c p) d -> p e c d", p=P))

        t_ones = dve([], memset, ones_bf[:, :], 1.0)
        t_ident = dve([g_const], tensor_copy, ident_bf[:, :], ident[:, :])
        t_nid = dve([], tensor_scalar, neg_ident[:, :], ident[:, :], -1.0, None, ALU.mult)
        t_causal = dve([], tensor_copy, causal[:, :], causal_f[:, :])
        consts_ready = [t_ones, t_ident, t_nid, t_causal]

        t_e = act([g_const], activation, mod_e[:, :, :], modc[:, :, :], ACT.Exp, scale=-1.0)
        t_e = dve([t_e], tensor_scalar, mod_e[:, :, :], mod_e[:, :, :], 1.0, None, ALU.add)
        t_e = dve([t_e], reciprocal, mod_e[:, :, :], mod_e[:, :, :])
        t_silu = dve([t_e], tensor_tensor, modc[:, :, :], modc[:, :, :], mod_e[:, :, :], ALU.mult)
        for L in range(2):
            for j in range(6):
                t_mod = mm([t_silu, g_const], psum[:, 7, (L * 6 + j) * B:(L * 6 + j + 1) * B],
                           wmod[:, L, j * D:(j + 1) * D], modc[:, L, :], start=(L + j == 0))
        t_mod = dve([t_mod], tensor_copy, 
            mod[:, :, :, :].rearrange("p a b c -> p (a b c)"), psum[:, 7, 0:12 * B])
        bank_free[7] = [t_mod]
        SH_A, SC_A, GA_A, SH_B, SC_B, GA_B = range(6)
        t_sc = [dve([t_mod], tensor_scalar, mod[:, :, j, :], mod[:, :, j, :], 1.0, None, ALU.add)
                for j in (SC_A, SC_B)]
        for n, j in enumerate((GA_A, GA_B)):
            g, sgn, mag = mod[:, :, j, :], modg[:, :, n, 0, :], modg[:, :, n, 1, :]
            t1 = dve([t_mod], tensor_scalar, sgn, g, 0.0, 2.0, ALU.is_ge, ALU.mult)
            t2 = dve([t1], tensor_scalar, sgn, sgn, -1.0, None, ALU.add)
            t3 = dve([t_mod], tensor_scalar, mag, g, -1.0, None, ALU.mult)
            t3 = dve([t3], tensor_tensor, mag, mag, g, ALU.max)
            t3 = dve([t3], tensor_scalar, mag, mag, 0.25, None, ALU.max)
            t_g = dve([t2, t3], tensor_tensor, g, sgn, mag, ALU.mult)
            t_sc.append(t_g)
        mod_ready = t_sc

        def rotate(dst, src, wait):
            d2, s2 = (a.rearrange("p (n two) -> p n two", two=2) for a in (dst, src))
            a = dve(wait, tensor_scalar, d2[:, :, 0:1], s2[:, :, 1:2], -1.0, None, ALU.mult)
            b = dve([], tensor_copy, d2[:, :, 1:2], s2[:, :, 0:1])
            return [a, b]

        w0_ready = [g_w0] + rotate(wq_rot, wq, [g_w0]) + rotate(wk_rot, wk, [])
        t_mh = pool([], memset, minus_half[:, :], -0.5)
        t_kz = [pool([], memset, k_even[64:128, :, :], 0.0),
                pool([], memset, k_odd[0:64, :, :], 0.0),
                pool([], memset, v_ones[:, :, :, HD0:P], 1.0)]

        x_ready = [[] for _ in range(B)]
        for b in range(B):
            k = b % 4
            for n in range(NT):
                tk = pe([g_x, g_const, bank_free[k]], transpose, 
                    psum[:, k, n * P:(n + 1) * P], xn[:, b * NT + n, :], ident[:, :])
            tk = act([tk], copy, xT[:, b * S:(b + 1) * S], psum[:, k, :])
            bank_free[k] = [tk]
            x_ready[b] = [tk]

        hT_free = [[], []]
        ln_count = [0]

        def layer_norm(b, L, sc, sh, xn_out, xn_wait, banks=(0, 1)):
            k0, k1 = banks
            for n in range(NT):
                tk = pe([x_ready[b], bank_free[k0], g_const], transpose, 
                    psum[:, k0, n * P:(n + 1) * P], xT[:, b * S + n * P:b * S + (n + 1) * P], ident[:, :])
            for n in range(NT):
                ts = dve([tk], bn_stats, stats[:, n, :], psum[:, k0, n * P:(n + 1) * P])
            for n in range(NT):
                ta = dve([ts], bn_aggr, moments[:, n, :], stats[:, n, :])
            tr = pool([ta], tensor_scalar, moments[:, :, 1], moments[:, :, 1], EPS, None, ALU.add)
            tr = pool([tr, t_mh], tensor_tensor, rstd[:, :], moments[:, :, 1], minus_half[:, :], ALU.pow)
            for n in range(NT):
                tx = dve([tr, xn_wait], tensor_scalar, 
                    xn_out[:, n, :], psum[:, k0, n * P:(n + 1) * P], moments[:, n, 0:1], rstd[:, n:n + 1],
                    ALU.subtract, ALU.mult)
            bank_free[k0] = [tx]
            for n in range(NT):
                tk = pe([tx, bank_free[k1]], transpose, 
                    psum[:, k1, n * P:(n + 1) * P], xn_out[:, n, :], ident[:, :])
            i = ln_count[0] % 2
            ln_count[0] += 1
            th = dve([tk, hT_free[i], mod_ready], tensor_scalar, 
                hT[:, i, :], psum[:, k1, :], mod[:, L, sc, b:b + 1], mod[:, L, sh, b:b + 1], ALU.mult, ALU.add)
            bank_free[k1] = [th]
            return i, th, tx, tk

        SLOT = {0: (0, 1, 2, 3), 1: (4, 5)}
        AUX, CTX = 6, 7
        ORDER = [(3, 0), (1, 1), (2, 0), (0, 1)]

        def attention(scale, n_groups, emit_scores, emit_values, prob_free):
            units = [(g, i, slot) for g in range(n_groups) for i, slot in ORDER]
            st = [dict(g=g, i=i, k0=SLOT[slot][0], n=u) for u, (g, i, slot) in enumerate(units)]
            cm_free = [[], []]
            dg_free = [[], []]

            def scores(u):
                k0, i, z = u["k0"], u["i"], u["n"] % 2
                u["scored"] = emit_scores(u)
                if i:
                    u["cm"] = dve([u["scored"], cm_free[z]], tensor_reduce, 
                        colmax[:, z, :], psum[:, k0:k0 + i + 1, :].rearrange("p j c -> p c j"), AX.X, ALU.max)
                else:
                    u["cm"] = dve([u["scored"], cm_free[z]], tensor_copy, 
                        colmax[:, z, :], psum[:, k0, :])

            def maxima(u):
                z = u["n"] % 2
                for h in range(GRP):
                    tk = pe([u["cm"], bank_free[AUX]], transpose, 
                        psum[:, AUX, h * P:(h + 1) * P], colmax[:, z, h * P:(h + 1) * P], ident[:, :])
                cm_free[z] = [tk]
                tr = dve([tk], tensor_reduce, 
                    rowmax[:, z, :], psum[:, AUX, :].rearrange("p (h k) -> p h k", h=GRP), AX.X, ALU.max)
                bank_free[AUX] = [tr]
                for h in range(GRP):
                    td = dve([tr, dg_free[z]], tensor_scalar, 
                        negmax[:, z, h, :], neg_ident[:, :], rowmax[:, z, h:h + 1], None, ALU.mult)
                u["diag"] = td

            def shift_and_exp(u):
                k0, i, z = u["k0"], u["i"], u["n"] % 2
                for j in range(i + 1):
                    tk = mm([u["diag"], u["cm"]], psum[:, k0 + j, :], ones_bf[:, :], negmax[:, z, :, :], False)
                dg_free[z] = [tk]
                u["prob"] = act([tk, prob_free[z]], activation, 
                    prob[:, z, 0:(i + 1) * BANK], psum[:, k0:k0 + i + 1, :], ACT.Exp, scale=scale)
                for j in range(i + 1):
                    bank_free[k0 + j] = [u["prob"]]

            scores(st[0])
            maxima(st[0])
            if len(st) > 1:
                scores(st[1])
            for n, u in enumerate(st):
                shift_and_exp(u)
                if n:
                    prob_free[(n - 1) % 2] = [emit_values(st[n - 1])]
                if n + 1 < len(st):
                    maxima(st[n + 1])
                if n + 2 < len(st):
                    scores(st[n + 2])
            prob_free[st[-1]["n"] % 2] = [emit_values(st[-1])]

        prob_free = [[], []]
        attn0_done = []
        ctx_free = []
        rope_free = [[], []]
        for b in range(B):
            i, h_ready, _, _ = layer_norm(b, 0, SC_A, SH_A, xn[:, b * NT:(b + 1) * NT, :], x_ready[b])
            h_in = hT[:, i, :]
            rot = [0]

            def project(w, w_rot, finish):
                z = rot[0] % 2
                ka, kb = 2 * z, 2 * z + 1
                rot[0] += 1
                ta = mm([h_ready, w0_ready, bank_free[ka]], psum[:, ka, :], w, h_in, True)
                tb = mm([bank_free[kb]], psum[:, kb, :], w_rot, h_in, True)
                ma = dve([ta, rope_free[z]], tensor_tensor, rope_a[:, z, :], psum[:, ka, :], rope0[:, 0, :], ALU.mult)
                mb = dve([tb], tensor_tensor, rope_b[:, z, :], psum[:, kb, :], rope0[:, 1, :], ALU.mult)
                bank_free[ka], bank_free[kb] = [ma], [mb]
                rope_free[z] = finish([ma, mb], z)
                return rope_free[z]

            k_ready = []
            for kv in range(KV0):
                def fin(w, z, kv=kv):
                    a = pool([w, attn0_done, t_kz], tensor_tensor, 
                        k_even[0:64, kv, :], rope_a[0:64, z, :], rope_b[0:64, z, :], ALU.add)
                    c = pool([], tensor_tensor, 
                        k_odd[64:128, kv, :], rope_a[64:128, z, :], rope_b[64:128, z, :], ALU.add)
                    return [a, c]
                k_ready += project(wk[:, kv * P:(kv + 1) * P], wk_rot[:, kv * P:(kv + 1) * P], fin)
            for n in range(NT):
                k = 4 + n % 2
                tv = mm([h_ready, bank_free[k]], psum[:, k, 0:KV0 * HD0], h_in[:, n * P:(n + 1) * P], wv, True)
                tv = act([tv, attn0_done, t_kz], copy, 
                    v_ones[:, n, :, 0:HD0], psum[:, k, 0:KV0 * HD0].rearrange("p (k d) -> p k d", k=KV0))
                bank_free[k] = [tv]
            v_ready = tv
            q_ready = []
            for p in range(PAIRS):
                def fin(w, z, p=p):
                    return [pool([w, attn0_done], tensor_tensor, 
                        qT[:, p, :], rope_a[:, z, :], rope_b[:, z, :], ALU.add)]
                q_ready.append(project(wq[:, p * P:(p + 1) * P], wq_rot[:, p * P:(p + 1) * P], fin))
            hT_free[i] = [prog.last["tensor"]]

            def scores0(u):
                g, i, k0 = u["g"], u["i"], u["k0"]
                for j in range(i + 1):
                    for par, kk in enumerate((k_even, k_odd)):
                        tk = mm([q_ready[2 * g], q_ready[2 * g + 1], k_ready, bank_free[k0 + j]],
                                psum[:, k0 + j, par * 256:(par + 1) * 256].rearrange("p (a q) -> p a q", a=2),
                                kk[:, g, j * P:(j + 1) * P], qT[:, 2 * g:2 * g + 2, i * P:(i + 1) * P],
                                start=(par == 0))
                return mm([consts_ready], psum[:, k0 + i, :], ident_bf[:, :],
                          causal[:, :].unsqueeze(1).to_broadcast([P, GRP, P]), False)

            def values0(u):
                g, i, z = u["g"], u["i"], u["n"] % 2
                for j in range(i + 1):
                    tk = mm([u["prob"], v_ready, bank_free[CTX]], psum[:, CTX, :], v_ones[:, j, g, :],
                            prob[:, z, j * BANK:(j + 1) * BANK], start=(j == 0))
                tr = dve([tk], reciprocal, recip[:, :], psum[64:128, CTX, :])
                for par in range(2):
                    tm = dve([tr, ctx_free], tensor_tensor, 
                        ctxT[par * 64:par * 64 + 64, 2 * g:2 * g + 2, i * P:(i + 1) * P],
                        psum[0:64, CTX, par * 256:(par + 1) * 256].rearrange("p (a q) -> p a q", a=2),
                        recip[:, par * 256:(par + 1) * 256].rearrange("p (a q) -> p a q", a=2), ALU.mult)
                bank_free[CTX] = [tm]
                return tk

            attention(HD0 ** -0.5, KV0, scores0, values0, prob_free)
            attn0_done = [prog.last["tensor"]]
            ctx_ready = [prog.last["vector"]]
            for p in range(PAIRS):
                tk = mm([ctx_ready, bank_free[0]], psum[:, 0, :], wo[:, p, :], ctxT[:, p, :], start=(p == 0))
            ctx_free = [tk]
            cols = slice(b * S, (b + 1) * S)
            tx = dve([tk, mod_ready], scalar_tensor_tensor, 
                xT[:, cols], psum[:, 0, :], mod[:, 0, GA_A, b:b + 1], xT[:, cols], ALU.mult, ALU.add)
            bank_free[0] = [tx]
            x_ready[b] = [tx]

            i, h_ready, _, _ = layer_norm(b, 0, SC_B, SH_B, xn[:, b * NT:(b + 1) * NT, :], [])
            for n in range(NT):
                tk = mm([h_ready, g_w0, bank_free[2]], psum[:, 2, n * E:(n + 1) * E],
                        hT[:, i, n * P:(n + 1) * P], gate, start=(n == 0))
            hT_free[i] = [tk]
            gsc = psum[:, 2, 0:NT * E].rearrange("p (n e) -> p n e", n=NT)
            t1 = dve([tk], tensor_reduce, gmax, gsc, AX.X, ALU.max)
            t1 = dve([t1], tensor_tensor, gexp, gsc, gmax.unsqueeze(2).to_broadcast([P, NT, E]), ALU.subtract)
            bank_free[2] = [t1]
            t1 = act([t1], activation, gexp, gexp, ACT.Exp)
            t1 = dve([t1], tensor_reduce, gsum, gexp, AX.X, ALU.add)
            t1 = dve([t1], reciprocal, gsum, gsum)
            t1 = dve([t1], tensor_tensor, 
                prob_tok[:, :, b, :], gexp, gsum.unsqueeze(2).to_broadcast([P, NT, E]), ALU.mult)
        barrier()

        NBE = B * E
        xn = carve([B * NT, D], restart=True)
        Arena.at = ARENA - NT * NBE
        prob_keep = carve([NT, B, E])
        Arena.at = B * NT * D
        t_pk = pool([], tensor_copy, prob_keep, prob_tok)
        barrier()
        prob_tok = prob_keep
        xin = carve([E, B, CAP])
        onehot = carve([NT, E, CAP])
        hid = carve([2, FC, 4 * CAP])
        back = carve([2, S])
        slot_gate = carve([B, E])
        posT = carve([NT, NBE])
        iota = carve([P])
        iota_col = carve([1])
        mark = Arena.at
        assert mark <= ARENA - NT * NBE
        Arena.at = B * NT * D + E * B * CAP + NT * E * CAP
        pw = carve([S])
        work = carve([S])
        top8 = carve([8])
        sel = carve([S])
        eq = carve([S])
        cum = carve([S])
        cnt = carve([1])
        pos_bf = rope_a[:, 0, :].bitcast(BF16)[:, 0:S]
        g_iota = prog.dma_group("d_iota")
        prog.dma(g_iota, iota, t["iota"])
        prog.dma(g_iota, iota_col, t["iota_col"])
        R = slice(0, NBE)
        for n in range(NT):
            tk = pe([], transpose, psum[0:NBE, 0, n * P:(n + 1) * P],
                                                   prob_tok[:, n, :, :].rearrange("p b e -> p (b e)"), ident[:, :])
        tp = dve([tk], tensor_copy, pw[R, :], psum[R, 0, :])
        tw = dve([tk], tensor_copy, work[R, :], psum[R, 0, :])
        bank_free[0] = [tw]
        for r in range(CAP // 8):
            tm = dve([tw], max8, top8[R, :], work[R, :])
            if r < CAP // 8 - 1:
                tw = dve([tm], match_replace, work[R, :], top8[R, :], work[R, :], -1.0)
        thr = top8[R, 7:8]
        t1 = dve([tm], tensor_scalar, sel[R, :], pw[R, :], thr, None, ALU.is_gt)
        t2 = dve([tm], tensor_scalar, eq[R, :], pw[R, :], thr, None, ALU.is_equal)
        t3 = dve([t1], tensor_reduce, cnt[R, :], sel[R, :], AX.X, ALU.add)
        t4 = dve([], memset, work[R, :], 1.0)
        t5 = dve([t2, t4], tensor_tensor_scan, cum[R, :], work[R, :], eq[R, :], 0.0, ALU.mult, ALU.add)
        t6 = dve([t3, t5], tensor_scalar, cum[R, :], cum[R, :], cnt[R, 0:1], float(CAP), ALU.add, ALU.is_le)
        t7 = dve([t6], tensor_tensor, eq[R, :], eq[R, :], cum[R, :], ALU.mult)
        t8 = dve([t7], tensor_tensor, sel[R, :], sel[R, :], eq[R, :], ALU.add)
        t9 = dve([t8], tensor_tensor_scan, cum[R, :], work[R, :], sel[R, :], 0.0, ALU.mult, ALU.add)
        t9 = dve([t9], tensor_tensor, cum[R, :], cum[R, :], sel[R, :], ALU.mult)
        t9 = dve([t9], tensor_scalar, cum[R, :], cum[R, :], -1.0, None, ALU.add)
        t10 = dve([t9], tensor_copy, pos_bf[R, :], cum[R, :])
        for n in range(NT):
            tk = pe([t9], transpose, psum[:, 1, n * NBE:(n + 1) * NBE],
                                                     cum[R, n * P:(n + 1) * P], ident[R, R])
        tpos = dve([tk], tensor_copy, posT, psum[:, 1, 0:NT * NBE].rearrange("p (n r) -> p n r", n=NT))
        bank_free[1] = [tpos]
        select_done = [tk, t10, tpos]

        oh_free = []
        xin_ready = []
        for b in range(B):
            for n in range(NT):
                oh_ready = dve([tpos, g_iota, oh_free], tensor_tensor, onehot[:, n, :, :],
                               iota.unsqueeze(1).to_broadcast([P, E, CAP]),
                               posT[:, n, b * E:(b + 1) * E].unsqueeze(2).to_broadcast([P, E, CAP]), ALU.is_equal)
            for q in range(2):
                k = 2 * (b % 2) + q
                for n in range(NT):
                    tk = mm([oh_ready, bank_free[k]], psum[:, k, :], xn[:, b * NT + n, :],
                            onehot[:, n, 4 * q:4 * q + 4, :], start=(n == 0), stop=(n == NT - 1))
                xin_dst = xin[:, 4 * q:4 * q + 4, b, :]
                xin_src = psum[:, k, :].rearrange("p (x c) -> p x c", x=4)
                scale, shift = mod[:, 0, SC_B, b:b + 1], mod[:, 0, SH_B, b:b + 1]
                if q:
                    te = dve([tk], tensor_scalar, xin_dst, xin_src, scale, shift, ALU.mult, ALU.add)
                else:
                    te = act([tk], activation, xin_dst, xin_src, ACT.Identity, scale=scale, bias=shift)
                bank_free[k] = [te]
                xin_ready.append(te)
            kg = 4 + b % 2
            for x in range(E):
                for n in range(NT):
                    tk = mm([oh_ready, bank_free[kg]], psum[:, kg, x:x + 1], onehot[:, n, x, :],
                            prob_tok[:, n, b, x:x + 1], start=(x == 0 and n == 0), stop=(n == NT - 1))
            oh_free = [tk]
            tg = dve([tk], tensor_copy, slot_gate[:, b, :], psum[:, kg, 0:E])
            bank_free[kg] = [tg]

        hid_free = [[], []]
        rnd = 0
        y_ready = []
        for x in range(E):
            for hb in range(2):
                z = rnd % 2
                rnd += 1
                th = []
                for c in range(FC):
                    k = c
                    tk = mm([g_ff0, xin_ready, bank_free[k]], psum[:, k, :], w1[:, x, c * P:(c + 1) * P],
                            xin[:, x, 4 * hb:4 * hb + 4, :], start=True)
                    ta = act([tk, hid_free[z], select_done], activation, 
                        hid[:, z, c, :], psum[:, k, :], ACT.Gelu)
                    bank_free[k] = [ta]
                    th.append(ta)
                up_done = tk
                ky = 4 + z
                for s in range(4):
                    for c in range(FC):
                        tk = mm([th[c], bank_free[ky]], psum[:, ky, s * P:(s + 1) * P],
                                hid[:, z, c, s * CAP:(s + 1) * CAP], w2[:, x, c, :],
                                start=(s == 0 and c == 0), stop=(c == FC - 1))
                hid_free[z] = [tk]
                ty = dve([tk, up_done, tg], tensor_tensor, 
                    xin[:, x, 4 * hb:4 * hb + 4, :], psum[:, ky, :].rearrange("p (s d) -> p s d", s=4),
                    slot_gate[:, 4 * hb:4 * hb + 4, x].unsqueeze(2).to_broadcast([P, 4, D]), ALU.mult)
                bank_free[ky] = [ty]
                y_ready = [ty]

        back_free = [[], []]
        for b in range(B):
            ko = 4 + b % 2
            for x in range(E):
                r = b * E + x
                z = r % 2
                kb = r % 4
                tk = mm([t10, bank_free[kb]], psum[:, kb, :],
                        ident_bf[R, r:r + 1].to_broadcast([NBE, P]), pos_bf[R, :], start=True)
                tb = dve([tk, back_free[z], g_iota], tensor_scalar, 
                    back[:, z, :], psum[:, kb, :], iota_col[:, 0:1], None, ALU.is_equal)
                bank_free[kb] = [tb]
                tk = mm([tb, y_ready, bank_free[ko]], psum[:, ko, :], xin[:, x, b, :], back[:, z, :],
                        start=(x == 0), stop=(x == E - 1))
                back_free[z] = [tk]
            cols = slice(b * S, (b + 1) * S)
            tx = dve([tk], scalar_tensor_tensor, 
                xT[:, cols], psum[:, ko, :], mod[:, 0, GA_B, b:b + 1], xT[:, cols], ALU.mult, ALU.add)
            bank_free[ko] = [tx]
            x_ready[b] = [tx]
        barrier()

        k_head = carve([H1, S], restart=True)
        v_head = carve([NT, H1, P])
        qx = carve([2, GRP, S])
        q1T = carve([S])
        k1T = carve([S])
        ctx1T = carve([S])
        gm = carve([GRP, P])
        fold = carve([8, P])
        spread = carve([H1, P])
        rope1 = carve([2, S])
        wq1, wq1_rot, wk1, wk1_rot, wv1, wo1 = (carve([D]) for _ in range(6))
        band = carve([BAND_W])
        band_T = carve([NCH + 2, P])
        chunk_mask = carve([P])
        head_rows = carve([H1])
        rel0_col = carve([1])
        rel0_row = carve([HD1])
        xn1 = carve([NT, D])
        for dst, src in ((wq1, "w_qT"), (wk1, "w_kT"), (wv1, "w_vT"), (wo1, "w_oT"), (fold, "fold"), (spread, "spread"),
                         (rope1, "rope1"), (band, "band"), (chunk_mask, "chunk_mask"),
                         (head_rows, "head_rows")):
            prog.dma(g_w1, dst, t[src])
        prog.dma(g_w1, rel0_row, t["rel_emb"][0:1, :].partition_broadcast(P))
        prog.dma(g_ff1, w1, t["L1_W1"].rearrange("e d f -> d e f"))
        prog.dma(g_ff1, w2, t["L1_W2"].rearrange("e (c p) d -> p e c d", p=P))
        w1_ready = [g_w1] + rotate(wq1_rot, wq1, [g_w1]) + rotate(wk1_rot, wk1, [])
        t_r0 = dve([g_w1], tensor_copy, rel0_col, band[:, 0:1])
        t_band = dve([t_r0], tensor_scalar, band, band, rel0_col[:, 0:1], None, ALU.subtract)
        for c in range(NCH + 2):
            e0 = BAND_E0 - CH * c if c < NCH else BAND_E0 - P - CH * (c - NCH)
            k = c // 4
            tk = pe([t_band], transpose, 
                psum[:, k, (c % 4) * P:(c % 4 + 1) * P], band[:, e0:e0 + P], ident[:, :])
        for k, n in ((0, 4), (1, 4), (2, NCH + 2 - 8)):
            t_bt = dve([tk], tensor_copy, 
                band_T[:, 4 * k:4 * k + n, :], psum[:, k, 0:n * P].rearrange("p (c q) -> p c q", c=n))
            bank_free[k] = [t_bt]
        t_vz = pool([], memset, v_head.rearrange("p a b c -> p (a b c)"), 0.0)

        def head_cols(n, first):
            a = v_head[:, n, 0, first:first + HD1]
            return bass.AP(a.tensor, a.offset, [list(a.ap[0]), [8 * P, 2], [P + HD1, 8], [1, HD1]])

        t_v1 = [pool([t_vz], memset, head_cols(n, 64), 1.0) for n in range(NT)]

        def band_slice(c):
            e0 = BAND_E0 - CH * c if c < NCH else BAND_E0 - P - CH * (c - NCH)
            return band[:, e0:e0 + P]

        def cols4(a, c):
            return a.rearrange("p (h q) -> p h q", h=GRP)[:, :, c * CH:(c + 1) * CH]

        prob_free = [[], []]
        attn1_done, ctx_free, rope_free = [], [], [[], []]
        qx_free = [[], []]
        gm_free = []
        xn1_free = []
        for b in range(B):
            i, h_ready, _, xn1_free = layer_norm(b, 1, SC_A, SH_A, xn1, xn1_free)
            h_in = hT[:, i, :]
            made = []
            for z, (w, w_rot, dst) in enumerate(((wk1, wk1_rot, k1T), (wq1, wq1_rot, q1T))):
                ka, kb = 2 * z, 2 * z + 1
                ta = mm([h_ready, w1_ready, bank_free[ka]], psum[:, ka, :], w, h_in, True)
                tb = mm([bank_free[kb]], psum[:, kb, :], w_rot, h_in, True)
                ma = dve([ta, rope_free[z]], tensor_tensor, 
                    rope_a[:, z, :], psum[:, ka, :], rope1[:, 0, :], ALU.mult)
                mb = dve([tb], tensor_tensor, 
                    rope_b[:, z, :], psum[:, kb, :], rope1[:, 1, :], ALU.mult)
                bank_free[ka], bank_free[kb] = [ma], [mb]
                tq = pool([ma, mb, attn1_done], tensor_tensor, 
                    dst, rope_a[:, z, :], rope_b[:, z, :], ALU.add)
                rope_free[z] = [tq]
                made.append(tq)
            k1_ready, q1_ready = made
            kh_ready = []
            for h in range(H1):
                eng = dve if h % 2 == 0 else pool
                kh_ready.append(eng([k1_ready, t_r0, attn1_done], tensor_scalar, 
                    k_head[:, h, :], k1T, rel0_col[:, 0:1], head_rows[:, h:h + 1], ALU.add, ALU.mult))
            for n in range(NT):
                tk = mm([h_ready, bank_free[4]], psum[:, 4, n * P:(n + 1) * P], h_in[:, n * P:(n + 1) * P], wv1,
                        start=(n == 0))
            hT_free[i] = [tk]
            for n in range(NT):
                v1_ready = dve([tk, t_v1, attn1_done], tensor_tensor, 
                    head_cols(n, 0), psum[:, 4, n * P:(n + 1) * P].rearrange("p (a h d) -> p a h d", a=2, h=8),
                    rel0_row.unsqueeze(1).unsqueeze(1).to_broadcast([P, 2, 8, HD1]), ALU.add)
            bank_free[4] = [v1_ready]

            qx_ready = {}

            def expand(h):
                z = (h // GRP) % 2
                tk = mm([q1_ready, bank_free[AUX]], psum[:, AUX, :],
                        spread[:, h, :], q1T, True)
                qx_ready[h] = dve([tk, qx_free[z]], tensor_tensor, 
                    qx[:, z, h % GRP, :].rearrange("p (i q) -> p i q", i=NT),
                    psum[:, AUX, :].rearrange("p (i q) -> p i q", i=NT),
                    chunk_mask.unsqueeze(1).to_broadcast([P, NT, P]), ALU.mult)
                bank_free[AUX] = [qx_ready[h]]

            for h in range(GRP):
                expand(h)

            def scores1(u):
                g, i, k0 = u["g"], u["i"], u["k0"]
                z = g % 2
                for j in range(i + 1):
                    for h in range(GRP):
                        mm([kh_ready[GRP * g + h], q1_ready, bank_free[k0 + j]],
                           psum[:, k0 + j, h * P:(h + 1) * P], k_head[:, GRP * g + h, j * P:(j + 1) * P],
                           q1T[:, i * P:(i + 1) * P], start=(h == 0))
                mm([consts_ready], psum[:, k0 + i, :], ident_bf[:, :],
                   causal[:, :].unsqueeze(1).to_broadcast([P, GRP, P]), False)
                for c in list(range(NCH)) + ([NCH, NCH + 1] if i else []):
                    k, cc = (k0 + i, c) if c < NCH else (k0 + i - 1, c - NCH)
                    tk = mm([[qx_ready[GRP * g + h] for h in range(GRP)], t_band], cols4(psum[:, k, :], cc),
                            band_slice(c), qx[:, z, :, i * P + cc * CH:i * P + (cc + 1) * CH], False)
                if i == 0:
                    qx_free[z] = [tk]
                if g + 1 < H1 // GRP:
                    n = [3, 1, 2, 0].index(i)
                    expand(GRP * (g + 1) + n)
                return tk

            def values1(u):
                g, i, z = u["g"], u["i"], u["n"] % 2
                pz = prob[:, z, :]
                for c in range(NCH):
                    t_g = mm([u["prob"], t_bt, bank_free[AUX]], cols4(psum[:, AUX, :], c), band_T[:, c, :],
                             cols4(pz[:, i * BANK:(i + 1) * BANK], c), start=(c == 0))
                if i:
                    for c in range(2):
                        t_g = mm([], cols4(psum[:, AUX, :], c), band_T[:, NCH + c, :],
                                 cols4(pz[:, (i - 1) * BANK:i * BANK], c), False)
                t_gm = dve([t_g, gm_free], tensor_tensor, 
                    gm, psum[:, AUX, :].rearrange("p (h q) -> p h q", h=GRP),
                    chunk_mask.unsqueeze(1).to_broadcast([P, GRP, P]), ALU.mult)
                bank_free[AUX] = [t_gm]
                first = g % 2 == 0 and i == ORDER[0][0]
                for j in range(i + 1):
                    for h in range(GRP):
                        tk = mm([v1_ready, bank_free[CTX]], psum[:, CTX, i * P:(i + 1) * P],
                                v_head[:, j, GRP * g + h, :], pz[:, j * BANK + h * P:j * BANK + (h + 1) * P],
                                start=(first and j == 0 and h == 0))
                for h in range(GRP):
                    t_f = mm([t_gm], psum[:, CTX, i * P:(i + 1) * P], fold[:, GRP * (g % 2) + h, :], gm[:, h, :], False)
                gm_free[:] = [t_f]
                if g % 2 == 1 and i == ORDER[-1][0]:
                    half = g // 2
                    tr = dve([t_f], reciprocal, recip[:, :], psum[64:128, CTX, :])
                    tm = dve([tr, ctx_free], tensor_tensor, 
                        ctx1T[64 * half:64 * half + 64, :], psum[0:64, CTX, :], recip[:, :], ALU.mult)
                    bank_free[CTX] = [tm]
                return tk

            attention(HD1 ** -0.5, H1 // GRP, scores1, values1, prob_free)
            attn1_done = [prog.last["tensor"]]
            ctx_ready = [prog.last["vector"]]
            tk = mm([ctx_ready, bank_free[0]], psum[:, 0, :], wo1, ctx1T, True)
            ctx_free = [tk]
            cols = slice(b * S, (b + 1) * S)
            tx = dve([tk], scalar_tensor_tensor, 
                xT[:, cols], psum[:, 0, :], mod[:, 1, GA_A, b:b + 1], xT[:, cols], ALU.mult, ALU.add)
            bank_free[0] = [tx]
            x_ready[b] = [tx]
        barrier()

        hid = carve([2, FC, S], restart=True)
        acc = carve([2, NT, D])
        wr = carve([E])
        br_row = carve([E])
        b1 = carve([E, FC])
        b2 = carve([D])
        keep = carve([NT * E])
        sc = carve([NT, E])
        gt, eq, cum, ex = (carve([NT, E]) for _ in range(4))
        top = carve([NT, 8])
        ngt = carve([NT])
        rw = carve([2, NT, E])
        rwT = carve([2, S])
        xn1 = carve([NT, D])
        out_tok = carve([2, NT, D])
        g_w2 = prog.dma_group("d_w2")
        for dst, src in ((wr, t["Wr"]), (keep, t["keep"]), (b1, t["b1"]),
                         (b2[0:E, :], t["b2"])):
            prog.dma(g_w2, dst, src)
        prog.dma(g_w2, br_row, t["br"].rearrange("(a e) -> a e", a=1).partition_broadcast(P))
        hid_free, acc_free, rwT_free, out_free = [[], []], [[], []], [[], []], [None, None]
        xn1_free, rnd, stores = [], 0, []
        out_v = out.rearrange("b (n p) d -> p (b n) d", p=P)
        for b in range(B):
            zb = b % 2
            i, h_ready, _, xn1_free = layer_norm(b, 1, SC_B, SH_B, xn1, xn1_free, banks=(6, 7))
            h_in = hT[:, i, :]
            for n in range(NT):
                tk = mm([h_ready, g_w2, bank_free[6]], psum[:, 6, n * E:(n + 1) * E], h_in[:, n * P:(n + 1) * P],
                        wr, start=(n == 0))
            t1 = dve([tk], tensor_tensor, 
                sc, psum[:, 6, 0:NT * E].rearrange("p (n e) -> p n e", n=NT),
                br_row.unsqueeze(1).to_broadcast([P, NT, E]), ALU.add)
            bank_free[6] = [t1]
            for n in range(NT):
                t2 = dve([t1], max8, top[:, n, :], sc[:, n, :])
            second = top[:, :, 1:2].to_broadcast([P, NT, E])
            ta = dve([t2], tensor_tensor, gt, sc, second, ALU.is_gt)
            tb = dve([t2], tensor_tensor, eq, sc, second, ALU.is_equal)
            t3 = dve([ta], tensor_reduce, ngt, gt, AX.X, ALU.add)
            t4 = dve([tb], tensor_tensor_scan, 
                cum.rearrange("p n e -> p (n e)"), keep, eq.rearrange("p n e -> p (n e)"), 0.0, ALU.mult, ALU.add)
            t4 = dve([t3, t4], tensor_tensor, cum, cum, ngt.unsqueeze(2).to_broadcast([P, NT, E]), ALU.add)
            t4 = dve([t4], tensor_scalar, cum, cum, 2.0, None, ALU.is_le)
            t4 = dve([t4], tensor_tensor, eq, eq, cum, ALU.mult)
            t4 = dve([t4], tensor_tensor, gt, gt, eq, ALU.add)
            t5 = dve([t2], tensor_tensor, ex, sc, top[:, :, 0:1].to_broadcast([P, NT, E]), ALU.subtract)
            t5 = act([t5], activation, ex, ex, ACT.Exp)
            t5 = dve([t5, t4], tensor_tensor, ex, ex, gt, ALU.mult)
            t6 = dve([t5], tensor_reduce, ngt, ex, AX.X, ALU.add)
            t6 = dve([t6], reciprocal, ngt, ngt)
            t_rw = dve([t6], tensor_tensor, 
                rw[:, zb, :, :], ex, ngt.unsqueeze(2).to_broadcast([P, NT, E]), ALU.mult)
            for n in range(NT):
                tk = pe([t_rw, bank_free[6]], transpose, 
                    psum[0:E, 6, n * P:(n + 1) * P], rw[:, zb, n, :], ident[:, :])
            t_rwT = dve([tk, rwT_free[zb]], tensor_copy, rwT[0:E, zb, :], psum[0:E, 6, :])
            bank_free[6] = [t_rwT]
            for n in range(NT):
                tk = mm([t_rwT, bank_free[6]], psum[:, 6, n * P:(n + 1) * P], rwT[0:E, zb, n * P:(n + 1) * P],
                        b2[0:E, :], start=(n == 0))
            rwT_free[zb] = [tk]
            t_acc = [act([tk, acc_free[zb]], copy, 
                acc[:, zb, :, :], psum[:, 6, :].rearrange("p (n d) -> p n d", n=NT))] * NT
            bank_free[6] = [t_acc[0]]
            for x in range(E):
                z = rnd % 2
                rnd += 1
                th = []
                for c in range(FC):
                    tk = mm([g_ff1, bank_free[c]], psum[:, c, :], w1[:, x, c * P:(c + 1) * P], h_in, True)
                    ta = act([tk, hid_free[z], g_w2], activation, 
                        hid[:, z, c, :], psum[:, c, :], ACT.Gelu_apprx_tanh, bias=b1[:, x, c:c + 1])
                    bank_free[c] = [ta]
                    th.append(ta)
                if x == E - 1:
                    hT_free[i] = [tk]
                ky = 4 + z
                for n in range(NT):
                    for c in range(FC):
                        tk = mm([th[c], bank_free[ky]], psum[:, ky, n * P:(n + 1) * P],
                                hid[:, z, c, n * P:(n + 1) * P], w2[:, x, c, :],
                                start=(n == 0 and c == 0), stop=(c == FC - 1))
                hid_free[z] = [tk]
                t_new = []
                for n in range(NT):
                    t_new.append(dve([tk, t_acc[n]], scalar_tensor_tensor, 
                        acc[:, zb, n, :], psum[:, ky, n * P:(n + 1) * P], rw[:, zb, n, x:x + 1], acc[:, zb, n, :],
                        ALU.mult, ALU.add))
                t_acc = t_new
                bank_free[ky] = [t_acc[-1]]
            for n in range(NT):
                tk = pe([t_acc, bank_free[6]], transpose, 
                    psum[:, 6, n * P:(n + 1) * P], acc[:, zb, n, :], ident[:, :])
            acc_free[zb] = [tk]
            cols = slice(b * S, (b + 1) * S)
            tx = dve([tk], scalar_tensor_tensor, 
                xT[:, cols], psum[:, 6, :], mod[:, 1, GA_B, b:b + 1], xT[:, cols], ALU.mult, ALU.add)
            bank_free[6] = [tx]
            for n in range(NT):
                tk = pe([tx, bank_free[7]], transpose, 
                    psum[:, 7, n * P:(n + 1) * P], xT[:, b * S + n * P:b * S + (n + 1) * P], ident[:, :])
            to = act([tk, out_free[zb]], copy, 
                out_tok[:, zb, :, :], psum[:, 7, :].rearrange("p (n d) -> p n d", n=NT))
            bank_free[7] = [to]
            g_o = prog.dma_group(f"d_out{b}")
            prog.dma(g_o, out_v[:, b * NT:(b + 1) * NT, :], out_tok[:, zb, :, :], wait=[to])
            out_free[zb] = g_o
            stores.append(g_o)
        prog.wait_only("sync", stores)

        prog.run(ctx.enter_context(nc.Block()))


def kernel(**inputs):
    import concourse.bacc as bacc
    from concourse.bass_utils import run_bass_kernel_spmd

    a = {k: np.ascontiguousarray(v) for k, v in inputs.items()}
    arrays = {
        "x": a["L0_attn_hidden_states"], "Wq": a["L0_attn_Wq"], "Wk": a["L0_attn_Wk"], "Wv": a["L0_attn_Wv"],
        "Wo": a["L0_attn_Wo"], "gateT": a["L0_ffn_gate_w"].T, "L0_w1": a["L0_ffn_w1"], "L0_w2": a["L0_ffn_w2"],
        "L0_cT": a["L0_c"].T, "L0_wmod": a["L0_wmod"], "L1_cT": a["L1_c"].T, "L1_wmod": a["L1_wmod"],
        "w_qT": a["L1_attn_w_q"].T, "w_kT": a["L1_attn_w_k"].T, "w_vT": a["L1_attn_w_v"].T,
        "w_oT": a["L1_attn_w_o"].T, "rel_emb": a["L1_attn_rel_emb"],
        "band": a["L1_attn_rel_emb"][band_index()].transpose(0, 2, 1).reshape(P, BAND_W),
        "L1_W1": a["L1_ffn_W1"], "b1": a["L1_ffn_b1"].reshape(E, FC, P).transpose(2, 0, 1), "L1_W2": a["L1_ffn_W2"], "b2": a["L1_ffn_b2"],
        "Wr": a["L1_ffn_Wr"], "br": a["L1_ffn_br"],
    }
    arrays.update(shape_constants())
    nc = bacc.Bacc("TRN2", target_bir_lowering=False, num_devices=1)
    feed, t = {}, {}
    for name, v in arrays.items():
        v = np.ascontiguousarray(v)
        feed[f"in_{name}"] = v
        t[name] = nc.dram_tensor(f"in_{name}", v.shape, mybir.dt.from_np(v.dtype), kind="ExternalInput").ap()
    out = nc.dram_tensor("out", (B, S, D), F32, kind="ExternalOutput").ap()
    build(nc, t, out)
    r = run_bass_kernel_spmd(nc, [feed], core_ids=[0])
    return r.results[0]["out"]
```

```python
from contextlib import ExitStack

import concourse.bass as bass
import numpy as np
from concourse import mybir

F32 = mybir.dt.float32
BF16 = mybir.dt.bfloat16
ALU = mybir.AluOpType
ACT = mybir.ActivationFunctionType
AX = mybir.AxisListType

P = 128
B, S, D = 8, 512, 128
NT = S // P
BANK = 512
H0, KV0, HD0 = 16, 4, 64
PAIRS = H0 // 2
H1, HD1 = 16, 8
RMAX = 32
NREL = RMAX + 1
CH = 16
NCH = P // CH
GRP = 4
E, F = 8, 512
FC = F // P
CAP = 2 * S // E
EPS = 1e-5
NEG = -1e30
BAND_E0 = P + CH
BAND_W = BAND_E0 + P

ARENA = 28384

ENGINES = ("tensor", "vector", "scalar", "gpsimd", "sync")


class Token:

    def __init__(self, owner):
        self.owner, self.used, self.value = owner, False, None


class DmaGroup:

    def __init__(self, sem):
        self.sem, self.count = sem, 0
        self.used = True

    @property
    def value(self):
        return 16 * self.count

    def so_far(self):
        now = Token(self)
        now.sem, now.value, now.used = self.sem, 16 * self.count, True
        return now


class Program:

    def __init__(self, nc, ctx):
        self.nc, self.ctx = nc, ctx
        self.queue = {e: [] for e in ENGINES}
        self.sem = {e: ctx.enter_context(nc.semaphore(f"{e}_progress")) for e in ENGINES}
        self.last = {}

    def op(self, engine, wait, emit, *args, **kw):
        token = Token(engine)
        waits = [w for w in flat(wait) if w is not None]
        for w in waits:
            w.used = True
        self.queue[engine].append((waits, lambda e: emit(e, *args, **kw), token))
        self.last[engine] = token
        return token

    def pe(self, wait, emit, *args, **kw):
        return self.op("tensor", wait, emit, *args, **kw)

    def dve(self, wait, emit, *args, **kw):
        return self.op("vector", wait, emit, *args, **kw)

    def act(self, wait, emit, *args, **kw):
        return self.op("scalar", wait, emit, *args, **kw)

    def pool(self, wait, emit, *args, **kw):
        return self.op("gpsimd", [wait, self.last.get("gpsimd")], emit, *args, **kw)

    def dma_group(self, name):
        return DmaGroup(self.ctx.enter_context(self.nc.semaphore(name)))

    def dma(self, group, out, src, wait=(), engine="sync"):
        waits = [w for w in flat(wait) if w is not None]
        for w in waits:
            w.used = True
        group.count += 1
        self.queue[engine].append((waits, lambda e: e.dma_start(out, src).then_inc(group.sem, 16), None))

    def wait_only(self, engine, wait):
        waits = [w for w in flat(wait) if w is not None]
        for w in waits:
            w.used = True
        self.queue[engine].append((waits, None, None))

    def run(self, block):
        for e in ENGINES:
            n = 0
            for _, _, token in self.queue[e]:
                if token is not None and token.used:
                    n += 1
                    token.value = n
        for e in ENGINES:
            getter = {"tensor": block.tensor, "vector": block.vector, "scalar": block.scalar,
                      "gpsimd": block.gpsimd, "sync": block.sync}[e]

            def body(eng, items=self.queue[e], own=self.sem[e]):
                passed = {}
                for waits, emit, token in items:
                    need = {}
                    for w in waits:
                        group = w if isinstance(w, DmaGroup) else w.owner
                        s = group.sem if isinstance(group, DmaGroup) else self.sem[group]
                        k = id(group) if isinstance(group, DmaGroup) else group
                        if w.value > max(passed.get(k, 0), need.get(k, (None, 0))[1]):
                            need[k] = (s, w.value)
                    for k, (s, v) in need.items():
                        eng.wait_ge(s, v)
                        passed[k] = v
                    if emit is None:
                        continue
                    ins = emit(eng)
                    if token is not None and token.used:
                        ins.then_inc(own, 1)

            getter(body)


def activation(eng, *args, **kw):
    return eng.activation(*args, **kw)


def bn_aggr(eng, *args, **kw):
    return eng.bn_aggr(*args, **kw)


def bn_stats(eng, *args, **kw):
    return eng.bn_stats(*args, **kw)


def copy(eng, *args, **kw):
    return eng.copy(*args, **kw)


def match_replace(eng, *args, **kw):
    return eng.match_replace(*args, **kw)


def matmul(eng, *args, **kw):
    return eng.matmul(*args, **kw)


def max8(eng, *args, **kw):
    return eng.max(*args, **kw)


def memset(eng, *args, **kw):
    return eng.memset(*args, **kw)


def reciprocal(eng, *args, **kw):
    return eng.reciprocal(*args, **kw)


def scalar_tensor_tensor(eng, *args, **kw):
    return eng.scalar_tensor_tensor(*args, **kw)


def stream_shuffle(eng, *args, **kw):
    return eng.stream_shuffle(*args, **kw)


def tensor_copy(eng, *args, **kw):
    return eng.tensor_copy(*args, **kw)


def tensor_reduce(eng, *args, **kw):
    return eng.tensor_reduce(*args, **kw)


def tensor_scalar(eng, *args, **kw):
    return eng.tensor_scalar(*args, **kw)


def tensor_tensor(eng, *args, **kw):
    return eng.tensor_tensor(*args, **kw)


def tensor_tensor_scan(eng, *args, **kw):
    return eng.tensor_tensor_scan(*args, **kw)


def transpose(eng, *args, **kw):
    return eng.transpose(*args, **kw)


def flat(x):
    if isinstance(x, (list, tuple)):
        return [z for y in x for z in flat(y)]
    return [x]


def rope_tables(seq, dim, pick_even):
    inv = 1.0 / np.float32(10000.0) ** (np.arange(0, dim, 2, dtype=np.float32) / np.float32(dim))
    ang = np.arange(seq, dtype=np.float32)[:, None] * inv.astype(np.float32)[None, :]
    cos, sin = np.cos(ang), np.sin(ang)
    if pick_even:
        cos = np.concatenate([cos, cos], -1)[:, 0::2]
        sin = np.concatenate([sin, sin], -1)[:, 0::2]
    sign = np.where(np.arange(dim) % 2 == 0, 1.0, -1.0)[:, None]
    return np.repeat(cos.T, 2, 0).astype(np.float32), (sign * np.repeat(sin.T, 2, 0)).astype(np.float32)


SWAP = [p ^ 1 for p in range(32)]


def shape_constants():
    c0, s0 = rope_tables(S, HD0, True)
    c1, s1 = rope_tables(S, HD1, False)
    p = np.arange(P)
    out = {
        "rope0": np.stack([np.tile(c0, (P // HD0, 1)), np.tile(s0, (P // HD0, 1))], 1),
        "rope1": np.stack([np.tile(c1, (P // HD1, 1)), np.tile(s1, (P // HD1, 1))], 1),
        "ident": np.eye(P, dtype=np.float32),
        "causal": np.where(p[:, None] <= p[None, :], 0.0, NEG).astype(np.float32),
        "chunk_mask": (p[None, :] % CH == p[:, None] // HD1).astype(np.float32),
        "iota": np.tile(np.arange(P, dtype=np.float32), (P, 1)),
        "iota_col": p[:, None].astype(np.float32),
    }
    fold = np.zeros((P, 8, P), np.float32)
    for h in range(8):
        for i in range(CH):
            for d in range(HD1):
                fold[i * HD1 + d, h, h * HD1 + d] = 1.0
    out["fold"] = fold
    r = p % 64
    out["spread"] = (np.isin(r // HD1, (0, 1, 4))[:, None] &
                     (r[:, None] % HD1 == p[None, :] % HD1)).astype(np.float32)
    keep = np.ones((P, NT * E), np.float32)
    keep[:, 0::E] = 0.0
    out["keep"] = keep
    return out


def band_index():
    i = np.arange(CH)[:, None]
    e = np.arange(BAND_W)[None, :] - BAND_E0
    return np.clip(e - i, -RMAX, 0) + RMAX


def build(nc, t, out):
    ctx = ExitStack()
    with ctx:
        prog = Program(nc, ctx)
        pe, dve, act, pool = prog.pe, prog.dve, prog.act, prog.pool

        def sb(name, shape, dt=F32):
            return ctx.enter_context(nc.sbuf_tensor(name, shape, dt))

        psum = ctx.enter_context(nc.psum_tensor("psum", [P, 8, BANK], F32))
        xT = sb("xT", [P, B * S])
        ffw = sb("ffw", [P, 2 * E * F])
        w1 = ffw[:, 0:E * F].rearrange("p (e f) -> p e f", e=E)
        w2 = ffw[:, E * F:2 * E * F].rearrange("p (e c d) -> p e c d", e=E, c=FC)
        arena = sb("arena", [P, ARENA])
        ident = sb("ident", [P, P])
        ident_bf = sb("ident_bf", [P, P], BF16)
        neg_ident = sb("neg_ident", [P, P], BF16)
        ones_bf = sb("ones_bf", [P, P], BF16)
        causal_f = sb("causal_f", [P, P])
        causal = sb("causal", [P, P], BF16)
        modc = sb("modc", [P, 2, B])
        mod_e = sb("mod_e", [P, 2, B])
        mod = sb("mod", [P, 2, 6, B])
        modg = sb("modg", [P, 2, 2, 2, B])
        prob = sb("prob", [P, 2, 4 * BANK])
        colmax = sb("colmax", [P, 2, BANK])
        rowmax = sb("rowmax", [P, 2, GRP])
        negmax = sb("negmax", [P, 2, GRP, P], BF16)
        hT = sb("hT", [P, 2, S])
        rope_a = sb("rope_a", [P, 2, S])
        rope_b = sb("rope_b", [P, 2, S])
        raw = sb("raw", [P, 2, S])
        ctx_sum = sb("ctx_sum", [P, 2, 2, BANK])
        stats = sb("stats", [P, NT, 6])
        moments = sb("moments", [P, NT, 2])
        rstd = sb("rstd", [P, NT])
        minus_half = sb("minus_half", [P, NT])

        class Arena:
            at = 0

        def carve(shape, restart=False):
            if restart:
                Arena.at = 0
            n = int(np.prod(shape))
            a = arena[:, Arena.at:Arena.at + n]
            Arena.at += n
            assert Arena.at <= ARENA, Arena.at
            names = "abcd"[:len(shape)]
            if len(shape) == 1:
                return a
            return a.rearrange(f"p ({' '.join(names)}) -> p {' '.join(names)}",
                               **{k: v for k, v in zip(names, shape)})

        bank_free = [[] for _ in range(8)]

        def mm(wait, o, lhsT, rhs, start, stop=True):
            return pe(wait, matmul, o, lhsT, rhs, start=start, stop=stop,
                                               skip_group_check=True)

        def barrier():
            ends = [prog.last[e] for e in ENGINES if e in prog.last]
            for e in ENGINES:
                prog.wait_only(e, ends)

        g_const, g_x, g_w0, g_ff0 = (prog.dma_group(n) for n in ("d_const", "d_x", "d_w0", "d_ff0"))
        g_w1, g_ff1 = (prog.dma_group(n) for n in ("d_w1", "d_ff1"))

        xn = carve([B * NT, D], restart=True)
        wq = carve([D * H0 * HD0 // P])
        wk = carve([KV0 * P])
        wv = carve([KV0 * HD0])
        wo = carve([PAIRS, D])
        gate = carve([E])
        rope0 = carve([2, S])
        prob_tok = carve([NT, B, E])
        gmax = carve([NT])
        gsum = carve([NT])
        gexp = carve([NT, E])
        kq = ffw[:, :]
        qT = [carve([PAIRS, S]), kq[:, 0:PAIRS * S].rearrange("p (a s) -> p a s", a=PAIRS)]
        kq = kq[:, PAIRS * S:].rearrange("p (c a s) -> p c a s", c=2, a=KV0)
        k_even = [carve([KV0, S]), kq[:, 0, :, :]]
        k_odd = [carve([KV0, S]), kq[:, 1, :, :]]
        v_ones = [carve([NT, KV0, P]) for _ in range(2)]
        ctxT = carve([PAIRS, S])
        wmod = ctxT.rearrange("p a s -> p (a s)")[:, 0:12 * D].rearrange("p (a s) -> p a s", a=2)

        prog.dma(g_const, ident[:, :], t["ident"])
        prog.dma(g_const, causal_f[:, :], t["causal"])
        prog.dma(g_const, modc[:, 0, :], t["L0_cT"])
        prog.dma(g_const, modc[:, 1, :], t["L1_cT"])
        prog.dma(g_const, wmod[:, 0, :], t["L0_wmod"])
        prog.dma(g_const, wmod[:, 1, :], t["L1_wmod"])
        prog.dma(g_const, rope0, t["rope0"])
        x_tok = t["x"].rearrange("b (n p) d -> p (b n) d", p=P)
        for h in range(2):
            n = B * NT // 2
            prog.dma(g_x, xn[:, h * n:(h + 1) * n, :], x_tok[:, h * n:(h + 1) * n, :])
        prog.dma(g_w0, wq, t["Wq"])
        for c in range(2):
            prog.dma(g_w0, wk.rearrange("p (k c d) -> p k c d", k=KV0, c=2)[:, :, c, :],
                     t["Wk"].rearrange("p (k d) -> p k d", k=KV0))
        prog.dma(g_w0, wv, t["Wv"])
        wo_src = t["Wo"].rearrange("(m half a c p) d -> m half p c a d", m=KV0 // 2, half=2, a=2, c=2)
        for m in range(KV0 // 2):
            for half in range(2):
                for c in range(2):
                    prog.dma(g_w0, wo[half * HD0:(half + 1) * HD0, 4 * m + 2 * c:4 * m + 2 * c + 2, :],
                             wo_src[m, half, :, c])
        prog.dma(g_w0, gate, t["gateT"])

        t_ones = dve([], memset, ones_bf[:, :], 1.0)
        t_ident = dve([g_const], tensor_copy, ident_bf[:, :], ident[:, :])
        t_nid = dve([], tensor_scalar, neg_ident[:, :], ident[:, :], -1.0, None, ALU.mult)
        t_causal = dve([], tensor_copy, causal[:, :], causal_f[:, :])
        consts_ready = [t_ones, t_ident, t_nid, t_causal]

        t_e = act([g_const], activation, mod_e[:, :, :], modc[:, :, :], ACT.Exp, scale=-1.0)
        t_e = dve([t_e], tensor_scalar, mod_e[:, :, :], mod_e[:, :, :], 1.0, None, ALU.add)
        t_e = dve([t_e], reciprocal, mod_e[:, :, :], mod_e[:, :, :])
        t_silu = dve([t_e], tensor_tensor, modc[:, :, :], modc[:, :, :], mod_e[:, :, :], ALU.mult)
        for L in range(2):
            for j in range(6):
                t_mod = mm([t_silu, g_const], psum[:, 7, (L * 6 + j) * B:(L * 6 + j + 1) * B],
                           wmod[:, L, j * D:(j + 1) * D], modc[:, L, :], start=(L + j == 0))
        t_mod = dve([t_mod], tensor_copy, 
            mod[:, :, :, :].rearrange("p a b c -> p (a b c)"), psum[:, 7, 0:12 * B])
        bank_free[7] = [t_mod]
        SH_A, SC_A, GA_A, SH_B, SC_B, GA_B = range(6)
        t_sc = [dve([t_mod], tensor_scalar, mod[:, :, j, :], mod[:, :, j, :], 1.0, None, ALU.add)
                for j in (SC_A, SC_B)]
        for n, j in enumerate((GA_A, GA_B)):
            g, sgn, mag = mod[:, :, j, :], modg[:, :, n, 0, :], modg[:, :, n, 1, :]
            t1 = dve([t_mod], tensor_scalar, sgn, g, 0.0, 2.0, ALU.is_ge, ALU.mult)
            t2 = dve([t1], tensor_scalar, sgn, sgn, -1.0, None, ALU.add)
            t3 = dve([t_mod], tensor_scalar, mag, g, -1.0, None, ALU.mult)
            t3 = dve([t3], tensor_tensor, mag, mag, g, ALU.max)
            t3 = dve([t3], tensor_scalar, mag, mag, 0.25, None, ALU.max)
            t_g = dve([t2, t3], tensor_tensor, g, sgn, mag, ALU.mult)
            t_sc.append(t_g)
        mod_ready = t_sc

        t_mh = pool([], memset, minus_half[:, :], -0.5)
        t_kz = [pool([], memset, a, v) for z in range(2) for a, v in (
            (k_even[z][64:128, :, :], 0.0), (k_odd[z][0:64, :, :], 0.0), (v_ones[z][:, :, :, HD0:P], 1.0))]

        x_ready = [[] for _ in range(B)]
        for b in range(B):
            k = b % 4
            for n in range(NT):
                tk = pe([g_x, g_const, bank_free[k]], transpose, 
                    psum[:, k, n * P:(n + 1) * P], xn[:, b * NT + n, :], ident[:, :])
            tk = act([tk], copy, xT[:, b * S:(b + 1) * S], psum[:, k, :])
            bank_free[k] = [tk]
            x_ready[b] = [tk]

        AUX, CTX = 6, 7
        hT_free = [[], []]

        def tokens_from_xT(b, dst, wait):
            for n in range(NT):
                tk = pe([x_ready[b], bank_free[AUX]], transpose, psum[:, AUX, n * P:(n + 1) * P],
                        xT[:, b * S + n * P:b * S + (n + 1) * P], ident[:, :])
            tk = act([tk, wait], copy, dst, psum[:, AUX, :].rearrange("p (n d) -> p n d", n=NT))
            bank_free[AUX] = [tk]
            return tk

        def normalise(tok, wait):
            for n in range(NT):
                ts = dve([wait], bn_stats, stats[:, n, :], tok[:, n, :])
            for n in range(NT):
                ta = dve([ts], bn_aggr, moments[:, n, :], stats[:, n, :])
            tr = pool([ta], tensor_scalar, moments[:, :, 1], moments[:, :, 1], EPS, None, ALU.add)
            tr = pool([tr, t_mh], tensor_tensor, rstd[:, :], moments[:, :, 1], minus_half[:, :], ALU.pow)
            for n in range(NT):
                tx = dve([tr], tensor_scalar, tok[:, n, :], tok[:, n, :], moments[:, n, 0:1], rstd[:, n:n + 1],
                         ALU.subtract, ALU.mult)
            return tx

        def modulate(b, L, sc, sh, tok, wait, z):
            for n in range(NT):
                tk = pe([wait, bank_free[AUX]], transpose, psum[:, AUX, n * P:(n + 1) * P], tok[:, n, :], ident[:, :])
            th = act([tk, hT_free[z], mod_ready], activation, hT[:, z, :], psum[:, AUX, :], ACT.Identity,
                     scale=mod[:, L, sc, b:b + 1], bias=mod[:, L, sh, b:b + 1])
            bank_free[AUX] = [th]
            return tk, th

        NU = H0 // GRP * NT

        def attention(scale, order, emit_scores, emit_values, side):
            st = [dict(b=b, g=g, i=i, k0=k0, late=lambda: None) for b in range(B) for g, i, k0 in order]
            for n, u in enumerate(st):
                u["n"] = n
            cm_free, dg_free, prob_free = [[], []], [[], []], [[], []]

            def scores(u):
                k0, i, z = u["k0"], u["i"], u["n"] % 2
                u["scored"] = emit_scores(u)
                if i:
                    u["cm"] = dve([u["scored"], cm_free[z]], tensor_reduce, colmax[:, z, :],
                                  psum[:, k0:k0 + i + 1, :].rearrange("p j c -> p c j"), AX.X, ALU.max)
                else:
                    u["cm"] = act([u["scored"], cm_free[z]], copy, colmax[:, z, :], psum[:, k0, :])

            def maxima(u):
                z = u["n"] % 2
                for h in range(GRP):
                    tk = pe([u["cm"], bank_free[AUX]], transpose, psum[:, AUX, h * P:(h + 1) * P],
                            colmax[:, z, h * P:(h + 1) * P], ident[:, :])
                cm_free[z] = [tk]
                tr = dve([tk], tensor_reduce, rowmax[:, z, :], psum[:, AUX, :].rearrange("p (h k) -> p h k", h=GRP),
                         AX.X, ALU.max)
                bank_free[AUX] = [tr]
                u["diag"] = dve([tr, dg_free[z]], tensor_tensor, negmax[:, z, :, :],
                                neg_ident[:, :].unsqueeze(1).to_broadcast([P, GRP, P]),
                                rowmax[:, z, :].unsqueeze(2).to_broadcast([P, GRP, P]), ALU.mult)

            def shift_and_exp(u):
                k0, i, z = u["k0"], u["i"], u["n"] % 2
                for j in range(i + 1):
                    tk = mm([u["diag"], u["cm"]], psum[:, k0 + j, :], ones_bf[:, :], negmax[:, z, :, :], False)
                dg_free[z] = [tk]
                u["prob"] = act([tk, prob_free[z]], activation, prob[:, z, 0:(i + 1) * BANK],
                                psum[:, k0:k0 + i + 1, :], ACT.Exp, scale=scale)
                for j in range(i + 1):
                    bank_free[k0 + j] = [u["prob"]]

            for f in side.get(-1, []):
                f()
                finish_rotations()
            scores(st[0])
            maxima(st[0])
            scores(st[1])
            for n, u in enumerate(st):
                shift_and_exp(u)
                if n:
                    prob_free[(n - 1) % 2] = [emit_values(st[n - 1])]
                work = side.get(n, [])
                for f in work[0:len(work) // 2]:
                    f()
                if n + 1 < len(st):
                    maxima(st[n + 1])
                if n + 2 < len(st):
                    scores(st[n + 2])
                finish_rotations()
                for f in work[len(work) // 2:]:
                    f()
                if n:
                    st[n - 1]["late"]()
            emit_values(st[-1])
            st[-1]["late"]()
            for f in side.get(len(st), []):
                f()

        def spread_steps(side, steps, first, last):
            for k, f in enumerate(steps):
                side.setdefault(first + k * (last - first + 1) // len(steps), []).append(f)

        st0 = [dict(k={}, q={}, v={}) for _ in range(B)]
        raw_free, rope_free = [[], []], [[], []]
        rot, rotations = [0], []

        def rotate_into(wait_raw, z, table, wait_table, finish):
            ma = pool([wait_raw, wait_table, rope_free[z]], tensor_tensor, rope_a[:, z, :], raw[:, z, :],
                      table[:, 0, :], ALU.mult)
            mb = pool([], tensor_tensor, rope_b[:, z, :], raw[:, z, :], table[:, 1, :], ALU.mult)

            def swap_and_add():
                sw = dve([mb], stream_shuffle, raw[:, z, :], rope_b[:, z, :], SWAP)
                rope_free[z] = raw_free[z] = [finish([ma, sw], z)]

            rotations.append((z, swap_and_add))

        def finish_rotations():
            while rotations:
                rotations.pop(0)[1]()

        def next_rotation():
            rot[0] += 1
            z = rot[0] % 2
            if any(y == z for y, _ in rotations):
                finish_rotations()
            return z

        def project0(b, w, finish):
            z = next_rotation()
            tk = mm([st0[b]["h"], g_w0, bank_free[AUX]], psum[:, AUX, :], w, hT[:, 0, :], True)
            tr = act([tk, raw_free[z]], copy, raw[:, z, :], psum[:, AUX, :])
            bank_free[AUX] = [tr]
            rotate_into(tr, z, rope0, g_const, finish)
            return tk

        kv_free, q_free = [[], []], [[], []]

        def prepare0(b):
            z2 = b % 2
            tok = xn[:, b * NT:(b + 1) * NT, :]

            def stat():
                st0[b]["xn"] = normalise(tok, x_ready[b])

            def norm():
                _, st0[b]["h"] = modulate(b, 0, SC_A, SH_A, tok, st0[b]["xn"], 0)

            def key(kv):
                def fin(w, z):
                    pool([w, kv_free[z2], t_kz], tensor_tensor, k_even[z2][0:64, kv, :], rope_a[0:64, z, :],
                         raw[0:64, z, :], ALU.add)
                    st0[b]["k"][kv] = pool([], tensor_tensor, k_odd[z2][64:128, kv, :], rope_a[64:128, z, :],
                                           raw[64:128, z, :], ALU.add)
                    return st0[b]["k"][kv]
                project0(b, wk[:, kv * P:(kv + 1) * P], fin)

            def value(half):
                for n in (2 * half, 2 * half + 1):
                    tk = mm([st0[b]["h"], g_w0, bank_free[AUX]], psum[:, AUX, (n % 2) * 256:(n % 2 + 1) * 256],
                            hT[:, 0, n * P:(n + 1) * P], wv, start=(n % 2 == 0))
                tv = act([tk, kv_free[z2], t_kz], copy, v_ones[z2][:, 2 * half:2 * half + 2, :, 0:HD0],
                         psum[:, AUX, :].rearrange("p (n k d) -> p n k d", n=2, k=KV0))
                bank_free[AUX] = [tv]
                st0[b]["v"] = tv

            def query(p):
                def fin(w, z):
                    st0[b]["q"][p] = pool([w, q_free[z2]], tensor_tensor, qT[z2][:, p, :], rope_a[:, z, :],
                                          raw[:, z, :], ALU.add)
                    return st0[b]["q"][p]
                tk = project0(b, wq[:, p * P:(p + 1) * P], fin)
                if p == PAIRS - 1:
                    hT_free[0] = [tk]

            return ([stat, norm] + [lambda kv=kv: key(kv) for kv in range(KV0)] +
                    [lambda h=h: value(h) for h in range(2)] + [lambda p=p: query(p) for p in range(PAIRS)])

        def scores0(u):
            b, g, i, k0 = u["b"], u["g"], u["i"], u["k0"]
            z2 = b % 2
            for j in range(i + 1):
                for par, kk in enumerate((k_even[z2], k_odd[z2])):
                    mm([st0[b]["q"][2 * g], st0[b]["q"][2 * g + 1], st0[b]["k"][g], bank_free[k0 + j]],
                       psum[:, k0 + j, par * 256:(par + 1) * 256].rearrange("p (a q) -> p a q", a=2),
                       kk[:, g, j * P:(j + 1) * P], qT[z2][:, 2 * g:2 * g + 2, i * P:(i + 1) * P], start=(par == 0))
            tk = mm([consts_ready], psum[:, k0 + i, :], ident_bf[:, :],
                    causal[:, :].unsqueeze(1).to_broadcast([P, GRP, P]), False)
            if u["n"] % NU == NU - 1:
                q_free[z2] = [tk]
            return tk

        cs_free = [[], []]
        ctx_ready, wo_done = {}, {}

        def values0(u):
            b, g, i, z, z2 = u["b"], u["g"], u["i"], u["n"] % 2, u["b"] % 2
            for j in range(i + 1):
                tk = mm([u["prob"], st0[b]["v"], bank_free[CTX]], psum[:, CTX, :], v_ones[z2][:, j, g, :],
                        prob[:, z, j * BANK:(j + 1) * BANK], start=(j == 0))
            half, zp = g % 2, u["n"] % 2
            rows = slice(64 * half, 64 * half + 64)
            act([tk, cs_free[zp]], copy, ctx_sum[rows, 0, zp, :], psum[0:64, CTX, :])
            tc = act([tk], copy, ctx_sum[rows, 1, zp, :], psum[64:128, CTX, :])
            bank_free[CTX] = [tc]

            def late():
                tr = dve([tc], reciprocal, ctx_sum[:, 1, zp, :], ctx_sum[:, 1, zp, :])
                ctx_ready[b, i] = cs_free[zp] = pool(
                    [tr, wo_done[b - 1, i] if b else []], tensor_tensor,
                    ctxT[:, 2 * g - 2:2 * g + 2, i * P:(i + 1) * P],
                    ctx_sum[:, 0, zp, :].rearrange("p (a q) -> p a q", a=4),
                    ctx_sum[:, 1, zp, :].rearrange("p (a q) -> p a q", a=4), ALU.mult)
            if half:
                u["late"] = late
            if u["n"] % NU == NU - 1:
                kv_free[z2] = [tk]
            return tk

        def finish0(b):
            tok = xn[:, b * NT:(b + 1) * NT, :]

            def out_proj(i):
                for p in range(PAIRS):
                    tk = mm([ctx_ready[b, i], g_w0, bank_free[AUX]], psum[:, AUX, 0:P], wo[:, p, :],
                            ctxT[:, p, i * P:(i + 1) * P], start=(p == 0))
                wo_done[b, i] = tk
                cols = slice(b * S + i * P, b * S + (i + 1) * P)
                tx = dve([tk, mod_ready], scalar_tensor_tensor, xT[:, cols], psum[:, AUX, 0:P],
                         mod[:, 0, GA_A, b:b + 1], xT[:, cols], ALU.mult, ALU.add)
                bank_free[AUX] = [tx]
                x_ready[b] = x_ready[b] + [tx]

            def stat():
                tk = tokens_from_xT(b, tok, [])
                st0[b]["xn2"] = normalise(tok, tk)

            def norm():
                _, st0[b]["h2"] = modulate(b, 0, SC_B, SH_B, tok, st0[b]["xn2"], 1)

            def router():
                for n in range(NT):
                    tk = mm([st0[b]["h2"], g_w0, bank_free[AUX]], psum[:, AUX, n * E:(n + 1) * E],
                            hT[:, 1, n * P:(n + 1) * P], gate, start=(n == 0))
                hT_free[1] = [tk]
                t1 = act([tk], copy, gexp, psum[:, AUX, 0:NT * E].rearrange("p (n e) -> p n e", n=NT))
                bank_free[AUX] = [t1]
                t1 = dve([t1], tensor_reduce, gmax, gexp, AX.X, ALU.max)
                t1 = dve([t1], tensor_tensor, gexp, gexp, gmax.unsqueeze(2).to_broadcast([P, NT, E]), ALU.subtract)
                t1 = act([t1], activation, gexp, gexp, ACT.Exp)
                t1 = dve([t1], tensor_reduce, gsum, gexp, AX.X, ALU.add)
                t1 = dve([t1], reciprocal, gsum, gsum)
                t1 = dve([t1], tensor_tensor, prob_tok[:, :, b, :], gexp, gsum.unsqueeze(2).to_broadcast([P, NT, E]),
                         ALU.mult)

            return [lambda i=i: out_proj(i) for i in (3, 1, 2, 0)] + [stat, norm, router]

        side = {-1: prepare0(0) + prepare0(1)[0:1], B * NU: finish0(B - 1)}
        for b in range(B):
            if b:
                for k, f in zip((0, 0, 1, 2, 3, 5, 6), finish0(b - 1)):
                    side.setdefault(b * NU + k, []).append(f)
            if b + 1 < B:
                spread_steps(side, prepare0(b + 1)[1:], b * NU, b * NU + NU - 4)
            if b + 2 < B:
                side[b * NU + 8].append(prepare0(b + 2)[0])
        order0 = [(g + m, i, k0) for g in range(0, KV0, 2) for two in (((3, 0), (1, 4)), ((2, 0), (0, 4)))
                  for m in range(2) for i, k0 in two]
        attention(HD0 ** -0.5, order0, scores0, values0, side)
        barrier()

        NBE = B * E
        xn = carve([B * NT, D], restart=True)
        Arena.at = ARENA - NT * NBE
        prob_keep = carve([NT, B, E])
        Arena.at = B * NT * D
        t_pk = pool([], tensor_copy, prob_keep, prob_tok)
        barrier()
        prob_tok = prob_keep
        xin = carve([E, B, CAP])
        onehot = carve([NT, E, CAP])
        hid = carve([2, FC, 4 * CAP])
        BACKS = 4
        back = carve([BACKS, S])
        slot_gate = carve([B, E])
        posT = carve([NT, NBE])
        iota = carve([P])
        iota_col = carve([1])
        mark = Arena.at
        assert mark <= ARENA - NT * NBE
        Arena.at = B * NT * D + E * B * CAP + NT * E * CAP
        pw = carve([S])
        work = carve([S])
        top8 = carve([8])
        sel = carve([S])
        eq = carve([S])
        cum = carve([S])
        cnt = carve([1])
        pos_bf = rope_a[:, 0, :].bitcast(BF16)[:, 0:S]
        g_iota = prog.dma_group("d_iota")
        prog.dma(g_ff0, w1, t["L0_w1"].rearrange("e d f -> d e f"))
        prog.dma(g_ff0, w2, t["L0_w2"].rearrange("e (c p) d -> p e c d", p=P))
        prog.dma(g_iota, iota, t["iota"])
        prog.dma(g_iota, iota_col, t["iota_col"])
        R = slice(0, NBE)
        for n in range(NT):
            tk = pe([], transpose, psum[0:NBE, 0, n * P:(n + 1) * P],
                                                   prob_tok[:, n, :, :].rearrange("p b e -> p (b e)"), ident[:, :])
        tp = dve([tk], tensor_copy, pw[R, :], psum[R, 0, :])
        tw = dve([tk], tensor_copy, work[R, :], psum[R, 0, :])
        bank_free[0] = [tw]
        for r in range(CAP // 8):
            tm = dve([tw], max8, top8[R, :], work[R, :])
            if r < CAP // 8 - 1:
                tw = dve([tm], match_replace, work[R, :], top8[R, :], work[R, :], -1.0)
        thr = top8[R, 7:8]
        t1 = dve([tm], tensor_scalar, sel[R, :], pw[R, :], thr, None, ALU.is_gt)
        t2 = dve([tm], tensor_scalar, eq[R, :], pw[R, :], thr, None, ALU.is_equal)
        t3 = dve([t1], tensor_reduce, cnt[R, :], sel[R, :], AX.X, ALU.add)
        t4 = dve([], memset, work[R, :], 1.0)
        t5 = dve([t2, t4], tensor_tensor_scan, cum[R, :], work[R, :], eq[R, :], 0.0, ALU.mult, ALU.add)
        t6 = dve([t3, t5], tensor_scalar, cum[R, :], cum[R, :], cnt[R, 0:1], float(CAP), ALU.add, ALU.is_le)
        t7 = dve([t6], tensor_tensor, eq[R, :], eq[R, :], cum[R, :], ALU.mult)
        t8 = dve([t7], tensor_tensor, sel[R, :], sel[R, :], eq[R, :], ALU.add)
        t9 = dve([t8], tensor_tensor_scan, cum[R, :], work[R, :], sel[R, :], 0.0, ALU.mult, ALU.add)
        t9 = dve([t9], tensor_tensor, cum[R, :], cum[R, :], sel[R, :], ALU.mult)
        t9 = dve([t9], tensor_scalar, cum[R, :], cum[R, :], -1.0, None, ALU.add)
        t10 = dve([t9], tensor_copy, pos_bf[R, :], cum[R, :])
        for n in range(NT):
            tk = pe([t9], transpose, psum[:, 1, n * NBE:(n + 1) * NBE],
                                                     cum[R, n * P:(n + 1) * P], ident[R, R])
        tpos = dve([tk], tensor_copy, posT, psum[:, 1, 0:NT * NBE].rearrange("p (n r) -> p n r", n=NT))
        bank_free[1] = [tpos]
        select_done = [tk, t10, tpos]

        oh_free = []
        xin_ready = []
        for b in range(B):
            for n in range(NT):
                oh_ready = dve([tpos, g_iota, oh_free], tensor_tensor, onehot[:, n, :, :],
                               iota.unsqueeze(1).to_broadcast([P, E, CAP]),
                               posT[:, n, b * E:(b + 1) * E].unsqueeze(2).to_broadcast([P, E, CAP]), ALU.is_equal)
            for q in range(2):
                k = 2 * (b % 2) + q
                for n in range(NT):
                    tk = mm([oh_ready, bank_free[k]], psum[:, k, :], xn[:, b * NT + n, :],
                            onehot[:, n, 4 * q:4 * q + 4, :], start=(n == 0), stop=(n == NT - 1))
                xin_dst = xin[:, 4 * q:4 * q + 4, b, :]
                xin_src = psum[:, k, :].rearrange("p (x c) -> p x c", x=4)
                scale, shift = mod[:, 0, SC_B, b:b + 1], mod[:, 0, SH_B, b:b + 1]
                if q:
                    te = dve([tk], tensor_scalar, xin_dst, xin_src, scale, shift, ALU.mult, ALU.add)
                else:
                    te = act([tk], activation, xin_dst, xin_src, ACT.Identity, scale=scale, bias=shift)
                bank_free[k] = [te]
                xin_ready.append(te)
            kg = 4 + b % 2
            for x in range(E):
                for n in range(NT):
                    tk = mm([oh_ready, bank_free[kg]], psum[:, kg, x:x + 1], onehot[:, n, x, :],
                            prob_tok[:, n, b, x:x + 1], start=(x == 0 and n == 0), stop=(n == NT - 1))
            oh_free = [tk]
            tg = dve([tk], tensor_copy, slot_gate[:, b, :], psum[:, kg, 0:E])
            bank_free[kg] = [tg]

        rounds = [(x, hb) for x in range(E) for hb in range(2)]
        hid_free, hid_ready = [[], []], {}

        def up0(r):
            x, hb = rounds[r]
            for c in range(FC):
                tk = mm([g_ff0, xin_ready, bank_free[c]], psum[:, c, :], w1[:, x, c * P:(c + 1) * P],
                        xin[:, x, 4 * hb:4 * hb + 4, :], start=True)
                hid_ready[r, c] = act([tk, hid_free[r % 2], select_done], activation, hid[:, r % 2, c, :],
                                      psum[:, c, :], ACT.Gelu)
                bank_free[c] = [hid_ready[r, c]]

        def down0(r):
            x, hb = rounds[r]
            z, ky = r % 2, 4 + r % 2
            for s in range(4):
                for c in range(FC):
                    tk = mm([hid_ready[r, c], bank_free[ky]], psum[:, ky, s * P:(s + 1) * P],
                            hid[:, z, c, s * CAP:(s + 1) * CAP], w2[:, x, c, :],
                            start=(s == 0 and c == 0), stop=(c == FC - 1))
            hid_free[z] = [tk]
            ty = dve([tk, tg], tensor_tensor,
                     xin[:, x, 4 * hb:4 * hb + 4, :], psum[:, ky, :].rearrange("p (s d) -> p s d", s=4),
                     slot_gate[:, 4 * hb:4 * hb + 4, x].unsqueeze(2).to_broadcast([P, 4, D]), ALU.mult)
            bank_free[ky] = [ty]
            return ty

        up0(0)
        for r in range(len(rounds)):
            if r + 1 < len(rounds):
                up0(r + 1)
            y_ready = down0(r)

        back_ready, back_free = {}, [[] for _ in range(BACKS)]

        def slots_of_tokens(r):
            kb, z = r % 4, r % BACKS
            tk = mm([t10, bank_free[kb]], psum[:, kb, :], ident_bf[R, r:r + 1].to_broadcast([NBE, P]), pos_bf[R, :],
                    start=True)
            back_ready[r] = dve([tk, back_free[z], g_iota], tensor_scalar, back[:, z, :], psum[:, kb, :],
                                iota_col[:, 0:1], None, ALU.is_equal)
            bank_free[kb] = [back_ready[r]]

        for r in range(BACKS - 1):
            slots_of_tokens(r)
        for b in range(B):
            ko = 4 + b % 2
            for x in range(E):
                r = b * E + x
                if r + BACKS - 1 < NBE:
                    slots_of_tokens(r + BACKS - 1)
                tk = mm([back_ready[r], y_ready, bank_free[ko]], psum[:, ko, :], xin[:, x, b, :],
                        back[:, r % BACKS, :], start=(x == 0), stop=(x == E - 1))
                back_free[r % BACKS] = [tk]
            cols = slice(b * S, (b + 1) * S)
            tx = dve([tk], scalar_tensor_tensor,
                xT[:, cols], psum[:, ko, :], mod[:, 0, GA_B, b:b + 1], xT[:, cols], ALU.mult, ALU.add)
            bank_free[ko] = [tx]
            x_ready[b] = [tx]
        barrier()

        PARTS_K, PARTS_Q = (0, 0, 1, 1, 0, 2), (0, 1, 0, 1, 2, 0)
        ROWS = HD1 * len(PARTS_K)
        k_st = carve([H1 * S // 2], restart=True).bitcast(BF16).rearrange("p (h s) -> p h s", h=H1)
        q_st = carve([H1 * S // 2]).bitcast(BF16).rearrange("p (h s) -> p h s", h=H1)
        v_head = carve([NT, H1, P])
        qx = carve([2, GRP, S])
        part = carve([2, 3, S // 2]).bitcast(BF16)
        rest = carve([S])
        ctx1T = carve([S])
        gm = carve([GRP, P])
        fold = carve([8, P])
        rope1 = carve([2, S])
        wq1, wk1, wv1, wo1 = (carve([D]) for _ in range(4))
        band = carve([BAND_W])
        band_T = carve([NCH + 2, P])
        chunk_mask = carve([P])
        rel0_col = carve([1])
        rel0_row = carve([HD1])
        xn1 = carve([NT, D])
        spread_f = ctx1T[:, 0:P]
        spread = carve([P // 2]).bitcast(BF16)
        for dst, src in ((wq1, "w_qT"), (wk1, "w_kT"), (wv1, "w_vT"), (wo1, "w_oT"), (fold, "fold"),
                         (rope1, "rope1"), (band, "band"), (chunk_mask, "chunk_mask"), (spread_f, "spread")):
            prog.dma(g_w1, dst, t[src])
        prog.dma(g_w1, rel0_row, t["rel_emb"][0:1, :].partition_broadcast(P))
        prog.dma(g_ff1, w1, t["L1_W1"].rearrange("e d f -> d e f"))
        prog.dma(g_ff1, w2, t["L1_W2"].rearrange("e (c p) d -> p e c d", p=P))
        t_spread = dve([g_w1], tensor_copy, spread, spread_f)
        t_r0 = dve([g_w1], tensor_copy, rel0_col, band[:, 0:1])
        t_band = dve([t_r0], tensor_scalar, band, band, rel0_col[:, 0:1], None, ALU.subtract)

        def band_keys(c):
            if c >= NCH:
                return slice(P - RMAX, P)
            first, last = max(CH * c - RMAX, 0), CH * (c + 1)
            return slice(first // 64 * 64, -(-last // 32) * 32)

        def band_slice(c):
            e0 = BAND_E0 - CH * c if c < NCH else BAND_E0 - P - CH * (c - NCH)
            return band[:, e0:e0 + P]

        for c in range(NCH + 2):
            k = c // 4
            tk = pe([t_band], transpose, psum[:, k, (c % 4) * P:(c % 4 + 1) * P], band_slice(c), ident[:, :])
        for k, n in ((0, 4), (1, 4), (2, NCH + 2 - 8)):
            t_bt = dve([tk], tensor_copy, band_T[:, 4 * k:4 * k + n, :],
                       psum[:, k, 0:n * P].rearrange("p (c q) -> p c q", c=n))
            bank_free[k] = [t_bt]
        t_vz = pool([], memset, v_head.rearrange("p a b c -> p (a b c)"), 0.0)

        def head_cols(n, first):
            a = v_head[:, n, 0, first:first + HD1]
            return bass.AP(a.tensor, a.offset, [list(a.ap[0]), [8 * P, 2], [P + HD1, 8], [1, HD1]])

        t_v1 = [pool([t_vz], memset, head_cols(n, 64), 1.0) for n in range(NT)]

        def cols4(a, c):
            return a.rearrange("p (h q) -> p h q", h=GRP)[:, :, c * CH:(c + 1) * CH]

        st1 = [dict() for _ in range(B)]
        g_st = [[prog.dma_group(f"d_stack{w}{z}") for w in "kq"] for z in range(2)]
        g_parts = [prog.dma_group(f"d_parts{w}") for w in "kq"]
        parts_dram = nc.dram_tensor("qk_parts", (B, 2, P, 3, S), BF16, kind="Internal").ap()
        stack_need = {}
        part_free = [[], []]
        rest_free, xn1_free, ctx1_free, v_free, gm_free = [[]], [[]], [[]], [[]], [[]]
        stack_free, qx_free = [[], []], [[], []]
        qx_ready = {}

        def prepare1(b):
            zb = b % 2

            def load():
                st1[b]["tok"] = tokens_from_xT(b, xn1, xn1_free[0])

            def stat():
                st1[b]["xn"] = normalise(xn1, st1[b]["tok"])

            def norm():
                tk, st1[b]["h"] = modulate(b, 1, SC_A, SH_A, xn1, st1[b]["xn"], zb)
                xn1_free[0] = [tk]

            def make(which):
                w, order, stack = ((wk1, PARTS_K, k_st), (wq1, PARTS_Q, q_st))[which]
                z = next_rotation()
                tk = mm([st1[b]["h"], g_w1, bank_free[AUX]], psum[:, AUX, :], w, hT[:, zb, :], True)
                tr = act([tk, raw_free[z]], copy, raw[:, z, :], psum[:, AUX, :])
                bank_free[AUX] = [tr]

                def fin(wait, z):
                    if which == 0:
                        ta = dve([wait, t_r0, rest_free[0]], scalar_tensor_tensor, rest, rope_a[:, z, :],
                                 rel0_col[:, 0:1], raw[:, z, :], ALU.add, ALU.add)
                    else:
                        ta = pool([wait, rest_free[0]], tensor_tensor, rest, rope_a[:, z, :], raw[:, z, :], ALU.add)
                    t1 = act([ta, part_free[which]], copy, part[:, which, 0, :], rest)
                    t2 = pool([t1], tensor_tensor, rest, rest, part[:, which, 0, :], ALU.subtract)
                    t3 = act([t2], copy, part[:, which, 1, :], rest)
                    t4 = pool([t3], tensor_tensor, part[:, which, 2, :], rest, part[:, which, 1, :], ALU.subtract)
                    rest_free[0] = [t4]
                    g_out = g_parts[which]
                    prog.dma(g_out, parts_dram[b, which], part[:, which, :, :], wait=[t4])
                    written = g_out.so_far()
                    part_free[which] = [written]
                    for r, pp in enumerate(order):
                        row = 64 * zb + HD1 * r
                        prog.dma(g_st[zb][which], stack[row:row + HD1, :, :],
                                 parts_dram[b, which, :, pp, :].rearrange("(h d) s -> d h s", h=H1),
                                 wait=[written, stack_free[zb]])
                    stack_need[b, which] = g_st[zb][which].so_far()
                    return ta

                rotate_into(tr, z, rope1, g_w1, fin)

            return [load, stat, norm, lambda: make(0), lambda: make(1)]

        def value1(b):
            zb = b % 2
            for n in range(NT):
                tk = mm([st1[b]["h"], g_w1, bank_free[AUX]], psum[:, AUX, n * P:(n + 1) * P],
                        hT[:, zb, n * P:(n + 1) * P], wv1, start=(n == 0))
            hT_free[zb] = [tk]
            for n in range(NT):
                tv = dve([tk, t_v1, v_free[0]], tensor_tensor, head_cols(n, 0),
                         psum[:, AUX, n * P:(n + 1) * P].rearrange("p (a h d) -> p a h d", a=2, h=8),
                         rel0_row.unsqueeze(1).unsqueeze(1).to_broadcast([P, 2, 8, HD1]), ALU.add)
            bank_free[AUX] = [tv]
            st1[b]["v"] = tv

        def expand(b, h):
            z, r0 = (h // GRP) % 2, 64 * (b % 2)
            tk = mm([stack_need[b, 1], t_spread, bank_free[AUX]], psum[:, AUX, :], spread[r0:r0 + ROWS, :],
                    q_st[r0:r0 + ROWS, h, :], True)
            qx_ready[b, h] = dve([tk, qx_free[z]], tensor_tensor,
                                 qx[:, z, h % GRP, :].rearrange("p (i q) -> p i q", i=NT),
                                 psum[:, AUX, :].rearrange("p (i q) -> p i q", i=NT),
                                 chunk_mask.unsqueeze(1).to_broadcast([P, NT, P]), ALU.mult)
            bank_free[AUX] = [qx_ready[b, h]]

        order1 = [(g, i, k0) for g in range(H1 // GRP) for i, k0 in ((3, 0), (1, 4), (2, 0), (0, 4))]

        def scores1(u):
            b, g, i, k0 = u["b"], u["g"], u["i"], u["k0"]
            z, r0 = g % 2, 64 * (b % 2)
            for j in range(i + 1):
                for h in range(GRP):
                    mm([stack_need[b, 0], stack_need[b, 1], bank_free[k0 + j]],
                       psum[:, k0 + j, h * P:(h + 1) * P], k_st[r0:r0 + ROWS, GRP * g + h, j * P:(j + 1) * P],
                       q_st[r0:r0 + ROWS, GRP * g + h, i * P:(i + 1) * P], start=(h == 0))
            mm([consts_ready], psum[:, k0 + i, :], ident_bf[:, :],
               causal[:, :].unsqueeze(1).to_broadcast([P, GRP, P]), False)
            ahead = u["n"] + NT
            if ahead < B * NU:
                expand(ahead // NU, ahead % NU)
            for c in list(range(NCH)) + ([NCH, NCH + 1] if i else []):
                k, cc = (k0 + i, c) if c < NCH else (k0 + i - 1, c - NCH)
                keys = band_keys(c)
                tk = mm([[qx_ready[b, GRP * g + h] for h in range(GRP)], t_band], cols4(psum[keys, k, :], cc),
                        band_slice(c)[:, keys], qx[:, z, :, i * P + cc * CH:i * P + (cc + 1) * CH], False)
            if i == order1[-1][1]:
                qx_free[z] = [tk]
                if g == NU // NT - 1:
                    stack_free[b % 2] = [tk]
            return tk

        def values1(u):
            b, g, i, z = u["b"], u["g"], u["i"], u["n"] % 2
            pz = prob[:, z, :]
            for c in range(NCH):
                t_g = mm([u["prob"], t_bt, bank_free[AUX]], cols4(psum[:, AUX, :], c), band_T[:, c, :],
                         cols4(pz[:, i * BANK:(i + 1) * BANK], c), start=(c == 0))
            if i:
                for c in range(2):
                    t_g = mm([], cols4(psum[:, AUX, :], c), band_T[:, NCH + c, :],
                             cols4(pz[:, (i - 1) * BANK:i * BANK], c), False)
            t_gm = dve([t_g, gm_free[0]], tensor_tensor, gm, psum[:, AUX, :].rearrange("p (h q) -> p h q", h=GRP),
                       chunk_mask.unsqueeze(1).to_broadcast([P, GRP, P]), ALU.mult)
            bank_free[AUX] = [t_gm]
            first = g % 2 == 0 and i == order1[0][1]
            for j in range(i + 1):
                for h in range(GRP):
                    tk = mm([st1[b]["v"], bank_free[CTX]], psum[:, CTX, i * P:(i + 1) * P],
                            v_head[:, j, GRP * g + h, :], pz[:, j * BANK + h * P:j * BANK + (h + 1) * P],
                            start=(first and j == 0 and h == 0))
            for h in range(GRP):
                t_f = mm([t_gm], psum[:, CTX, i * P:(i + 1) * P], fold[:, GRP * (g % 2) + h, :], gm[:, h, :], False)
            gm_free[0] = [t_f]
            if g % 2 == 1 and i == order1[-1][1]:
                rows = slice(64 * (g // 2), 64 * (g // 2) + 64)
                act([t_f, cs_free[0]], copy, ctx_sum[rows, 0, 0, :], psum[0:64, CTX, :])
                tc = act([t_f], copy, ctx_sum[rows, 1, 0, :], psum[64:128, CTX, :])
                bank_free[CTX] = [tc]

                def late():
                    tr = dve([tc], reciprocal, ctx_sum[:, 1, 0, :], ctx_sum[:, 1, 0, :])
                    st1[b]["ctx"] = pool([tr, ctx1_free[0]], tensor_tensor, ctx1T, ctx_sum[:, 0, 0, :],
                                         ctx_sum[:, 1, 0, :], ALU.mult)
                    cs_free[0] = [st1[b]["ctx"]]
                if g // 2:
                    u["late"] = late
            if u["n"] % NU == NU - 1:
                v_free[0] = [tk]
            return tk

        def finish1(b):
            tk = mm([st1[b]["ctx"], g_w1, bank_free[AUX]], psum[:, AUX, :], wo1, ctx1T, True)
            ctx1_free[0] = [tk]
            cols = slice(b * S, (b + 1) * S)
            tx = dve([tk], scalar_tensor_tensor, xT[:, cols], psum[:, AUX, :], mod[:, 1, GA_A, b:b + 1], xT[:, cols],
                     ALU.mult, ALU.add)
            bank_free[AUX] = [tx]
            x_ready[b] = [tx]

        side = {-1: prepare1(0) + [lambda: value1(0)] + [lambda h=h: expand(0, h) for h in range(GRP)],
                B * NU: [lambda: finish1(B - 1)]}
        for b in range(B):
            if b:
                side.setdefault(b * NU, []).append(lambda b=b: value1(b))
                side.setdefault(b * NU + 3, []).append(lambda b=b: finish1(b - 1))
            if b + 1 < B:
                spread_steps(side, prepare1(b + 1), b * NU, b * NU + 5)
        attention(HD1 ** -0.5, order1, scores1, values1, side)
        barrier()

        hid = carve([2, FC, S], restart=True)
        acc = carve([2, NT, D])
        wr = carve([E])
        br_row = carve([E])
        b1 = carve([E, FC])
        b2 = carve([D])
        keep = carve([NT * E])
        sc = carve([NT, E])
        gt, eq, cum, ex = (carve([NT, E]) for _ in range(4))
        top = carve([NT, 8])
        ngt = carve([NT])
        rw = carve([2, NT, E])
        rwT = carve([2, S])
        xn1 = carve([NT, D])
        out_tok = carve([2, NT, D])
        g_w2 = prog.dma_group("d_w2")
        for dst, src in ((wr, t["Wr"]), (keep, t["keep"]), (b1, t["b1"]),
                         (b2[0:E, :], t["b2"])):
            prog.dma(g_w2, dst, src)
        prog.dma(g_w2, br_row, t["br"].rearrange("(a e) -> a e", a=1).partition_broadcast(P))
        hid_free, hid_ready, acc_free, rwT_free, out_free = [[], []], {}, [[], []], [[], []], [None, None]
        xn1_free, stores = [[]], []
        out_v = out.rearrange("b (n p) d -> p (b n) d", p=P)
        st2 = [dict() for _ in range(B)]

        def before2(b):
            zb, v = b % 2, st2[b]

            def load():
                v["tok"] = tokens_from_xT(b, xn1, xn1_free[0])

            def stat():
                v["xn"] = normalise(xn1, v["tok"])

            def norm():
                tk, v["h"] = modulate(b, 1, SC_B, SH_B, xn1, v["xn"], zb)
                xn1_free[0] = [tk]

            def router():
                for n in range(NT):
                    tk = mm([v["h"], g_w2, bank_free[AUX]], psum[:, AUX, n * E:(n + 1) * E],
                            hT[:, zb, n * P:(n + 1) * P], wr, start=(n == 0))
                t1 = dve([tk], tensor_tensor,
                         sc, psum[:, AUX, 0:NT * E].rearrange("p (n e) -> p n e", n=NT),
                         br_row.unsqueeze(1).to_broadcast([P, NT, E]), ALU.add)
                bank_free[AUX] = [t1]
                for n in range(NT):
                    t2 = dve([t1], max8, top[:, n, :], sc[:, n, :])
                second = top[:, :, 1:2].to_broadcast([P, NT, E])
                ta = dve([t2], tensor_tensor, gt, sc, second, ALU.is_gt)
                tb = dve([t2], tensor_tensor, eq, sc, second, ALU.is_equal)
                t3 = dve([ta], tensor_reduce, ngt, gt, AX.X, ALU.add)
                t4 = dve([tb], tensor_tensor_scan,
                         cum.rearrange("p n e -> p (n e)"), keep, eq.rearrange("p n e -> p (n e)"), 0.0,
                         ALU.mult, ALU.add)
                t4 = dve([t3, t4], tensor_tensor, cum, cum, ngt.unsqueeze(2).to_broadcast([P, NT, E]), ALU.add)
                t4 = dve([t4], tensor_scalar, cum, cum, 2.0, None, ALU.is_le)
                t4 = dve([t4], tensor_tensor, eq, eq, cum, ALU.mult)
                t4 = dve([t4], tensor_tensor, gt, gt, eq, ALU.add)
                t5 = dve([t2], tensor_tensor, ex, sc, top[:, :, 0:1].to_broadcast([P, NT, E]), ALU.subtract)
                v["ex"] = act([t5], activation, ex, ex, ACT.Exp)
                v["gt"] = t4

            def weights():
                t5 = dve([v["ex"], v["gt"]], tensor_tensor, ex, ex, gt, ALU.mult)
                t6 = dve([t5], tensor_reduce, ngt, ex, AX.X, ALU.add)
                t6 = dve([t6], reciprocal, ngt, ngt)
                v["rw"] = dve([t6], tensor_tensor,
                              rw[:, zb, :, :], ex, ngt.unsqueeze(2).to_broadcast([P, NT, E]), ALU.mult)

            def transposed():
                for n in range(NT):
                    tk = pe([v["rw"], bank_free[AUX]], transpose,
                            psum[0:E, AUX, n * P:(n + 1) * P], rw[:, zb, n, :], ident[:, :])
                v["rwT"] = dve([tk, rwT_free[zb]], tensor_copy, rwT[0:E, zb, :], psum[0:E, AUX, :])
                bank_free[AUX] = [v["rwT"]]

            def bias():
                for n in range(NT):
                    tk = mm([v["rwT"], bank_free[AUX]], psum[:, AUX, n * P:(n + 1) * P],
                            rwT[0:E, zb, n * P:(n + 1) * P], b2[0:E, :], start=(n == 0))
                rwT_free[zb] = [tk]
                v["acc"] = [act([tk, acc_free[zb]], copy,
                                acc[:, zb, :, :], psum[:, AUX, :].rearrange("p (n d) -> p n d", n=NT))] * NT
                bank_free[AUX] = [v["acc"][0]]

            return [load, stat, norm, router, weights, transposed, bias]

        def after2(b):
            zb, v = b % 2, st2[b]

            def residual():
                for n in range(NT):
                    tk = pe([v["acc"], bank_free[AUX]], transpose,
                            psum[:, AUX, n * P:(n + 1) * P], acc[:, zb, n, :], ident[:, :])
                acc_free[zb] = [tk]
                cols = slice(b * S, (b + 1) * S)
                v["x"] = dve([tk], scalar_tensor_tensor,
                             xT[:, cols], psum[:, AUX, :], mod[:, 1, GA_B, b:b + 1], xT[:, cols], ALU.mult, ALU.add)
                bank_free[AUX] = [v["x"]]

            def store():
                for n in range(NT):
                    tk = pe([v["x"], bank_free[7]], transpose,
                            psum[:, 7, n * P:(n + 1) * P], xT[:, b * S + n * P:b * S + (n + 1) * P], ident[:, :])
                to = act([tk, out_free[zb]], copy,
                         out_tok[:, zb, :, :], psum[:, 7, :].rearrange("p (n d) -> p n d", n=NT))
                bank_free[7] = [to]
                g_o = prog.dma_group(f"d_out{b}")
                prog.dma(g_o, out_v[:, b * NT:(b + 1) * NT, :], out_tok[:, zb, :, :], wait=[to])
                out_free[zb] = g_o
                stores.append(g_o)

            return [residual, store]

        def up1(r):
            b, x = divmod(r, E)
            for c in range(FC):
                tk = mm([st2[b]["h"], g_ff1, bank_free[c]], psum[:, c, :], w1[:, x, c * P:(c + 1) * P],
                        hT[:, b % 2, :], True)
                hid_ready[r, c] = act([tk, hid_free[r % 2], g_w2], activation, hid[:, r % 2, c, :], psum[:, c, :],
                                      ACT.Gelu_apprx_tanh, bias=b1[:, x, c:c + 1])
                bank_free[c] = [hid_ready[r, c]]
            if x == E - 1:
                hT_free[b % 2] = [tk]

        def down1(r):
            b, x = divmod(r, E)
            z, ky = r % 2, 4 + r % 2
            for n in range(NT):
                for c in range(FC):
                    tk = mm([hid_ready[r, c], bank_free[ky]], psum[:, ky, n * P:(n + 1) * P],
                            hid[:, z, c, n * P:(n + 1) * P], w2[:, x, c, :],
                            start=(n == 0 and c == 0), stop=(c == FC - 1))
            hid_free[z] = [tk]
            st2[b]["acc"] = [dve([tk, st2[b]["acc"][n]], scalar_tensor_tensor,
                                 acc[:, b % 2, n, :], psum[:, ky, n * P:(n + 1) * P], rw[:, b % 2, n, x:x + 1],
                                 acc[:, b % 2, n, :], ALU.mult, ALU.add) for n in range(NT)]
            bank_free[ky] = [st2[b]["acc"][-1]]

        side = {}
        for b in range(B):
            if b + 1 < B:
                for k, f in enumerate(before2(b + 1)):
                    side.setdefault(b * E + k, []).append(f)
                for k, f in enumerate(after2(b)):
                    side.setdefault((b + 1) * E + 1 + 2 * k, []).append(f)
        for f in before2(0):
            f()
        up1(0)
        for r in range(B * E):
            if r + 1 < B * E:
                up1(r + 1)
            for f in side.get(r, []):
                f()
            down1(r)
        for f in after2(B - 1):
            f()
        prog.wait_only("sync", stores)

        prog.run(ctx.enter_context(nc.Block()))


def kernel(**inputs):
    import concourse.bacc as bacc
    from concourse.bass_utils import run_bass_kernel_spmd

    a = {k: np.ascontiguousarray(v) for k, v in inputs.items()}
    arrays = {
        "x": a["L0_attn_hidden_states"], "Wq": a["L0_attn_Wq"], "Wk": a["L0_attn_Wk"], "Wv": a["L0_attn_Wv"],
        "Wo": a["L0_attn_Wo"], "gateT": a["L0_ffn_gate_w"].T, "L0_w1": a["L0_ffn_w1"], "L0_w2": a["L0_ffn_w2"],
        "L0_cT": a["L0_c"].T, "L0_wmod": a["L0_wmod"], "L1_cT": a["L1_c"].T, "L1_wmod": a["L1_wmod"],
        "w_qT": a["L1_attn_w_q"].T, "w_kT": a["L1_attn_w_k"].T, "w_vT": a["L1_attn_w_v"].T,
        "w_oT": a["L1_attn_w_o"].T, "rel_emb": a["L1_attn_rel_emb"],
        "band": a["L1_attn_rel_emb"][band_index()].transpose(0, 2, 1).reshape(P, BAND_W),
        "L1_W1": a["L1_ffn_W1"], "b1": a["L1_ffn_b1"].reshape(E, FC, P).transpose(2, 0, 1), "L1_W2": a["L1_ffn_W2"], "b2": a["L1_ffn_b2"],
        "Wr": a["L1_ffn_Wr"], "br": a["L1_ffn_br"],
    }
    arrays.update(shape_constants())
    nc = bacc.Bacc("TRN2", target_bir_lowering=False, num_devices=1)
    feed, t = {}, {}
    for name, v in arrays.items():
        v = np.ascontiguousarray(v)
        feed[f"in_{name}"] = v
        t[name] = nc.dram_tensor(f"in_{name}", v.shape, mybir.dt.from_np(v.dtype), kind="ExternalInput").ap()
    out = nc.dram_tensor("out", (B, S, D), F32, kind="ExternalOutput").ap()
    build(nc, t, out)
    r = run_bass_kernel_spmd(nc, [feed], core_ids=[0])
    return r.results[0]["out"]
```

```python
from contextlib import ExitStack

import concourse.bass as bass
import numpy as np
from concourse import mybir

F32 = mybir.dt.float32
BF16 = mybir.dt.bfloat16
ALU = mybir.AluOpType
ACT = mybir.ActivationFunctionType
AX = mybir.AxisListType

P = 128
B, S, D = 8, 512, 128
NT = S // P
BANK = 512
H0, KV0, HD0 = 16, 4, 64
PAIRS = H0 // 2
H1, HD1 = 16, 8
RMAX = 32
CH = 16
NCH = P // CH
GRP = 4
E, F = 8, 512
FC = F // P
CAP = 2 * S // E
HALF = 4
EPS = 1e-5
NEG = -1e30
BAND_E0 = P + CH
BAND_W = BAND_E0 + P
TABLES1 = 8 * P + 2 * S + 4 * D + BAND_W + (NCH + 2) * P + P + 1 + HD1 + P // 2

ARENA = 27360

ENGINES = ("tensor", "vector", "scalar", "gpsimd", "sync")


class Token:

    def __init__(self, owner):
        self.owner, self.used, self.value = owner, False, None


class DmaGroup:

    def __init__(self, sem):
        self.sem, self.count = sem, 0
        self.used = True

    @property
    def value(self):
        return 16 * self.count

    def so_far(self):
        now = Token(self)
        now.sem, now.value, now.used = self.sem, 16 * self.count, True
        return now


class Program:

    def __init__(self, nc, ctx):
        self.nc, self.ctx = nc, ctx
        self.queue = {e: [] for e in ENGINES}
        self.sem = {e: ctx.enter_context(nc.semaphore(f"{e}_progress")) for e in ENGINES}
        self.last = {}

    def op(self, engine, wait, emit, *args, **kw):
        token = Token(engine)
        waits = [w for w in flat(wait) if w is not None]
        for w in waits:
            w.used = True
        self.queue[engine].append((waits, lambda e: emit(e, *args, **kw), token))
        self.last[engine] = token
        return token

    def pe(self, wait, emit, *args, **kw):
        return self.op("tensor", wait, emit, *args, **kw)

    def dve(self, wait, emit, *args, **kw):
        return self.op("vector", wait, emit, *args, **kw)

    def act(self, wait, emit, *args, **kw):
        return self.op("scalar", wait, emit, *args, **kw)

    def pool(self, wait, emit, *args, **kw):
        return self.op("gpsimd", [wait, self.last.get("gpsimd")], emit, *args, **kw)

    def dma_group(self, name):
        return DmaGroup(self.ctx.enter_context(self.nc.semaphore(name)))

    def dma(self, group, out, src, wait=(), engine="sync"):
        waits = [w for w in flat(wait) if w is not None]
        for w in waits:
            w.used = True
        group.count += 1
        self.queue[engine].append((waits, lambda e: e.dma_start(out, src).then_inc(group.sem, 16), None))

    def wait_only(self, engine, wait):
        waits = [w for w in flat(wait) if w is not None]
        for w in waits:
            w.used = True
        self.queue[engine].append((waits, None, None))

    def run(self, block):
        for e in ENGINES:
            n = 0
            for _, _, token in self.queue[e]:
                if token is not None and token.used:
                    n += 1
                    token.value = n
        for e in ENGINES:
            getter = {"tensor": block.tensor, "vector": block.vector, "scalar": block.scalar,
                      "gpsimd": block.gpsimd, "sync": block.sync}[e]

            def body(eng, items=self.queue[e], own=self.sem[e]):
                passed = {}
                for waits, emit, token in items:
                    need = {}
                    for w in waits:
                        group = w if isinstance(w, DmaGroup) else w.owner
                        s = group.sem if isinstance(group, DmaGroup) else self.sem[group]
                        k = id(group) if isinstance(group, DmaGroup) else group
                        if w.value > max(passed.get(k, 0), need.get(k, (None, 0))[1]):
                            need[k] = (s, w.value)
                    for k, (s, v) in need.items():
                        eng.wait_ge(s, v)
                        passed[k] = v
                    if emit is None:
                        continue
                    ins = emit(eng)
                    if token is not None and token.used:
                        ins.then_inc(own, 1)

            getter(body)


def activation(eng, *args, **kw):
    return eng.activation(*args, **kw)


def bn_aggr(eng, *args, **kw):
    return eng.bn_aggr(*args, **kw)


def bn_stats(eng, *args, **kw):
    return eng.bn_stats(*args, **kw)


def copy(eng, *args, **kw):
    return eng.copy(*args, **kw)


def match_replace(eng, *args, **kw):
    return eng.match_replace(*args, **kw)


def matmul(eng, *args, **kw):
    return eng.matmul(*args, **kw)


def max8(eng, *args, **kw):
    return eng.max(*args, **kw)


def memset(eng, *args, **kw):
    return eng.memset(*args, **kw)


def reciprocal(eng, *args, **kw):
    return eng.reciprocal(*args, **kw)


def scalar_tensor_tensor(eng, *args, **kw):
    return eng.scalar_tensor_tensor(*args, **kw)


def stream_shuffle(eng, *args, **kw):
    return eng.stream_shuffle(*args, **kw)


def tensor_copy(eng, *args, **kw):
    return eng.tensor_copy(*args, **kw)


def tensor_reduce(eng, *args, **kw):
    return eng.tensor_reduce(*args, **kw)


def tensor_scalar(eng, *args, **kw):
    return eng.tensor_scalar(*args, **kw)


def tensor_tensor(eng, *args, **kw):
    return eng.tensor_tensor(*args, **kw)


def tensor_tensor_scan(eng, *args, **kw):
    return eng.tensor_tensor_scan(*args, **kw)


def transpose(eng, *args, **kw):
    return eng.transpose(*args, **kw)


def flat(x):
    if isinstance(x, (list, tuple)):
        return [z for y in x for z in flat(y)]
    return [x]


def rope_tables(seq, dim, pick_even):
    inv = 1.0 / np.float32(10000.0) ** (np.arange(0, dim, 2, dtype=np.float32) / np.float32(dim))
    ang = np.arange(seq, dtype=np.float32)[:, None] * inv.astype(np.float32)[None, :]
    cos, sin = np.cos(ang), np.sin(ang)
    if pick_even:
        cos = np.concatenate([cos, cos], -1)[:, 0::2]
        sin = np.concatenate([sin, sin], -1)[:, 0::2]
    sign = np.where(np.arange(dim) % 2 == 0, 1.0, -1.0)[:, None]
    return np.repeat(cos.T, 2, 0).astype(np.float32), (sign * np.repeat(sin.T, 2, 0)).astype(np.float32)


SWAP = [p ^ 1 for p in range(32)]


def shape_constants():
    c0, s0 = rope_tables(S, HD0, True)
    c1, s1 = rope_tables(S, HD1, False)
    p = np.arange(P)
    out = {
        "rope0": np.stack([np.tile(c0, (P // HD0, 1)), np.tile(s0, (P // HD0, 1))], 1),
        "rope1": np.stack([np.tile(c1, (P // HD1, 1)), np.tile(s1, (P // HD1, 1))], 1),
        "ident": np.eye(P, dtype=np.float32),
        "causal": np.where(p[:, None] <= p[None, :], 0.0, NEG).astype(np.float32),
        "chunk_mask": (p[None, :] % CH == p[:, None] // HD1).astype(np.float32),
        "iota": np.tile(np.arange(P, dtype=np.float32), (P, 1)),
        "iota_col": p[:, None].astype(np.float32),
    }
    fold = np.zeros((P, 8, P), np.float32)
    for h in range(8):
        for i in range(CH):
            for d in range(HD1):
                fold[i * HD1 + d, h, h * HD1 + d] = 1.0
    out["fold"] = fold
    r = p % 64
    out["spread"] = (np.isin(r // HD1, (0, 1, 4))[:, None] &
                     (r[:, None] % HD1 == p[None, :] % HD1)).astype(np.float32)
    keep = np.ones((P, NT * E), np.float32)
    keep[:, 0::E] = 0.0
    out["keep"] = keep
    return out


def band_index():
    i = np.arange(CH)[:, None]
    e = np.arange(BAND_W)[None, :] - BAND_E0
    return np.clip(e - i, -RMAX, 0) + RMAX


def build(nc, t, out):
    ctx = ExitStack()
    with ctx:
        prog = Program(nc, ctx)
        pe, dve, act, pool = prog.pe, prog.dve, prog.act, prog.pool

        def sb(name, shape, dt=F32):
            return ctx.enter_context(nc.sbuf_tensor(name, shape, dt))

        psum = ctx.enter_context(nc.psum_tensor("psum", [P, 8, BANK], F32))
        xT = sb("xT", [P, B * S])
        ffw = sb("ffw", [P, 2 * E * F])
        w1 = ffw[:, 0:E * F].rearrange("p (e f) -> p e f", e=E)
        w2 = ffw[:, E * F:2 * E * F].rearrange("p (e c d) -> p e c d", e=E, c=FC)
        arena = sb("arena", [P, ARENA])
        ident = sb("ident", [P, P])
        ident_bf = sb("ident_bf", [P, P], BF16)
        neg_ident = sb("neg_ident", [P, P], BF16)
        ones_bf = sb("ones_bf", [P, P], BF16)
        causal = sb("causal", [P, P], BF16)
        modc = sb("modc", [P, 2, B])
        mod_e = sb("mod_e", [P, 2, B])
        mod = sb("mod", [P, 2, 6, B])
        modg = sb("modg", [P, 2, 2, 2, B])
        prob = sb("prob", [P, 2, 4 * BANK])
        causal_f = prob[:, 0, 0:P]
        colmax = sb("colmax", [P, 2, BANK])
        rowmax = sb("rowmax", [P, 2, GRP])
        negmax = sb("negmax", [P, 2, GRP, P], BF16)
        hT = sb("hT", [P, 2, S])
        rope_a = sb("rope_a", [P, 2, S])
        rope_b = sb("rope_b", [P, 2, S])
        raw = sb("raw", [P, 2, S])
        ctx_sum = sb("ctx_sum", [P, 2, 2, BANK])
        gmax = sb("gmax", [P, NT])
        gsum = sb("gsum", [P, NT])
        gexp = sb("gexp", [P, NT, E])
        prob_tok = sb("prob_tok", [P, NT, B, E])
        pos_bf = sb("pos_bf", [HALF * E, 2, S], BF16)
        posT = sb("posT", [P, NT, B * E])
        stats = sb("stats", [P, NT, 6])
        moments = sb("moments", [P, NT, 2])
        rstd = sb("rstd", [P, NT])
        minus_half = sb("minus_half", [P, NT])

        class Arena:
            at = 0

        def carve(shape, restart=False):
            if restart:
                Arena.at = 0
            n = int(np.prod(shape))
            a = arena[:, Arena.at:Arena.at + n]
            Arena.at += n
            assert Arena.at <= ARENA, Arena.at
            names = "abcd"[:len(shape)]
            if len(shape) == 1:
                return a
            return a.rearrange(f"p ({' '.join(names)}) -> p {' '.join(names)}",
                               **{k: v for k, v in zip(names, shape)})

        bank_free = [[] for _ in range(8)]

        def mm(wait, o, lhsT, rhs, start, stop=True):
            return pe(wait, matmul, o, lhsT, rhs, start=start, stop=stop, skip_group_check=True)

        def barrier():
            ends = [prog.last[e] for e in ENGINES if e in prog.last]
            for e in ENGINES:
                prog.wait_only(e, ends)

        g_const, g_x0, g_x, g_w0, g_wo, g_ff0 = (
            prog.dma_group(n) for n in ("d_const", "d_x0", "d_x", "d_w0", "d_wo", "d_ff0"))
        g_w1, g_ff1 = (prog.dma_group(n) for n in ("d_w1", "d_ff1"))

        xn = carve([B * NT, D], restart=True)
        wo = carve([PAIRS, D])
        gate = carve([E])
        ctxT = carve([PAIRS, S])
        attention_at = Arena.at
        wq = carve([D * H0 * HD0 // P])
        wk = carve([KV0 * P])
        wv = carve([KV0 * HD0])
        rope0 = carve([2, S])
        kq = ffw[:, :]
        qT = [carve([PAIRS, S]), kq[:, 0:PAIRS * S].rearrange("p (a s) -> p a s", a=PAIRS)]
        kq = kq[:, PAIRS * S:].rearrange("p (c a s) -> p c a s", c=2, a=KV0)
        k_even = [carve([KV0, S]), kq[:, 0, :, :]]
        k_odd = [carve([KV0, S]), kq[:, 1, :, :]]
        v_ones = [carve([NT, KV0, P]) for _ in range(2)]
        select_at = Arena.at
        assert select_at + 5 * S + 9 <= ARENA
        wmod = ctxT.rearrange("p a s -> p (a s)")[:, 0:12 * D].rearrange("p (a s) -> p a s", a=2)

        x_tok = t["x"].rearrange("b (n p) d -> p (b n) d", p=P)
        prog.dma(g_x0, xn[:, 0:NT, :], x_tok[:, 0:NT, :])
        prog.dma(g_const, ident[:, :], t["ident"])
        prog.dma(g_const, modc[:, 0, :], t["L0_cT"])
        prog.dma(g_const, modc[:, 1, :], t["L1_cT"])
        prog.dma(g_const, wmod[:, 0, :], t["L0_wmod"])
        prog.dma(g_const, wmod[:, 1, :], t["L1_wmod"])
        for c in range(2):
            prog.dma(g_w0, wk.rearrange("p (k c d) -> p k c d", k=KV0, c=2)[:, :, c, :],
                     t["Wk"].rearrange("p (k d) -> p k d", k=KV0))
        prog.dma(g_w0, rope0, t["rope0"])
        prog.dma(g_w0, wq, t["Wq"])
        prog.dma(g_w0, wv, t["Wv"])
        prog.dma(g_x, causal_f, t["causal"])
        prog.dma(g_x, xn[:, NT:B * NT, :], x_tok[:, NT:B * NT, :])
        wo_src = t["Wo"].rearrange("(m half a c p) d -> m half p c a d", m=KV0 // 2, half=2, a=2, c=2)
        for m in range(KV0 // 2):
            for half in range(2):
                for c in range(2):
                    prog.dma(g_wo, wo[half * HD0:(half + 1) * HD0, 4 * m + 2 * c:4 * m + 2 * c + 2, :],
                             wo_src[m, half, :, c])
        prog.dma(g_wo, gate, t["gateT"])

        t_ones = dve([], memset, ones_bf[:, :], 1.0)
        t_ident = dve([g_const], tensor_copy, ident_bf[:, :], ident[:, :])
        t_nid = dve([], tensor_scalar, neg_ident[:, :], ident[:, :], -1.0, None, ALU.mult)

        t_e = act([g_const], activation, mod_e[:, :, :], modc[:, :, :], ACT.Exp, scale=-1.0)
        t_e = dve([t_e], tensor_scalar, mod_e[:, :, :], mod_e[:, :, :], 1.0, None, ALU.add)
        t_e = dve([t_e], reciprocal, mod_e[:, :, :], mod_e[:, :, :])
        t_silu = dve([t_e], tensor_tensor, modc[:, :, :], modc[:, :, :], mod_e[:, :, :], ALU.mult)
        for L in range(2):
            for j in range(6):
                t_mod = mm([t_silu, g_const], psum[:, 7, (L * 6 + j) * B:(L * 6 + j + 1) * B],
                           wmod[:, L, j * D:(j + 1) * D], modc[:, L, :], start=(L + j == 0))
        t_mod = dve([t_mod], tensor_copy,
            mod[:, :, :, :].rearrange("p a b c -> p (a b c)"), psum[:, 7, 0:12 * B])
        bank_free[7] = [t_mod]
        SH_A, SC_A, GA_A, SH_B, SC_B, GA_B = range(6)
        t_sc = [dve([t_mod], tensor_scalar, mod[:, :, j, :], mod[:, :, j, :], 1.0, None, ALU.add)
                for j in (SC_A, SC_B)]
        for n, j in enumerate((GA_A, GA_B)):
            g, sgn, mag = mod[:, :, j, :], modg[:, :, n, 0, :], modg[:, :, n, 1, :]
            t1 = dve([t_mod], tensor_scalar, sgn, g, 0.0, 2.0, ALU.is_ge, ALU.mult)
            t2 = dve([t1], tensor_scalar, sgn, sgn, -1.0, None, ALU.add)
            t3 = dve([t_mod], tensor_scalar, mag, g, -1.0, None, ALU.mult)
            t3 = dve([t3], tensor_tensor, mag, mag, g, ALU.max)
            t3 = dve([t3], tensor_scalar, mag, mag, 0.25, None, ALU.max)
            t_g = dve([t2, t3], tensor_tensor, g, sgn, mag, ALU.mult)
            t_sc.append(t_g)
        mod_ready = t_sc
        t_causal = dve([g_x], tensor_copy, causal[:, :], causal_f)
        consts_ready = [t_ones, t_ident, t_nid, t_causal]

        t_mh = pool([], memset, minus_half[:, :], -0.5)
        t_kz = {}

        def constant_parts(z):
            t_kz[z] = [pool([], memset, a, v) for a, v in (
                (k_even[z][64:128, :, :], 0.0), (k_odd[z][0:64, :, :], 0.0), (v_ones[z][:, :, :, HD0:P], 1.0))]

        constant_parts(0)

        x_ready = [[] for _ in range(B)]

        def transpose_x(b):
            k = b % 4
            for n in range(NT):
                tk = pe([g_x if b else g_x0, g_const, bank_free[k]], transpose,
                        psum[:, k, n * P:(n + 1) * P], xn[:, b * NT + n, :], ident[:, :])
            tk = act([tk], copy, xT[:, b * S:(b + 1) * S], psum[:, k, :])
            bank_free[k] = [tk]
            x_ready[b] = [tk]

        AUX, CTX = 6, 7
        hT_free = [[], []]

        def tokens_from_xT(b, dst, wait):
            for n in range(NT):
                tk = pe([x_ready[b], bank_free[AUX]], transpose, psum[:, AUX, n * P:(n + 1) * P],
                        xT[:, b * S + n * P:b * S + (n + 1) * P], ident[:, :])
            tk = act([tk, wait], copy, dst, psum[:, AUX, :].rearrange("p (n d) -> p n d", n=NT))
            bank_free[AUX] = [tk]
            return tk

        moments_free = [[]]

        def statistics(tok, wait):
            for n in range(NT):
                ts = dve([wait, moments_free[0]], bn_stats, stats[:, n, :], tok[:, n, :])
            for n in range(NT):
                ta = dve([ts], bn_aggr, moments[:, n, :], stats[:, n, :])
            tr = pool([ta], tensor_scalar, moments[:, :, 1], moments[:, :, 1], EPS, None, ALU.add)
            return pool([tr, t_mh], tensor_tensor, rstd[:, :], moments[:, :, 1], minus_half[:, :], ALU.pow)

        def normalise(tok, wait):
            for n in range(NT):
                tx = dve([wait], tensor_scalar, tok[:, n, :], tok[:, n, :], moments[:, n, 0:1], rstd[:, n:n + 1],
                         ALU.subtract, ALU.mult)
            moments_free[0] = [tx]
            return tx

        def modulate(b, L, sc, sh, tok, wait, z):
            for n in range(NT):
                tk = pe([wait, bank_free[AUX]], transpose, psum[:, AUX, n * P:(n + 1) * P], tok[:, n, :], ident[:, :])
            th = act([tk, hT_free[z], mod_ready], activation, hT[:, z, :], psum[:, AUX, :], ACT.Identity,
                     scale=mod[:, L, sc, b:b + 1], bias=mod[:, L, sh, b:b + 1])
            bank_free[AUX] = [th]
            return tk, th

        NU = H0 // GRP * NT

        prob_free = [[], []]

        def attention(scale, order, emit_scores, emit_values, side, pairs=False,
                      at_end=lambda: None):
            st = [dict(b=b, g=g, i=i, k0=k0, late=lambda: None) for b in range(B) for g, i, k0 in order]
            for n, u in enumerate(st):
                u["n"] = n
            cm_free, dg_free = [[], []], [[], []]

            def scores(u):
                k0, i, z = u["k0"], u["i"], u["n"] % 2
                u["scored"] = emit_scores(u)
                if i:
                    u["cm"] = dve([u["scored"], cm_free[z]], tensor_reduce, colmax[:, z, :],
                                  psum[:, k0:k0 + i + 1, :].rearrange("p j c -> p c j"), AX.X, ALU.max)
                else:
                    u["cm"] = act([u["scored"], cm_free[z]], copy, colmax[:, z, :], psum[:, k0, :])

            def maxima(u):
                z = u["n"] % 2
                for h in range(GRP):
                    tk = pe([u["cm"], bank_free[AUX]], transpose, psum[:, AUX, h * P:(h + 1) * P],
                            colmax[:, z, h * P:(h + 1) * P], ident[:, :])
                cm_free[z] = [tk]
                tr = dve([tk], tensor_reduce, rowmax[:, z, :], psum[:, AUX, :].rearrange("p (h k) -> p h k", h=GRP),
                         AX.X, ALU.max)
                bank_free[AUX] = [tr]
                u["diag"] = dve([tr, dg_free[z]], tensor_tensor, negmax[:, z, :, :],
                                neg_ident[:, :].unsqueeze(1).to_broadcast([P, GRP, P]),
                                rowmax[:, z, :].unsqueeze(2).to_broadcast([P, GRP, P]), ALU.mult)

            def shift(u):
                for j in range(u["i"] + 1):
                    tk = mm([u["diag"], u["cm"]], psum[:, u["k0"] + j, :], ones_bf[:, :],
                            negmax[:, u["n"] % 2, :, :], False)
                dg_free[u["n"] % 2] = [tk]
                u["shifted"] = tk

            def exponentiate(u):
                k0, i, z = u["k0"], u["i"], u["n"] % 2
                u["prob"] = act([u["shifted"], prob_free[z]], activation, prob[:, z, 0:(i + 1) * BANK],
                                psum[:, k0:k0 + i + 1, :], ACT.Exp, scale=scale)
                for j in range(i + 1):
                    bank_free[k0 + j] = [u["prob"]]

            for f in side.get(-1, []):
                f()
                finish_rotations()
            scores(st[0])
            maxima(st[0])
            scores(st[1])
            for n, u in enumerate(st):
                early = n == 0 or not pairs or n % 2
                shift(u)
                if early:
                    exponentiate(u)
                if n:
                    emit_values(st[n - 1])
                if not early:
                    exponentiate(u)
                work = side.get(n, [])
                for f in work[0:len(work) // 2]:
                    f()
                if n + 1 < len(st):
                    maxima(st[n + 1])
                if n + 2 < len(st):
                    scores(st[n + 2])
                finish_rotations()
                for f in work[len(work) // 2:]:
                    f()
                if n:
                    st[n - 1]["late"]()
            emit_values(st[-1])
            at_end()
            st[-1]["late"]()
            for f in side.get(len(st), []):
                f()

        def spread_steps(side, steps, first, last):
            for k, f in enumerate(steps):
                side.setdefault(first + k * (last - first + 1) // len(steps), []).append(f)

        st0 = [dict(k={}, q={}) for _ in range(B)]
        raw_free, rope_free = [[], []], [[], []]
        turns, rotations = [0], []

        def rotate_into(wait_raw, z, table, wait_table, finish, mult=pool):
            ma = mult([wait_raw, wait_table, rope_free[z]], tensor_tensor, rope_a[:, z, :], raw[:, z, :],
                      table[:, 0, :], ALU.mult)
            mb = pool([wait_raw, wait_table, rope_free[z]], tensor_tensor, rope_b[:, z, :], raw[:, z, :],
                      table[:, 1, :], ALU.mult)

            def swap_and_add():
                sw = dve([ma, mb], stream_shuffle, raw[:, z, :], rope_b[:, z, :], SWAP)
                rope_free[z] = raw_free[z] = [finish([ma, sw], z)]

            rotations.append((z, swap_and_add))

        def finish_rotations():
            while rotations:
                rotations.pop(0)[1]()

        def next_rotation():
            turns[0] += 1
            z = turns[0] % 2
            if any(y == z for y, _ in rotations):
                finish_rotations()
            return z

        def project0(b, w, finish):
            z = next_rotation()
            tk = mm([st0[b]["h"], g_w0, bank_free[AUX]], psum[:, AUX, :], w, hT[:, 0, :], True)
            tr = act([tk, raw_free[z]], copy, raw[:, z, :], psum[:, AUX, :])
            bank_free[AUX] = [tr]
            rotate_into(tr, z, rope0, g_w0, finish, pool if b else dve)
            return tk

        kv_free, q_free = [[], []], [[], []]

        def prepare0(b):
            z2 = b % 2
            tok = xn[:, b * NT:(b + 1) * NT, :]

            def stat():
                st0[b]["stat"] = statistics(tok, x_ready[b])

            def center():
                st0[b]["xn"] = normalise(tok, st0[b]["stat"])

            def norm():
                _, st0[b]["h"] = modulate(b, 0, SC_A, SH_A, tok, st0[b]["xn"], 0)

            def key(kv):
                def fin(w, z):
                    pool([w, kv_free[z2], t_kz[z2]], tensor_tensor, k_even[z2][0:64, kv, :], rope_a[0:64, z, :],
                         raw[0:64, z, :], ALU.add)
                    st0[b]["k"][kv] = pool([], tensor_tensor, k_odd[z2][64:128, kv, :], rope_a[64:128, z, :],
                                           raw[64:128, z, :], ALU.add)
                    return st0[b]["k"][kv]
                project0(b, wk[:, kv * P:(kv + 1) * P], fin)

            def value(half):
                for n in (2 * half, 2 * half + 1):
                    tk = mm([st0[b]["h"], g_w0, bank_free[AUX]], psum[:, AUX, (n % 2) * 256:(n % 2 + 1) * 256],
                            hT[:, 0, n * P:(n + 1) * P], wv, start=(n % 2 == 0))
                tv = act([tk, kv_free[z2], t_kz[z2]], copy, v_ones[z2][:, 2 * half:2 * half + 2, :, 0:HD0],
                         psum[:, AUX, :].rearrange("p (n k d) -> p n k d", n=2, k=KV0))
                bank_free[AUX] = [tv]
                st0[b]["v"] = tv

            def query(p):
                def fin(w, z):
                    st0[b]["q"][p] = pool([w, q_free[z2]], tensor_tensor, qT[z2][:, p, :], rope_a[:, z, :],
                                          raw[:, z, :], ALU.add)
                    return st0[b]["q"][p]
                tk = project0(b, wq[:, p * P:(p + 1) * P], fin)
                hT_free[0] = [tk]

            keys = [lambda kv=kv: key(kv) for kv in range(KV0)]
            queries = [lambda p=p: query(p) for p in range(PAIRS)]
            return ([stat, center, norm, keys[0], *queries[0:2], keys[1], *queries[2:4],
                     lambda: value(0), lambda: value(1)], keys[2:] + queries[4:])

        def select(half, scratch):
            rows = HALF * E
            pw, work, sel, eq, cum = (scratch[0:rows, k * S:(k + 1) * S] for k in range(5))
            top8, cnt = scratch[0:rows, 5 * S:5 * S + 8], scratch[0:rows, 5 * S + 8:5 * S + 9]
            v = {}

            def load():
                for n in range(NT):
                    tk = pe([router_done[HALF * half + HALF - 1], bank_free[AUX]],
                            transpose, psum[0:rows, AUX, n * P:(n + 1) * P],
                            prob_tok[:, n, HALF * half:HALF * (half + 1), :].rearrange("p b e -> p (b e)"),
                            ident[:, :])
                dve([tk], tensor_copy, pw, psum[0:rows, AUX, :])
                v["w"] = dve([tk], tensor_copy, work, psum[0:rows, AUX, :])
                bank_free[AUX] = [v["w"]]

            def eight(r):
                v["top"] = dve([v["w"]], max8, top8, work)
                if r < CAP // 8 - 1:
                    v["w"] = dve([v["top"]], match_replace, work, top8, work, -1.0)

            def threshold():
                thr = top8[:, 7:8]
                t1 = dve([v["top"]], tensor_scalar, sel, pw, thr, None, ALU.is_gt)
                t2 = dve([v["top"]], tensor_scalar, eq, pw, thr, None, ALU.is_equal)
                t3 = dve([t1], tensor_reduce, cnt, sel, AX.X, ALU.add)
                t4 = dve([v["top"]], memset, work, 1.0)
                v["t5"] = [t3, dve([t2, t4], tensor_tensor_scan, cum, work, eq, 0.0, ALU.mult, ALU.add)]

            def choice():
                t6 = dve(v["t5"], tensor_scalar, cum, cum, cnt, float(CAP), ALU.add, ALU.is_le)
                t7 = dve([t6], tensor_tensor, eq, eq, cum, ALU.mult)
                v["t8"] = dve([t7], tensor_tensor, sel, sel, eq, ALU.add)

            def slots():
                t9 = dve([v["t8"]], tensor_tensor_scan, cum, work, sel, 0.0, ALU.mult, ALU.add)
                t9 = dve([t9], tensor_tensor, cum, cum, sel, ALU.mult)
                v["t9"] = dve([t9], tensor_scalar, cum, cum, -1.0, None, ALU.add)
                v["bf"] = dve([v["t9"]], tensor_copy, pos_bf[:, half, :], cum)

            def transposed():
                for n in range(NT):
                    tk = pe([v["t9"], bank_free[AUX]], transpose, psum[:, AUX, n * rows:(n + 1) * rows],
                            cum[:, n * P:(n + 1) * P], ident[0:rows, 0:rows])
                tp = dve([tk], tensor_copy, posT[:, :, half * rows:(half + 1) * rows],
                         psum[:, AUX, 0:NT * rows].rearrange("p (n r) -> p n r", n=NT))
                bank_free[AUX] = [tp]
                chosen[half] = [v["bf"], tp]

            return ([load] + [lambda r=r: eight(r) for r in range(CAP // 8)] +
                    [threshold, choice, slots, transposed])

        router_done, chosen = {}, {}

        def scores0(u):
            b, g, i, k0 = u["b"], u["g"], u["i"], u["k0"]
            z2 = b % 2
            for j in range(i + 1):
                for par, kk in enumerate((k_even[z2], k_odd[z2])):
                    mm([st0[b]["q"][2 * g], st0[b]["q"][2 * g + 1], st0[b]["k"][g], bank_free[k0 + j]],
                       psum[:, k0 + j, par * 256:(par + 1) * 256].rearrange("p (a q) -> p a q", a=2),
                       kk[:, g, j * P:(j + 1) * P], qT[z2][:, 2 * g:2 * g + 2, i * P:(i + 1) * P], start=(par == 0))
            tk = mm([consts_ready], psum[:, k0 + i, :], ident_bf[:, :],
                    causal[:, :].unsqueeze(1).to_broadcast([P, GRP, P]), False)
            if u["n"] % NU == NU - 1:
                q_free[z2] = [tk]
            return tk

        cs_free = [[], []]
        ctx_ready, wo_done = {}, {}

        def values0(u):
            b, g, i, z, z2 = u["b"], u["g"], u["i"], u["n"] % 2, u["b"] % 2
            for j in range(i + 1):
                tk = mm([u["prob"], st0[b]["v"], bank_free[CTX]], psum[:, CTX, :], v_ones[z2][:, j, g, :],
                        prob[:, z, j * BANK:(j + 1) * BANK], start=(j == 0))
            half, zp = g % 2, u["n"] % 2
            rows = slice(64 * half, 64 * half + 64)
            act([tk, cs_free[zp]], copy, ctx_sum[rows, 0, zp, :], psum[0:64, CTX, :])
            tc = act([tk], copy, ctx_sum[rows, 1, zp, :], psum[64:128, CTX, :])
            bank_free[CTX] = [tc]

            def late():
                tr = dve([tc], reciprocal, ctx_sum[:, 1, zp, :], ctx_sum[:, 1, zp, :])
                ctx_ready[b, i] = cs_free[zp] = pool(
                    [tr, wo_done[b - 1, i] if b else []], tensor_tensor,
                    ctxT[:, 2 * g - 2:2 * g + 2, i * P:(i + 1) * P],
                    ctx_sum[:, 0, zp, :].rearrange("p (a q) -> p a q", a=4),
                    ctx_sum[:, 1, zp, :].rearrange("p (a q) -> p a q", a=4), ALU.mult)
            if half:
                u["late"] = late
            prob_free[z] = [tk]
            if u["n"] % NU == NU - 1:
                kv_free[z2] = [tk]

        def finish0(b):
            tok = xn[:, b * NT:(b + 1) * NT, :]

            def out_proj(i):
                for p in range(PAIRS):
                    tk = mm([ctx_ready[b, i], g_wo, bank_free[AUX]], psum[:, AUX, 0:P], wo[:, p, :],
                            ctxT[:, p, i * P:(i + 1) * P], start=(p == 0))
                wo_done[b, i] = tk
                cols = slice(b * S + i * P, b * S + (i + 1) * P)
                tx = dve([tk, mod_ready], scalar_tensor_tensor, xT[:, cols], psum[:, AUX, 0:P],
                         mod[:, 0, GA_A, b:b + 1], xT[:, cols], ALU.mult, ALU.add)
                bank_free[AUX] = [tx]
                x_ready[b] = x_ready[b] + [tx]

            def stat():
                tk = tokens_from_xT(b, tok, [])
                st0[b]["stat2"] = statistics(tok, tk)

            def center():
                st0[b]["xn2"] = normalise(tok, st0[b]["stat2"])

            def norm():
                _, st0[b]["h2"] = modulate(b, 0, SC_B, SH_B, tok, st0[b]["xn2"], 1)

            def router():
                for n in range(NT):
                    tk = mm([st0[b]["h2"], g_wo, bank_free[AUX]], psum[:, AUX, n * E:(n + 1) * E],
                            hT[:, 1, n * P:(n + 1) * P], gate, start=(n == 0))
                hT_free[1] = [tk]
                t1 = act([tk], copy, gexp[:, :, :], psum[:, AUX, 0:NT * E].rearrange("p (n e) -> p n e", n=NT))
                bank_free[AUX] = [t1]
                t1 = dve([t1], tensor_reduce, gmax[:, :], gexp[:, :, :], AX.X, ALU.max)
                t1 = dve([t1], tensor_tensor, gexp[:, :, :], gexp[:, :, :],
                         gmax[:, :].unsqueeze(2).to_broadcast([P, NT, E]), ALU.subtract)
                t1 = act([t1], activation, gexp[:, :, :], gexp[:, :, :], ACT.Exp)
                t1 = dve([t1], tensor_reduce, gsum[:, :], gexp[:, :, :], AX.X, ALU.add)
                t1 = dve([t1], reciprocal, gsum[:, :], gsum[:, :])
                router_done[b] = dve([t1], tensor_tensor, prob_tok[:, :, b, :], gexp[:, :, :],
                                     gsum[:, :].unsqueeze(2).to_broadcast([P, NT, E]), ALU.mult)

            return [lambda i=i: out_proj(i) for i in (3, 1, 2, 0)] + [stat, center, norm, router]

        transpose_x(0)
        first, rest0 = prepare0(0)
        side = {-1: first + [lambda: [transpose_x(b) for b in range(1, B)], lambda: constant_parts(1)]}
        for b in range(B):
            if b:
                for k, f in enumerate(finish0(b - 1)):
                    side.setdefault(b * NU + k, []).append(f)
            for k, f in enumerate(rest0):
                side.setdefault(b * NU + k, []).append(f)
            if b + 1 < B:
                first, rest0 = prepare0(b + 1)
                for k, f in zip((1, 2, *range(6, 15)), first):
                    side.setdefault(b * NU + k, []).append(f)
            if b == HALF + 1:
                spread_steps(side, select(0, arena[:, select_at:select_at + 5 * S + 9]), b * NU, (b + 2) * NU - 1)
        order0 = [(g + m, i, k0) for g in range(0, KV0, 2) for two in (((3, 0), (1, 4)), ((2, 0), (0, 4)))
                  for m in range(2) for i, k0 in two]
        attention(HD0 ** -0.5, order0, scores0, values0, side, at_end=barrier)

        xn = carve([B * NT, D], restart=True)
        hid = carve([2, FC, 4 * CAP])
        assert Arena.at <= attention_at
        Arena.at = attention_at
        onehot = carve([NT * E * CAP]).bitcast(BF16).rearrange("p (z n e c) -> p z n e c", z=2, n=NT, e=E)
        xin = carve([E, B, CAP])
        BACKS = 4
        back_at = attention_at - E
        back = arena[:, back_at:back_at + BACKS * S].rearrange("p (a s) -> p a s", a=BACKS)
        slot_gate = carve([B, E])
        iota = carve([P])
        iota_col = carve([1])
        prob_parts = carve([3 * NT * B * E // 2]).bitcast(BF16).rearrange("p (n b e c) -> p n b e c", n=NT, b=B, e=E)
        prob_rest = rope_a[:, 0, 0:NT * B * E].rearrange("p (n b e) -> p n b e", n=NT, b=B)
        parts = [a[:, :, :].rearrange("p a s -> p (a s)").bitcast(BF16)[:, 0:3 * S].rearrange("p (c s) -> p c s", c=3)
                 for a in (rope_b, raw)]
        tables_at = ARENA - TABLES1
        assert Arena.at <= tables_at
        Arena.at = tables_at
        fold = carve([8, P])
        rope1 = carve([2, S])
        wq1, wk1, wv1, wo1 = (carve([D]) for _ in range(4))
        band = carve([BAND_W])
        band_T = carve([NCH + 2, P])
        chunk_mask = carve([P])
        rel0_col = carve([1])
        rel0_row = carve([HD1])
        spread = carve([P // 2]).bitcast(BF16)
        spread_f = colmax[:, 0, 0:P]
        g_iota = prog.dma_group("d_iota")
        prog.dma(g_iota, iota, t["iota"])
        prog.dma(g_iota, iota_col, t["iota_col"])
        prog.dma(g_ff0, w1, t["L0_w1"].rearrange("e d f -> d e f"))
        prog.dma(g_ff0, w2, t["L0_w2"].rearrange("e (c p) d -> p e c d", p=P))
        for dst, src in ((wq1, "w_qT"), (wk1, "w_kT"), (wv1, "w_vT"), (wo1, "w_oT"), (fold, "fold"),
                         (rope1, "rope1"), (band, "band"), (chunk_mask, "chunk_mask"), (spread_f, "spread")):
            prog.dma(g_w1, dst, t[src])
        prog.dma(g_w1, rel0_row, t["rel_emb"][0:1, :].partition_broadcast(P))

        def split_prob(half):
            bs = slice(half * HALF, (half + 1) * HALF)
            tok, rest = prob_tok[:, :, bs, :], prob_rest[:, :, bs, :]
            h, m, l = (prob_parts[:, :, bs, :, c] for c in range(3))
            t1 = act([router_done[(half + 1) * HALF - 1]], copy, h, tok)
            t2 = pool([t1], tensor_tensor, rest, tok, h, ALU.subtract)
            t3 = act([t2], copy, m, rest)
            prob_split[half] = pool([t3], tensor_tensor, l, rest, m, ALU.subtract)

        oh_free, part_free = [[], []], [[], []]
        xin_ready, gate_ready, prob_split = [[], []], [None, None], [None, None]
        gather_in = {}

        def before_gather(b):
            z, half = b % 2, b // HALF
            tok = xn[:, b * NT:(b + 1) * NT, :].rearrange("p n d -> p (n d)")
            t1 = act([part_free[z], st0[b]["h2"]], copy, parts[z][:, 0, :], tok)
            t2 = pool([t1], tensor_tensor, tok, tok, parts[z][:, 0, :], ALU.subtract)
            t3 = act([t2], copy, parts[z][:, 1, :], tok)
            t_parts = pool([t3], tensor_tensor, parts[z][:, 2, :], tok, parts[z][:, 1, :], ALU.subtract)
            for n in range(NT):
                oh_ready = dve([chosen[half], g_iota, oh_free[z]], tensor_tensor, onehot[:, z, n, :, :],
                               iota.unsqueeze(1).to_broadcast([P, E, CAP]),
                               posT[:, n, b * E:(b + 1) * E].unsqueeze(2).to_broadcast([P, E, CAP]), ALU.is_equal)
            gather_in[b] = [t_parts, oh_ready]

        def gather(b):
            z, half = b % 2, b // HALF
            for q in range(2):
                k = 2 * z + q
                for n in range(NT):
                    for c in range(3):
                        tk = mm([gather_in[b], bank_free[k]], psum[:, k, :], parts[z][:, c, n * P:(n + 1) * P],
                                onehot[:, z, n, 4 * q:4 * q + 4, :], start=(n + c == 0))
                te = act([tk], activation, xin[:, 4 * q:4 * q + 4, b, :],
                         psum[:, k, :].rearrange("p (x c) -> p x c", x=4), ACT.Identity,
                         scale=mod[:, 0, SC_B, b:b + 1], bias=mod[:, 0, SH_B, b:b + 1])
                bank_free[k] = [te]
                xin_ready[half].append(te)
            part_free[z] = [tk]
            kg = 4 + z
            for x in range(E):
                for n in range(NT):
                    tk = mm([prob_split[half], bank_free[kg]], psum[:, kg, 3 * x:3 * x + 3],
                            onehot[:, z, n, x, :], prob_parts[:, n, b, x, :], start=(x + n == 0))
            oh_free[z] = [tk]
            tg = dve([tk], tensor_reduce, slot_gate[:, b, :], psum[:, kg, 0:3 * E].rearrange("p (x c) -> p x c", x=E),
                     AX.X, ALU.add)
            bank_free[kg] = [tg]
            gate_ready[half] = tg

        rounds = [(x, hb) for hb in range(2) for x in range(E)]
        hid_free, hid_ready = [[], []], {}

        def up0(r):
            x, hb = rounds[r]
            for c in range(FC):
                tk = mm([g_ff0, xin_ready[hb], bank_free[c]], psum[:, c, :], w1[:, x, c * P:(c + 1) * P],
                        xin[:, x, 4 * hb:4 * hb + 4, :], start=True)
                hid_ready[r, c] = act([tk, hid_free[r % 2]], activation, hid[:, r % 2, c, :],
                                      psum[:, c, :], ACT.Gelu)
                bank_free[c] = [hid_ready[r, c]]

        def down0(r):
            x, hb = rounds[r]
            z, ky = r % 2, 4 + r % 2
            for s in range(4):
                for c in range(FC):
                    tk = mm([hid_ready[r, c], bank_free[ky]], psum[:, ky, s * P:(s + 1) * P],
                            hid[:, z, c, s * CAP:(s + 1) * CAP], w2[:, x, c, :],
                            start=(s == 0 and c == 0), stop=(c == FC - 1))
            hid_free[z] = [tk]
            ty = dve([tk, gate_ready[hb]], tensor_tensor,
                     xin[:, x, 4 * hb:4 * hb + 4, :], psum[:, ky, :].rearrange("p (s d) -> p s d", s=4),
                     slot_gate[:, 4 * hb:4 * hb + 4, x].unsqueeze(2).to_broadcast([P, 4, D]), ALU.mult)
            bank_free[ky] = [ty]
            return ty

        last_steps = finish0(B - 1)
        for n, f in enumerate(last_steps[0:5]):
            f()
            if n == 0:
                split_prob(0)
            if n == 1:
                before_gather(0)
        for b in range(HALF):
            if b + 1 < HALF:
                before_gather(b + 1)
            gather(b)
            for f in last_steps[5 + b:6 + b]:
                f()
        hid_free = [[wo_done[B - 1, 0]], [wo_done[B - 1, 0]]]
        choose = select(1, prob[:, :, :].rearrange("p a b -> p (a b)"))
        choose.pop(0)()
        slots_transposed = choose.pop()
        up0(0)
        for r in range(E):
            if r + 1 < E:
                up0(r + 1)
            down0(r)
            for f in choose[0:5]:
                f()
            choose = choose[5:]
            if r == E - 3:
                slots_transposed()
                split_prob(1)
                before_gather(HALF)
        for b in range(HALF, B):
            if b + 1 < B:
                before_gather(b + 1)
            gather(b)
        up0(E)
        for r in range(E, 2 * E):
            if r + 1 < 2 * E:
                up0(r + 1)
            y_ready = down0(r)
        rounds_done = y_ready

        PARTS_K, PARTS_Q = (0, 0, 1, 1, 0, 2), (0, 1, 0, 1, 2, 0)
        ROWS = HD1 * len(PARTS_K)
        k_st = carve([H1 * S // 2], restart=True).bitcast(BF16).rearrange("p (h s) -> p h s", h=H1)
        q_st = carve([H1 * S // 2]).bitcast(BF16).rearrange("p (h s) -> p h s", h=H1)
        ctx1T = carve([S])
        gm = [carve([BANK]), rope_b[:, 1, :]]
        Arena.at = back_at
        qx = [carve([GRP, S])]
        part = carve([2, 3, S // 2]).bitcast(BF16)
        v_head = carve([NT, H1, P])
        qx.append(carve([GRP, S]))
        assert Arena.at <= tables_at
        rest = ctx_sum[:, 0, 1, :]
        xn1 = ctx_sum[:, 1, 1, :].rearrange("p (n d) -> p n d", n=NT)

        t_spread = dve([g_w1], tensor_copy, spread, spread_f)
        t_r0 = dve([g_w1], tensor_copy, rel0_col, band[:, 0:1])
        t_band = dve([t_r0], tensor_scalar, band, band, rel0_col[:, 0:1], None, ALU.subtract)

        def band_keys(c):
            if c >= NCH:
                return slice(P - RMAX, P)
            first, last = max(CH * c - RMAX, 0), CH * (c + 1)
            return slice(first // 64 * 64, -(-last // 32) * 32)

        def band_slice(c):
            e0 = BAND_E0 - CH * c if c < NCH else BAND_E0 - P - CH * (c - NCH)
            return band[:, e0:e0 + P]

        for c in range(NCH + 2):
            k = c // 4
            tk = pe([t_band], transpose, psum[:, k, (c % 4) * P:(c % 4 + 1) * P], band_slice(c), ident[:, :])
        for k, n in ((0, 4), (1, 4), (2, NCH + 2 - 8)):
            t_bt = dve([tk], tensor_copy, band_T[:, 4 * k:4 * k + n, :],
                       psum[:, k, 0:n * P].rearrange("p (c q) -> p c q", c=n))
            bank_free[k] = [t_bt]

        def head_cols(n, first):
            a = v_head[:, n, 0, first:first + HD1]
            return bass.AP(a.tensor, a.offset, [list(a.ap[0]), [8 * P, 2], [P + HD1, 8], [1, HD1]])

        st1 = [dict() for _ in range(B)]
        g_st = [[prog.dma_group(f"d_stack{w}{z}") for w in "kq"] for z in range(2)]
        g_parts = [prog.dma_group(f"d_parts{w}") for w in "kq"]
        parts_dram = nc.dram_tensor("qk_parts", (B, 2, P, 3, S), BF16, kind="Internal").ap()
        stack_need = {}
        part_free = [[], []]
        rest_free, xn1_free, ctx1_free, v_free, gm_free = [[]], [[]], [[]], [[]], [[], []]
        stack_free, qx_free = [[], []], [[], []]
        qx_ready = {}

        def prepare1(b):
            zb = b % 2

            def load():
                st1[b]["tok"] = tokens_from_xT(b, xn1, xn1_free[0])

            def stat():
                st1[b]["stat"] = statistics(xn1, st1[b]["tok"])

            def center():
                st1[b]["xn"] = normalise(xn1, st1[b]["stat"])

            def norm():
                tk, st1[b]["h"] = modulate(b, 1, SC_A, SH_A, xn1, st1[b]["xn"], zb)
                xn1_free[0] = [tk]

            def make(which):
                w, order, stack = ((wk1, PARTS_K, k_st), (wq1, PARTS_Q, q_st))[which]
                finish_rotations()
                z = 0
                tk = mm([st1[b]["h"], g_w1, bank_free[AUX]], psum[:, AUX, :], w, hT[:, zb, :], True)
                tr = act([tk, raw_free[z]], copy, raw[:, z, :], psum[:, AUX, :])
                bank_free[AUX] = [tr]

                def fin(wait, z):
                    if which == 0:
                        ta = dve([wait, t_r0, rest_free[0]], scalar_tensor_tensor, rest, rope_a[:, z, :],
                                 rel0_col[:, 0:1], raw[:, z, :], ALU.add, ALU.add)
                    else:
                        ta = pool([wait, rest_free[0]], tensor_tensor, rest, rope_a[:, z, :], raw[:, z, :], ALU.add)
                    t1 = pool([ta, part_free[which]], tensor_copy, part[:, which, 0, :], rest)
                    t2 = pool([t1], tensor_tensor, rest, rest, part[:, which, 0, :], ALU.subtract)
                    t3 = pool([t2], tensor_copy, part[:, which, 1, :], rest)
                    t4 = pool([t3], tensor_tensor, part[:, which, 2, :], rest, part[:, which, 1, :], ALU.subtract)
                    rest_free[0] = [t4]
                    g_out = g_parts[which]
                    prog.dma(g_out, parts_dram[b, which], part[:, which, :, :], wait=[t4])
                    written = g_out.so_far()
                    part_free[which] = [written]
                    for r, pp in enumerate(order):
                        row = 64 * zb + HD1 * r
                        prog.dma(g_st[zb][which], stack[row:row + HD1, :, :],
                                 parts_dram[b, which, :, pp, :].rearrange("(h d) s -> d h s", h=H1),
                                 wait=[written, stack_free[zb]])
                    stack_need[b, which] = g_st[zb][which].so_far()
                    return ta

                rotate_into(tr, z, rope1, g_w1, fin)

            return [load, stat, center, norm, lambda: make(0), lambda: make(1)]

        ahead = prepare1(0)
        stack_free[0] = stack_free[1] = [rounds_done]
        back_ready, back_free = {}, [oh_free for _ in range(BACKS)]

        def slots_of_tokens(r):
            kb, z, rows = r % 4, r % BACKS, HALF * E
            tk = mm([chosen[r // rows], bank_free[kb]], psum[:, kb, :],
                    ident_bf[0:rows, r % rows:r % rows + 1].to_broadcast([rows, P]), pos_bf[:, r // rows, :],
                    start=True)
            back_ready[r] = dve([tk, back_free[z], g_iota], tensor_scalar, back[:, z, :], psum[:, kb, :],
                                iota_col[:, 0:1], None, ALU.is_equal)
            bank_free[kb] = [back_ready[r]]

        for r in range(BACKS - 1):
            slots_of_tokens(r)
        for b in range(B):
            ko = 4 + b % 2
            for x in range(E):
                r = b * E + x
                if r + BACKS - 1 < B * E:
                    slots_of_tokens(r + BACKS - 1)
                tk = mm([back_ready[r], y_ready, bank_free[ko]], psum[:, ko, :], xin[:, x, b, :],
                        back[:, r % BACKS, :], start=(x == 0), stop=(x == E - 1))
                back_free[r % BACKS] = [tk]
            cols = slice(b * S, (b + 1) * S)
            tx = dve([tk], scalar_tensor_tensor,
                xT[:, cols], psum[:, ko, :], mod[:, 0, GA_B, b:b + 1], xT[:, cols], ALU.mult, ALU.add)
            bank_free[ko] = [tx]
            x_ready[b] = [tx]
            for f in ahead[b:b + 1]:
                f()
                finish_rotations()
        barrier()

        prog.dma(g_ff1, w1, t["L1_W1"].rearrange("e d f -> d e f"))
        prog.dma(g_ff1, w2, t["L1_W2"].rearrange("e (c p) d -> p e c d", p=P))
        t_vz = [dve([], memset, v_head[:, 0:NT // 2, :, :].rearrange("p a b c -> p (a b c)"), 0.0),
                pool([], memset, v_head[:, NT // 2:NT, :, :].rearrange("p a b c -> p (a b c)"), 0.0)]
        t_v1 = [pool([t_vz], memset, head_cols(n, 64), 1.0) for n in range(NT)]

        def cols4(a, c):
            return a.rearrange("p (h q) -> p h q", h=GRP)[:, :, c * CH:(c + 1) * CH]

        def value1(b):
            zb = b % 2
            for n in range(NT):
                tk = mm([st1[b]["h"], g_w1, bank_free[AUX]], psum[:, AUX, n * P:(n + 1) * P],
                        hT[:, zb, n * P:(n + 1) * P], wv1, start=(n == 0))
            hT_free[zb] = [tk]
            for n in range(NT):
                tv = dve([tk, t_v1, v_free[0]], tensor_tensor, head_cols(n, 0),
                         psum[:, AUX, n * P:(n + 1) * P].rearrange("p (a h d) -> p a h d", a=2, h=8),
                         rel0_row.unsqueeze(1).unsqueeze(1).to_broadcast([P, 2, 8, HD1]), ALU.add)
            bank_free[AUX] = [tv]
            st1[b]["v"] = tv

        def expand(b, h):
            z, r0 = (h // GRP) % 2, 64 * (b % 2)
            tk = mm([stack_need[b, 1], t_spread, bank_free[AUX]], psum[:, AUX, :], spread[r0:r0 + ROWS, :],
                    q_st[r0:r0 + ROWS, h, :], True)
            qx_ready[b, h] = dve([tk, qx_free[z]], tensor_tensor,
                                 qx[z][:, h % GRP, :].rearrange("p (i q) -> p i q", i=NT),
                                 psum[:, AUX, :].rearrange("p (i q) -> p i q", i=NT),
                                 chunk_mask.unsqueeze(1).to_broadcast([P, NT, P]), ALU.mult)
            bank_free[AUX] = [qx_ready[b, h]]

        st2 = [dict() for _ in range(B)]

        small = raw[:, 1, :]
        wr, br_row, keep = small[:, 0:E], small[:, E:2 * E], small[:, 2 * E:2 * E + NT * E]
        sc, gt, eq, cum, ex, *rw, top = (
            small[:, 2 * E + k * NT * E:2 * E + (k + 1) * NT * E].rearrange("p (n e) -> p n e", n=NT)
            for k in range(1, 9))
        ngt = small[:, 2 * E + 9 * NT * E:2 * E + 9 * NT * E + NT]
        g_router = prog.dma_group("d_router")
        prog.dma(g_router, wr, t["Wr"])
        prog.dma(g_router, keep, t["keep"])
        prog.dma(g_router, br_row, t["br"].rearrange("(a e) -> a e", a=1).partition_broadcast(P))

        def route2(b):
            zb, v = b % 2, st2[b]

            def load():
                v["tok"] = tokens_from_xT(b, xn1, xn1_free[0])

            def stat():
                v["stat"] = statistics(xn1, v["tok"])

            def center():
                v["xn"] = normalise(xn1, v["stat"])

            def norm():
                tk, v["h"] = modulate(b, 1, SC_B, SH_B, xn1, v["xn"], zb)
                xn1_free[0] = [tk]

            def router():
                for n in range(NT):
                    tk = mm([v["h"], g_router, bank_free[AUX]], psum[:, AUX, n * E:(n + 1) * E],
                            hT[:, zb, n * P:(n + 1) * P], wr, start=(n == 0))
                t1 = dve([tk], tensor_tensor,
                         sc, psum[:, AUX, 0:NT * E].rearrange("p (n e) -> p n e", n=NT),
                         br_row.unsqueeze(1).to_broadcast([P, NT, E]), ALU.add)
                bank_free[AUX] = [t1]
                for n in range(NT):
                    t2 = dve([t1], max8, top[:, n, :], sc[:, n, :])
                second = top[:, :, 1:2].to_broadcast([P, NT, E])
                ta = dve([t2], tensor_tensor, gt, sc, second, ALU.is_gt)
                tb = dve([t2], tensor_tensor, eq, sc, second, ALU.is_equal)
                t3 = dve([ta], tensor_reduce, ngt, gt, AX.X, ALU.add)
                t4 = dve([tb], tensor_tensor_scan,
                         cum.rearrange("p n e -> p (n e)"), keep, eq.rearrange("p n e -> p (n e)"), 0.0,
                         ALU.mult, ALU.add)
                t4 = dve([t3, t4], tensor_tensor, cum, cum, ngt.unsqueeze(2).to_broadcast([P, NT, E]), ALU.add)
                t4 = dve([t4], tensor_scalar, cum, cum, 2.0, None, ALU.is_le)
                t4 = dve([t4], tensor_tensor, eq, eq, cum, ALU.mult)
                t4 = dve([t4], tensor_tensor, gt, gt, eq, ALU.add)
                t5 = dve([t2], tensor_tensor, ex, sc, top[:, :, 0:1].to_broadcast([P, NT, E]), ALU.subtract)
                v["ex"] = act([t5], activation, ex, ex, ACT.Exp)
                v["gt"] = t4

            def weights():
                t5 = dve([v["ex"], v["gt"]], tensor_tensor, ex, ex, gt, ALU.mult)
                t6 = dve([t5], tensor_reduce, ngt, ex, AX.X, ALU.add)
                t6 = dve([t6], reciprocal, ngt, ngt)
                v["rw"] = dve([t6], tensor_tensor,
                              rw[zb], ex, ngt.unsqueeze(2).to_broadcast([P, NT, E]), ALU.mult)

            return [load, stat, center, norm, router, weights]

        order1 = [(g, i, k0) for g in range(H1 // GRP) for i, k0 in ((1, 4), (3, 0), (0, 4), (2, 0))]

        def scores1(u):
            b, g, i, k0 = u["b"], u["g"], u["i"], u["k0"]
            z, r0 = g % 2, 64 * (b % 2)
            for j in range(i + 1):
                for h in range(GRP):
                    mm([stack_need[b, 0], stack_need[b, 1], bank_free[k0 + j]],
                       psum[:, k0 + j, h * P:(h + 1) * P], k_st[r0:r0 + ROWS, GRP * g + h, j * P:(j + 1) * P],
                       q_st[r0:r0 + ROWS, GRP * g + h, i * P:(i + 1) * P], start=(h == 0))
            mm([consts_ready], psum[:, k0 + i, :], ident_bf[:, :],
               causal[:, :].unsqueeze(1).to_broadcast([P, GRP, P]), False)
            ahead = u["n"] + NT
            if ahead < B * NU:
                expand(ahead // NU, ahead % NU)
            for c in list(range(NCH)) + ([NCH, NCH + 1] if i else []):
                k, cc = (k0 + i, c) if c < NCH else (k0 + i - 1, c - NCH)
                keys = band_keys(c)
                tk = mm([[qx_ready[b, GRP * g + h] for h in range(GRP)], t_band], cols4(psum[keys, k, :], cc),
                        band_slice(c)[:, keys], qx[z][:, :, i * P + cc * CH:i * P + (cc + 1) * CH], False)
            if i == order1[-1][1]:
                qx_free[z] = [tk]
                if g == NU // NT - 1:
                    stack_free[b % 2] = [tk]
            return tk

        def pair_probs(i, c):
            a = prob[:, 0, i * BANK + c * CH:i * BANK + (c + 1) * CH]
            return bass.AP(a.tensor, a.offset, [list(a.ap[0]), [4 * BANK + 2 * BANK, 2], [P, GRP], [1, CH]])

        def relative_part(u, half):
            i = u["i"] - 2
            for c in range(4 * half, 4 * half + 4):
                cols = psum[:, AUX, (c % 4) * P:(c % 4 + 1) * P]
                t_g = mm([u["prob"], t_bt, bank_free[AUX]], cols, band_T[:, c, :], pair_probs(i, c),
                         start=(c % 4 == 0))
                if c < 2:
                    if i:
                        t_g = mm([], cols, band_T[:, NCH + c, :], pair_probs(i - 1, c), False)
                    else:
                        t_g = mm([], cols[:, GRP * CH:P], band_T[:, NCH + c, :],
                                 cols4(prob[:, 1, BANK:2 * BANK], c), False)
            gm_ready = dve([t_g, gm_free[half]], tensor_tensor, gm[half].rearrange("p (a j) -> p a j", j=CH),
                           psum[:, AUX, :].rearrange("p (a j) -> p a j", j=CH),
                           chunk_mask[:, 0:CH].unsqueeze(1).to_broadcast([P, BANK // CH, CH]), ALU.mult)
            bank_free[AUX] = [gm_ready]
            return t_g, gm_ready

        def fold_part(u, half, gm_ready):
            i, g = u["i"] - 2, u["g"]
            for h in range(GRP):
                tk = mm([gm_ready],
                        psum[:, CTX, :].rearrange("p (w r c j) -> p w r c j", w=2, r=2, j=CH)[
                            :, :, i, 4 * half:4 * half + 4, :],
                        fold[:, GRP * (g % 2) + h, :],
                        gm[half].rearrange("p (c w h j) -> p w c h j", c=4, w=2, h=GRP)[:, :, :, h, :], False)
            gm_free[half] = [tk]
            return tk

        def values1(u):
            b, g, i, z = u["b"], u["g"], u["i"], u["n"] % 2
            pz = prob[:, z, :]
            if z:
                _, ready0 = relative_part(u, 0)
            first = g % 2 == 0 and i == order1[0][1]
            for j in range(i + 1):
                for h in range(GRP):
                    tk = mm([u["prob"], st1[b]["v"], bank_free[CTX]], psum[:, CTX, i * P:(i + 1) * P],
                            v_head[:, j, GRP * g + h, :], pz[:, j * BANK + h * P:j * BANK + (h + 1) * P],
                            start=(first and j == 0 and h == 0))
            if z:
                t_g, ready1 = relative_part(u, 1)
                fold_part(u, 0, ready0)
                t_f = fold_part(u, 1, ready1)
                prob_free[0], prob_free[1] = [t_g], [t_g]
            if g % 2 == 1 and i == order1[-1][1]:
                rows = slice(64 * (g // 2), 64 * (g // 2) + 64)
                act([t_f, cs_free[0]], copy, ctx_sum[rows, 0, 0, :], psum[0:64, CTX, :])
                tc = act([t_f], copy, ctx_sum[rows, 1, 0, :], psum[64:128, CTX, :])
                bank_free[CTX] = [tc]

                def late():
                    tr = dve([tc], reciprocal, ctx_sum[:, 1, 0, :], ctx_sum[:, 1, 0, :])
                    st1[b]["ctx"] = pool([tr, ctx1_free[0]], tensor_tensor, ctx1T, ctx_sum[:, 0, 0, :],
                                         ctx_sum[:, 1, 0, :], ALU.mult)
                    cs_free[0] = [st1[b]["ctx"]]
                if g // 2:
                    u["late"] = late
            if u["n"] % NU == NU - 1:
                v_free[0] = [tk]

        def finish1(b):
            tk = mm([st1[b]["ctx"], g_w1, bank_free[AUX]], psum[:, AUX, :], wo1, ctx1T, True)
            ctx1_free[0] = [tk]
            cols = slice(b * S, (b + 1) * S)
            tx = dve([tk], scalar_tensor_tensor, xT[:, cols], psum[:, AUX, :], mod[:, 1, GA_A, b:b + 1], xT[:, cols],
                     ALU.mult, ALU.add)
            bank_free[AUX] = [tx]
            x_ready[b] = [tx]

        side = {-1: [lambda: value1(0)] + [lambda h=h: expand(0, h) for h in range(GRP)],
                B * NU: [lambda: finish1(B - 1)]}
        for b in range(B):
            if b:
                side.setdefault(b * NU, []).append(lambda b=b: value1(b))
                side.setdefault(b * NU + 3, []).append(lambda b=b: finish1(b - 1))
            if b + 1 < B:
                spread_steps(side, prepare1(b + 1), b * NU, b * NU + 5)
        spread_steps(side, route2(0), (B - 1) * NU + 4, (B - 1) * NU + 11)
        attention(HD1 ** -0.5, order1, scores1, values1, side, pairs=True)
        barrier()

        hid = carve([2, FC, S], restart=True)
        acc = carve([2, NT, D])
        b1 = carve([E, FC])
        b2 = carve([D])
        rwT = carve([2, S])
        out_tok = carve([2, NT, D])
        g_w2 = prog.dma_group("d_w2")
        prog.dma(g_w2, b1, t["b1"])
        prog.dma(g_w2, b2[0:E, :], t["b2"])
        hid_free, hid_ready, acc_free, rwT_free, out_free = [[], []], {}, [[], []], [[], []], [None, None]
        stores = []
        out_v = out.rearrange("b (n p) d -> p (b n) d", p=P)

        def before2(b):
            zb, v = b % 2, st2[b]

            def transposed():
                for n in range(NT):
                    tk = pe([v["rw"], bank_free[AUX]], transpose,
                            psum[0:E, AUX, n * P:(n + 1) * P], rw[zb][:, n, :], ident[:, :])
                v["rwT"] = dve([tk, rwT_free[zb]], tensor_copy, rwT[0:E, zb, :], psum[0:E, AUX, :])
                bank_free[AUX] = [v["rwT"]]

            def bias():
                for n in range(NT):
                    tk = mm([v["rwT"], g_w2, bank_free[AUX]], psum[:, AUX, n * P:(n + 1) * P],
                            rwT[0:E, zb, n * P:(n + 1) * P], b2[0:E, :], start=(n == 0))
                rwT_free[zb] = [tk]
                v["acc"] = [act([tk, acc_free[zb]], copy,
                                acc[:, zb, :, :], psum[:, AUX, :].rearrange("p (n d) -> p n d", n=NT))] * NT
                bank_free[AUX] = [v["acc"][0]]

            return route2(b) + [transposed, bias]

        def after2(b):
            zb, v = b % 2, st2[b]

            def residual():
                for n in range(NT):
                    tk = pe([v["acc"], bank_free[AUX]], transpose,
                            psum[:, AUX, n * P:(n + 1) * P], acc[:, zb, n, :], ident[:, :])
                acc_free[zb] = [tk]
                cols = slice(b * S, (b + 1) * S)
                v["x"] = dve([tk], scalar_tensor_tensor,
                             xT[:, cols], psum[:, AUX, :], mod[:, 1, GA_B, b:b + 1], xT[:, cols], ALU.mult, ALU.add)
                bank_free[AUX] = [v["x"]]

            def store():
                for n in range(NT):
                    tk = pe([v["x"], bank_free[7]], transpose,
                            psum[:, 7, n * P:(n + 1) * P], xT[:, b * S + n * P:b * S + (n + 1) * P], ident[:, :])
                to = act([tk, out_free[zb]], copy,
                         out_tok[:, zb, :, :], psum[:, 7, :].rearrange("p (n d) -> p n d", n=NT))
                bank_free[7] = [to]
                g_o = prog.dma_group(f"d_out{b}")
                prog.dma(g_o, out_v[:, b * NT:(b + 1) * NT, :], out_tok[:, zb, :, :], wait=[to])
                out_free[zb] = g_o
                stores.append(g_o)

            return [residual, store]

        def up1(r):
            b, x = divmod(r, E)
            for c in range(FC):
                tk = mm([st2[b]["h"], g_ff1, bank_free[c]], psum[:, c, :], w1[:, x, c * P:(c + 1) * P],
                        hT[:, b % 2, :], True)
                hid_ready[r, c] = act([tk, hid_free[r % 2], g_w2], activation, hid[:, r % 2, c, :], psum[:, c, :],
                                      ACT.Gelu_apprx_tanh, bias=b1[:, x, c:c + 1])
                bank_free[c] = [hid_ready[r, c]]
            if x == E - 1:
                hT_free[b % 2] = [tk]

        def down1(r):
            b, x = divmod(r, E)
            z, ky = r % 2, 4 + r % 2
            for n in range(NT):
                for c in range(FC):
                    tk = mm([hid_ready[r, c], bank_free[ky]], psum[:, ky, n * P:(n + 1) * P],
                            hid[:, z, c, n * P:(n + 1) * P], w2[:, x, c, :],
                            start=(n == 0 and c == 0), stop=(c == FC - 1))
            hid_free[z] = [tk]
            st2[b]["acc"] = [dve([tk, st2[b]["acc"][n]], scalar_tensor_tensor,
                                 acc[:, b % 2, n, :], psum[:, ky, n * P:(n + 1) * P], rw[b % 2][:, n, x:x + 1],
                                 acc[:, b % 2, n, :], ALU.mult, ALU.add) for n in range(NT)]
            bank_free[ky] = [st2[b]["acc"][-1]]

        side = {}
        for b in range(B):
            if b + 1 < B:
                for k, f in enumerate(before2(b + 1)):
                    side.setdefault(b * E + k, []).append(f)
                for k, f in enumerate(after2(b)):
                    side.setdefault((b + 1) * E + 1 + 2 * k, []).append(f)
        for f in before2(0)[6:]:
            f()
        up1(0)
        for r in range(B * E):
            if r + 1 < B * E:
                up1(r + 1)
            for f in side.get(r, []):
                f()
            down1(r)
        for f in after2(B - 1):
            f()
        prog.wait_only("sync", stores)

        prog.run(ctx.enter_context(nc.Block()))


def kernel(**inputs):
    import concourse.bacc as bacc
    from concourse.bass_utils import run_bass_kernel_spmd

    a = {k: np.ascontiguousarray(v) for k, v in inputs.items()}
    arrays = {
        "x": a["L0_attn_hidden_states"], "Wq": a["L0_attn_Wq"], "Wk": a["L0_attn_Wk"], "Wv": a["L0_attn_Wv"],
        "Wo": a["L0_attn_Wo"], "gateT": a["L0_ffn_gate_w"].T, "L0_w1": a["L0_ffn_w1"], "L0_w2": a["L0_ffn_w2"],
        "L0_cT": a["L0_c"].T, "L0_wmod": a["L0_wmod"], "L1_cT": a["L1_c"].T, "L1_wmod": a["L1_wmod"],
        "w_qT": a["L1_attn_w_q"].T, "w_kT": a["L1_attn_w_k"].T, "w_vT": a["L1_attn_w_v"].T,
        "w_oT": a["L1_attn_w_o"].T, "rel_emb": a["L1_attn_rel_emb"],
        "band": a["L1_attn_rel_emb"][band_index()].transpose(0, 2, 1).reshape(P, BAND_W),
        "L1_W1": a["L1_ffn_W1"], "b1": a["L1_ffn_b1"].reshape(E, FC, P).transpose(2, 0, 1),
        "L1_W2": a["L1_ffn_W2"], "b2": a["L1_ffn_b2"],
        "Wr": a["L1_ffn_Wr"], "br": a["L1_ffn_br"],
    }
    arrays.update(shape_constants())
    nc = bacc.Bacc("TRN2", target_bir_lowering=False, num_devices=1)
    feed, t = {}, {}
    for name, v in arrays.items():
        v = np.ascontiguousarray(v)
        feed[f"in_{name}"] = v
        t[name] = nc.dram_tensor(f"in_{name}", v.shape, mybir.dt.from_np(v.dtype), kind="ExternalInput").ap()
    out = nc.dram_tensor("out", (B, S, D), F32, kind="ExternalOutput").ap()
    build(nc, t, out)
    r = run_bass_kernel_spmd(nc, [feed], core_ids=[0])
    return r.results[0]["out"]
```
